# Optimizing a Trainium2 kernel written in Bass

```python
import numpy as np
import jax
import jax.numpy as jnp

def _softmax(x, axis=-1):
    return jax.nn.softmax(x, axis=axis)

def _gelu(x):
    return jax.nn.gelu(x, approximate=True)

def _silu(x):
    return jax.nn.silu(x)

def _sigmoid(x):
    return jax.nn.sigmoid(x)

def _layernorm(x, axis=-1, eps=1e-05):
    m = jnp.mean(x, axis=axis, keepdims=True)
    v = jnp.var(x, axis=axis, keepdims=True)
    return (x - m) / jnp.sqrt(v + eps)

def _scatter_add(tgt, idx, src, axis=0):
    return tgt.at[idx].add(src)

def _segment_sum(src, seg, n):
    return jax.ops.segment_sum(src, seg, n)
kernel_name = 'mk_adaln_d1_jaxref_r8_8339ff'

def setup_inputs(seed: int=0):
    np.random.seed(seed)
    _w = jnp.asarray

    def _L0_attn_setup():
        import jax, jax.numpy as jnp
        import numpy as np
        from jax import lax
        H, KVH, D, CHUNK = (32, 8, 128, 128)
        ROPE_THETA = 10000.0
        RMS_EPS = 1e-05

        def _rope_tables(L):
            inv_freq = 1.0 / ROPE_THETA ** (jnp.arange(0, D, 2, dtype=jnp.float32) / D)
            ang = jnp.arange(L, dtype=jnp.float32)[:, None] * inv_freq
            cos = jnp.concatenate([jnp.cos(ang), jnp.cos(ang)], axis=-1)[:, None, :]
            sin = jnp.concatenate([jnp.sin(ang), jnp.sin(ang)], axis=-1)[:, None, :]
            return (cos, sin)

        def _apply_rope(x, cos, sin):
            half = D // 2
            rot = jnp.concatenate([-x[..., half:], x[..., :half]], axis=-1)
            return x * cos + rot * sin
        key = jax.random.key(seed)
        ks = jax.random.split(key, 10)
        B, L, HID = (1, 512, 512)
        s = lambda fan: 1.0 / np.sqrt(fan)
        return {'hidden_states': jax.random.normal(ks[0], (B, L, HID), jnp.float32), 'Wq': jax.random.normal(ks[1], (H * D, HID), jnp.float32) * s(HID), 'Wk': jax.random.normal(ks[2], (KVH * D, HID), jnp.float32) * s(HID), 'Wv': jax.random.normal(ks[3], (KVH * D, HID), jnp.float32) * s(HID), 'Wo': jax.random.normal(ks[4], (HID, H * D), jnp.float32) * s(H * D), 'Wg': jax.random.normal(ks[5], (H * D, HID), jnp.float32) * (s(HID) * 2 ** (-2.5)), 'Win': jax.random.normal(ks[6], (H, HID), jnp.float32) * s(HID), 'dt_bias': jnp.zeros((H,), jnp.float32), 'A_log_bias': jnp.log(jax.random.uniform(ks[7], (H,), jnp.float32, 1.0, 16.0)), 'gnorm_w': jnp.ones((D,), jnp.float32)}
    _L0_attn_in = _L0_attn_setup()

    def _L0_ffn_setup():
        import jax, jax.numpy as jnp
        import numpy as np
        HIDDEN = 512
        INTER = 1376
        key = jax.random.key(seed)
        k0, k1, k2, k3 = jax.random.split(key, 4)
        scale_h = 1.0 / np.sqrt(HIDDEN)
        scale_i = 1.0 / np.sqrt(INTER)
        return {'x': jax.random.normal(k0, (4, 32, HIDDEN), dtype=jnp.float32), 'w_gate': jax.random.normal(k1, (INTER, HIDDEN), dtype=jnp.float32) * scale_h, 'w_up': jax.random.normal(k2, (INTER, HIDDEN), dtype=jnp.float32) * scale_h, 'w_down': jax.random.normal(k3, (HIDDEN, INTER), dtype=jnp.float32) * scale_i}
    _L0_ffn_in = _L0_ffn_setup()
    _L0_c = _w((lambda *s: np.random.randn(*s).astype(np.float32) * 0.05)(4, 512))
    _L0_wmod = _w((lambda *s: np.random.randn(*s).astype(np.float32) * 0.05)(512, 6 * 512) * 512 ** (-0.5))
    _d = {'L0_attn_hidden_states': _L0_attn_in['hidden_states'], 'L0_attn_Wq': _L0_attn_in['Wq'], 'L0_attn_Wk': _L0_attn_in['Wk'], 'L0_attn_Wv': _L0_attn_in['Wv'], 'L0_attn_Wo': _L0_attn_in['Wo'], 'L0_attn_Wg': _L0_attn_in['Wg'], 'L0_attn_Win': _L0_attn_in['Win'], 'L0_attn_dt_bias': _L0_attn_in['dt_bias'], 'L0_attn_A_log_bias': _L0_attn_in['A_log_bias'], 'L0_attn_gnorm_w': _L0_attn_in['gnorm_w'], 'L0_ffn_w_gate': _L0_ffn_in['w_gate'], 'L0_ffn_w_up': _L0_ffn_in['w_up'], 'L0_ffn_w_down': _L0_ffn_in['w_down'], 'L0_c': _L0_c, 'L0_wmod': _L0_wmod}
    _x0 = _d['L0_attn_hidden_states']
    _d['L0_attn_hidden_states'] = jax.random.normal(jax.random.fold_in(jax.random.key(seed), 1), (4, 256, 512), dtype=_x0.dtype)
    del _x0
    return _d

def reference(L0_attn_hidden_states, L0_attn_Wq, L0_attn_Wk, L0_attn_Wv, L0_attn_Wo, L0_attn_Wg, L0_attn_Win, L0_attn_dt_bias, L0_attn_A_log_bias, L0_attn_gnorm_w, L0_ffn_w_gate, L0_ffn_w_up, L0_ffn_w_down, L0_c, L0_wmod):

    def _L0_attn_ref(hidden_states, Wq, Wk, Wv, Wo, Wg, Win, dt_bias, A_log_bias, gnorm_w):
        import jax, jax.numpy as jnp
        import numpy as np
        from jax import lax
        H, KVH, D, CHUNK = (32, 8, 128, 128)
        ROPE_THETA = 10000.0
        RMS_EPS = 1e-05

        def _rope_tables(L):
            inv_freq = 1.0 / ROPE_THETA ** (jnp.arange(0, D, 2, dtype=jnp.float32) / D)
            ang = jnp.arange(L, dtype=jnp.float32)[:, None] * inv_freq
            cos = jnp.concatenate([jnp.cos(ang), jnp.cos(ang)], axis=-1)[:, None, :]
            sin = jnp.concatenate([jnp.sin(ang), jnp.sin(ang)], axis=-1)[:, None, :]
            return (cos, sin)

        def _apply_rope(x, cos, sin):
            half = D // 2
            rot = jnp.concatenate([-x[..., half:], x[..., :half]], axis=-1)
            return x * cos + rot * sin
        B, L, HID = hidden_states.shape
        NC = L // CHUNK
        q = (hidden_states @ Wq.T).reshape(B, L, H, D)
        k = (hidden_states @ Wk.T).reshape(B, L, KVH, D)
        v = (hidden_states @ Wv.T).reshape(B, L, KVH, D)
        cos, sin = _rope_tables(L)
        q = _apply_rope(q, cos, sin)
        k = _apply_rope(k, cos, sin)
        k = jnp.repeat(k, H // KVH, axis=2)
        v = jnp.repeat(v, H // KVH, axis=2)
        dt = jax.nn.softplus(hidden_states @ Win.T + dt_bias)
        A = -jnp.exp(A_log_bias)
        g = dt * A

        def chunked(t):
            return t.transpose(0, 2, 1, 3).reshape(B, H, NC, CHUNK, D)
        qc, kc = (chunked(q), chunked(k))
        xc = chunked(v * dt[..., None])
        gc = g.transpose(0, 2, 1).reshape(B, H, NC, CHUNK)
        G = jnp.cumsum(gc, axis=-1)
        scores = jnp.einsum('bhnid,bhnjd->bhnij', qc, kc)
        idx = jnp.arange(CHUNK)
        causal = idx[:, None] >= idx[None, :]
        decay = jnp.where(causal, jnp.exp(G[..., :, None] - G[..., None, :]), 0.0)
        y_intra = jnp.einsum('bhnij,bhnjd->bhnid', scores * decay, xc)
        Glast = G[..., -1:]
        k_dec = kc * jnp.exp(Glast - G)[..., None]
        cstates = jnp.einsum('bhnjd,bhnje->bhnde', k_dec, xc)
        chunk_decay = jnp.exp(G[..., -1])

        def step(state, inp):
            dec, cs = inp
            return (state * dec + cs, state)
        init = jnp.zeros((B, H, D, D), hidden_states.dtype)
        _, prev = lax.scan(step, init, (chunk_decay.transpose(2, 0, 1)[..., None, None], cstates.transpose(2, 0, 1, 3, 4)))
        prev = prev.transpose(1, 2, 0, 3, 4)
        y_inter = jnp.einsum('bhnid,bhnde->bhnie', qc * jnp.exp(G)[..., None], prev)
        y = (y_intra + y_inter).reshape(B, H, L, D).transpose(0, 2, 1, 3)
        rms = jnp.sqrt(jnp.mean(jnp.square(y), axis=-1, keepdims=True) + RMS_EPS)
        y = y / rms * gnorm_w
        gate = (hidden_states @ Wg.T).reshape(B, L, H, D)
        y = y * (gate * jax.nn.sigmoid(gate))
        return y.reshape(B, L, H * D) @ Wo.T

    def _L0_ffn_ref(x, w_gate, w_up, w_down):
        import jax, jax.numpy as jnp
        import numpy as np
        HIDDEN = 512
        INTER = 1376
        gate = jax.nn.silu(jnp.einsum('bsh,ih->bsi', x, w_gate))
        up = jnp.einsum('bsh,ih->bsi', x, w_up)
        return jnp.einsum('bsi,hi->bsh', gate * up, w_down)
    x = L0_attn_hidden_states
    mod = (_silu(L0_c) @ L0_wmod).reshape(L0_c.shape[0], 6, 1, -1)
    sa, ca, ga, sb, cb, gb = (mod[:, 0], mod[:, 1], mod[:, 2], mod[:, 3], mod[:, 4], mod[:, 5])
    ga = (2 * (ga >= 0) - 1) * jnp.maximum(jnp.abs(ga), 0.25)
    gb = (2 * (gb >= 0) - 1) * jnp.maximum(jnp.abs(gb), 0.25)
    h = _layernorm(x, axis=-1) * (1 + ca) + sa
    x = x + ga * _L0_attn_ref(h, L0_attn_Wq, L0_attn_Wk, L0_attn_Wv, L0_attn_Wo, L0_attn_Wg, L0_attn_Win, L0_attn_dt_bias, L0_attn_A_log_bias, L0_attn_gnorm_w)
    h = _layernorm(x, axis=-1) * (1 + cb) + sb
    x = x + gb * _L0_ffn_ref(h, L0_ffn_w_gate, L0_ffn_w_up, L0_ffn_w_down)
    return x

_drawn_inputs = setup_inputs


def setup_inputs(seed=0):
    import zlib

    import numpy as np

    out = dict(_drawn_inputs(seed))
    spreads = {'L0_attn_dt_bias': (0.0, 0.1), 'L0_attn_gnorm_w': (1.0, 0.2)}
    factors = {}
    for name, (base, spread) in spreads.items():
        noise = np.random.default_rng([zlib.crc32(name.encode()), seed]).standard_normal(out[name].shape)
        drawn = base * np.exp(spread * noise) if base else spread * noise
        out[name] = jnp.asarray(drawn.astype(out[name].dtype))
    for name, factor in factors.items():
        out[name] = (out[name] * factor).astype(out[name].dtype)
    return out
```

```python
from contextlib import ExitStack

import concourse.bass as bass
from concourse import mybir

ALU = mybir.AluOpType
ACT = mybir.ActivationFunctionType
F32 = mybir.dt.float32
F32R = mybir.dt.float32r

P = 128
B, L, HID = 4, 256, 512
H, KVH, D = 32, 8, 128
CHUNK = 128
INTER = 1376
EPS = 1e-5
GRP = H // KVH
KT = HID // P
NT = B * L // P
CPB = L // CHUNK
IT = -(-INTER // P)
HALF = B * L // 2
assert CHUNK == P and D == P and CPB == 2 and HALF == 512 and GRP == 4 and NT == 8

C_ID, C_TRI, C_COST, C_SINT, C_COS, C_SIN, C_END = 0, 128, 256, 512, 768, 1024, 1280
EXP_CAP = 1e18
MASKED = -1e30
SA, CA, GA, SB, CB, GB = range(6)


def split_hi(engine, hi, full):
    return engine.tensor_copy(hi, full)


def split_lo(engine, lo, full, hi):
    return engine.tensor_tensor(lo, full, hi.bitcast(F32), ALU.subtract)


def three_products(pe, out, w_hi, w_lo, x_hi, x_lo, first, last):
    pe.matmul(out, w_hi, x_hi, start=first, stop=False)
    pe.matmul(out, w_hi, x_lo, start=False, stop=False)
    return pe.matmul(out, w_lo, x_hi, start=False, stop=last)


def build(nc, x_in, cT_in, wmod_in, wq_in, wg_in, wkv_in, wo_in, win_in, rows_in, gnorm_in,
          wgu_in, wd_in, cst_in, out):
    modrow = nc.dram_tensor("modrow", (2, B * HID), F32, kind="Internal").ap()
    gT_dram = nc.dram_tensor("gT_dram", (H, B * L), F32, kind="Internal").ap()

    with ExitStack() as outer:
        def sb(name, shape, dt=F32):
            return outer.enter_context(nc.sbuf_tensor(name, shape, dt))

        cst = sb("cst", [P, C_END])
        x1 = sb("x1", [P, NT, HID])
        hT_hi = sb("hT_hi", [P, KT, B * L], F32R)
        hT_lo = sb("hT_lo", [P, KT, B * L], F32R)
        tok = sb("tok", [P, NT, 3, H])
        modT = sb("modT", [P, 4, KT, B])
        gnorm = sb("gnorm", [P, 1])
        ident = cst[:, C_ID:C_ID + P]

        block_input(nc, cst, x1, hT_hi, hT_lo, tok, modT, gnorm, ident, modrow, gT_dram,
                    x_in, cT_in, wmod_in, win_in, rows_in, gnorm_in, cst_in)
        block_attention(nc, cst, x1, hT_hi, hT_lo, tok, gnorm, ident, gT_dram,
                        wq_in, wg_in, wkv_in, wo_in)
        block_ffn(nc, x1, hT_hi, hT_lo, modT, ident, modrow, x_in, wgu_in, wd_in, out)


class Norm:

    def __init__(self, ctx, nc, tag, x1, hT_hi, hT_lo, shift, scale, ident):
        def sb(name, shape, dt=F32):
            return ctx.enter_context(nc.sbuf_tensor(name + tag, shape, dt))

        def sem(name):
            return ctx.enter_context(nc.semaphore(name + tag))

        self.nc, self.x1, self.hT_hi, self.hT_lo = nc, x1, hT_hi, hT_lo
        self.shift, self.scale, self.ident = shift, scale, ident
        self.stats = sb("stats", [P, NT, 6])
        self.mv = sb("mv", [P, NT, 2])
        self.var = sb("var", [P, NT])
        self.rstd = sb("rstd", [P, NT])
        self.xn = sb("xn", [P, 2, HID])
        self.hf = sb("hf", [P, 2, KT, P])
        self.ps = [ctx.enter_context(nc.psum_tensor(f"ps_ln{i}{tag}", [P, KT, P], F32))
                   for i in range(2)]
        self.stats_done = sem("stats_done")
        self.mv_done = sem("mv_done")
        self.var_done = sem("var_done")
        self.lnvar_done = sem("lnvar_done")
        self.rstd_done = sem("rstd_done")
        self.xn_done = sem("xn_done")
        self.turned = sem("turned")
        self.hf_done = sem("hf_done")
        self.hi_done = sem("hi_done")
        self.lo_done = sem("lo_done")

    def vector_stats(self, dve, t):
        nc = self.nc
        nc.vector.bn_stats(self.stats[:, t], self.x1[:, t]).then_inc(self.stats_done, 1)
        dve.wait_ge(self.stats_done, t + 1)
        nc.vector.bn_aggr(self.mv[:, t], self.stats[:, t]).then_inc(self.mv_done, 1)

    def vector_var(self, dve):
        dve.wait_ge(self.mv_done, NT)
        self.nc.vector.tensor_scalar(self.var[:], self.mv[:, :, 1], EPS, None, ALU.add)\
            .then_inc(self.var_done, 1)

    def scalar_rstd(self, act):
        nc = self.nc
        act.wait_ge(self.var_done, 1)
        nc.scalar.activation(self.var[:], self.var[:], ACT.Ln).then_inc(self.lnvar_done, 1)
        act.wait_ge(self.lnvar_done, 1)
        nc.scalar.activation(self.rstd[:], self.var[:], ACT.Exp, scale=-0.5)\
            .then_inc(self.rstd_done, 1)

    def vector_normalise(self, dve, t):
        if t == 0:
            dve.wait_ge(self.rstd_done, 1)
        if t >= 2:
            dve.wait_ge(self.turned, t - 1)
        self.nc.vector.tensor_scalar(self.xn[:, t % 2], self.x1[:, t], self.mv[:, t, 0:1],
                                     self.rstd[:, t:t + 1], ALU.subtract, ALU.mult)\
            .then_inc(self.xn_done, 1)

    def tensor_turn(self, pe, t):
        pe.wait_ge(self.xn_done, t + 1)
        if t >= 2:
            pe.wait_ge(self.hf_done, t - 1)
        for k in range(KT):
            last = self.nc.tensor.transpose(self.ps[t % 2][:, k], self.xn[:, t % 2, k * P:(k + 1) * P],
                                            self.ident)
        last.then_inc(self.turned, 1)

    def scalar_modulate(self, act, t):
        b = t // CPB
        act.wait_ge(self.turned, t + 1)
        if t >= 2:
            act.wait_ge(self.lo_done, t - 1)
        for k in range(KT):
            last = self.nc.scalar.activation(self.hf[:, t % 2, k], self.ps[t % 2][:, k], ACT.Identity,
                                             bias=self.shift[:, k, b:b + 1],
                                             scale=self.scale[:, k, b:b + 1])
        last.then_inc(self.hf_done, 1)

    def vector_split(self, dve, t):
        hi, lo = self.hT_hi[:, :, t * P:(t + 1) * P], self.hT_lo[:, :, t * P:(t + 1) * P]
        dve.wait_ge(self.hf_done, t + 1)
        split_hi(self.nc.vector, hi, self.hf[:, t % 2]).then_inc(self.hi_done, 1)
        dve.wait_ge(self.hi_done, t + 1)
        split_lo(self.nc.vector, lo, self.hf[:, t % 2], hi).then_inc(self.lo_done, 1)

    def vector_all(self, dve):
        for t in range(NT + 1):
            if t < NT:
                self.vector_normalise(dve, t)
            if t >= 1:
                self.vector_split(dve, t - 1)


def block_input(nc, cst, x1, hT_hi, hT_lo, tok, modT, gnorm, ident, modrow, gT_dram,
                x_in, cT_in, wmod_in, win_in, rows_in, gnorm_in, cst_in):
    with ExitStack() as ctx:
        def sb(name, shape, dt=F32):
            return ctx.enter_context(nc.sbuf_tensor(name, shape, dt))

        def ps(name, shape):
            return ctx.enter_context(nc.psum_tensor(name, shape, F32))

        def sem(name):
            return ctx.enter_context(nc.semaphore(name))

        cT = sb("cT", [P, KT * B])
        sig_c = sb("sig_c", [P, KT * B])
        silu_c = sb("silu_c", [P, KT * B])
        wmod = sb("wmod", [P, 6, KT, HID])
        win = sb("win", [P, KT, H])
        win_hi = sb("win_hi", [P, KT, H], F32R)
        win_lo = sb("win_lo", [P, KT, H], F32R)
        rows = sb("rows", [P, 2, H])
        rate = sb("rate", [P, H])
        gates = sb("gates", [B, 2, HID])
        gmag = sb("gmag", [B, 2, HID])
        gneg = sb("gneg", [B, 2, HID])
        z = sb("z", [P, NT, H])
        za = sb("za", [P, NT, H])
        zs = sb("zs", [P, NT, H])
        zs2 = sb("zs2", [P, NT, H])
        zq = sb("zq", [P, NT, H])
        gdec = sb("gdec", [P, NT, H])
        gT = sb("gT", [H, B * L])
        ones = sb("ones", [P, P])
        ps_mod = ps("ps_mod", [P, 4, KT, B])
        ps_gate = [ps(f"ps_gate{i}", [B, HID]) for i in range(2)]
        ps_g = ps("ps_g", [P, 2, NT, H])
        ps_gt = [ps(f"ps_gt{i}", [H, HALF]) for i in range(2)]
        norm = Norm(ctx, nc, "1", x1, hT_hi, hT_lo, modT[:, 0], modT[:, 1], ident)

        cst_in_s = sem("cst_loaded")
        c_loaded = sem("c_loaded")
        x_loaded = [sem(f"x_loaded{i}") for i in range(2)]
        wmod_loaded = [sem(f"wmod_loaded{i}") for i in range(6)]
        small_loaded = sem("small_loaded")
        sigc_done = sem("sigc_done")
        siluc_done = sem("siluc_done")
        mod_ready = sem("mod_ready")
        modT_done = sem("modT_done")
        gate_rows_ready = sem("gate_rows_ready")
        guard = sem("guard")
        rate_done = sem("rate_done")
        win_split = sem("win_split")
        z_ready = sem("z_ready")
        step_done = sem("step_done")
        exp_done = sem("exp_done")
        ones_done = sem("ones_done")
        cum_ready = sem("cum_ready")
        gT_ready = sem("gT_ready")
        gT_copied = sem("gT_copied")
        stored = sem("stored")
        block = ctx.enter_context(nc.Block())
        MOD_ORDER = [SA, CA, SB, CB, GA, GB]
        SLOT = {SA: 0, CA: 1, SB: 2, CB: 3}

        @block.sync
        def _(sp):
            sp.dma_start(cT[:], cT_in).then_inc(c_loaded, 16)
            for half in range(2):
                a = half * NT // 2
                sp.dma_start(x1[:, a:a + NT // 2], x_in[a:a + NT // 2].rearrange("t p n -> p t n"))\
                    .then_inc(x_loaded[half], 16)
            for m in MOD_ORDER:
                sp.dma_start(wmod[:, m], wmod_in[m]).then_inc(wmod_loaded[m], 16)
            sp.wait_ge(guard, 6)
            for i in range(2):
                sp.dma_start(modrow[i].rearrange("(b n) -> b n", b=B), gates[:, i]).then_inc(stored, 16)
            sp.wait_ge(gT_copied, 2)
            sp.dma_start(gT_dram, gT[:]).then_inc(stored, 16)
            sp.wait_ge(stored, 48)

        @block.gpsimd
        def _(pool):
            nc.gpsimd.memset(ones[:], 1.0).then_inc(ones_done, 1)

        @block.scalar
        def _(act):
            act.dma_start(cst[:], cst_in).then_inc(cst_in_s, 16)
            act.dma_start(win[:], win_in).then_inc(small_loaded, 16)
            act.dma_start(rows[:], rows_in.partition_broadcast(P)).then_inc(small_loaded, 16)
            act.dma_start(gnorm[:], gnorm_in).then_inc(small_loaded, 16)
            nc.scalar.preload_act_table_set("natural_log_exp_and_others")
            act.wait_ge(c_loaded, 16)
            nc.scalar.activation(sig_c[:], cT[:], ACT.Exp, scale=-1.0).then_inc(sigc_done, 1)
            act.wait_ge(small_loaded, 48)
            nc.scalar.activation(rate[:], rows[:, 1], ACT.Exp).then_inc(rate_done, 1)
            norm.scalar_rstd(act)
            act.wait_ge(modT_done, 2)
            for t in range(NT):
                norm.scalar_modulate(act, t)
            act.wait_ge(step_done, 3)
            nc.scalar.activation(za[:], za[:], ACT.Exp, scale=-1.0).then_inc(exp_done, 1)
            act.wait_ge(cum_ready, 1)
            nc.scalar.activation(tok[:, :, 0], ps_g[:, 0], ACT.Copy, scale=-1.0).then_inc(exp_done, 1)
            for i in range(2):
                act.wait_ge(gT_ready, i + 1)
                nc.scalar.activation(gT[:, i * HALF:(i + 1) * HALF], ps_gt[i][:], ACT.Copy)\
                    .then_inc(gT_copied, 1)
            act.wait_ge(step_done, 17)
            nc.scalar.activation(zs[:], zs[:], ACT.Exp).then_inc(exp_done, 1)

        @block.vector
        def _(dve):
            dve.wait_ge(sigc_done, 1)
            nc.vector.tensor_scalar(sig_c[:], sig_c[:], 1.0, None, ALU.add).then_inc(siluc_done, 1)
            dve.wait_ge(siluc_done, 1)
            nc.vector.reciprocal(silu_c[:], sig_c[:]).then_inc(siluc_done, 1)
            dve.wait_ge(siluc_done, 2)
            nc.vector.tensor_tensor(silu_c[:], silu_c[:], cT[:], ALU.mult).then_inc(siluc_done, 1)
            for t in range(NT):
                if t % (NT // 2) == 0:
                    dve.wait_ge(x_loaded[t // (NT // 2)], 16)
                norm.vector_stats(dve, t)
            norm.vector_var(dve)
            dve.wait_ge(small_loaded, 48)
            split_hi(nc.vector, win_hi[:], win[:]).then_inc(win_split, 1)
            dve.wait_ge(win_split, 1)
            split_lo(nc.vector, win_lo[:], win[:], win_hi[:]).then_inc(win_split, 1)
            dve.wait_ge(mod_ready, 2)
            nc.vector.tensor_copy(modT[:, 0], ps_mod[:, 0]).then_inc(modT_done, 1)
            nc.vector.tensor_scalar(modT[:, 1], ps_mod[:, 1], 1.0, None, ALU.add).then_inc(modT_done, 1)
            norm.vector_all(dve)
            dve.wait_ge(mod_ready, 4)
            nc.vector.tensor_copy(modT[:, 2], ps_mod[:, 2]).then_inc(modT_done, 1)
            nc.vector.tensor_scalar(modT[:, 3], ps_mod[:, 3], 1.0, None, ALU.add).then_inc(modT_done, 1)
            dve.wait_ge(z_ready, 1)
            nc.vector.tensor_tensor(z[:], ps_g[:, 0], rows[:, 0].unsqueeze(1).broadcast_to([P, NT, H]),
                                    ALU.add).then_inc(step_done, 1)
            dve.wait_ge(step_done, 1)
            nc.vector.tensor_scalar(za[:], z[:], -1.0, None, ALU.mult).then_inc(step_done, 1)
            dve.wait_ge(step_done, 2)
            nc.vector.tensor_tensor(za[:], za[:], z[:], ALU.max).then_inc(step_done, 1)
            dve.wait_ge(exp_done, 1)
            nc.vector.tensor_scalar(zs2[:], za[:], 2.0, None, ALU.add).then_inc(step_done, 1)
            dve.wait_ge(step_done, 4)
            nc.vector.reciprocal(zs[:], zs2[:]).then_inc(step_done, 1)
            dve.wait_ge(step_done, 5)
            nc.vector.tensor_tensor(zs[:], zs[:], za[:], ALU.mult).then_inc(step_done, 1)
            dve.wait_ge(step_done, 6)
            nc.vector.tensor_tensor(zs2[:], zs[:], zs[:], ALU.mult).then_inc(step_done, 1)
            dve.wait_ge(step_done, 7)
            nc.vector.tensor_scalar(zq[:], zs2[:], 1.0 / 15, None, ALU.mult).then_inc(step_done, 1)
            dve.wait_ge(step_done, 8)
            for n, odd in enumerate((13, 11, 9, 7, 5, 3)):
                nc.vector.scalar_tensor_tensor(zq[:], zq[:], 1.0 / odd, zs2[:], ALU.add, ALU.mult)\
                    .then_inc(step_done, 1)
                dve.wait_ge(step_done, 9 + n)
            nc.vector.scalar_tensor_tensor(zq[:], zq[:], 1.0, zs[:], ALU.add, ALU.mult)\
                .then_inc(step_done, 1)
            nc.vector.tensor_scalar(z[:], z[:], 0.0, None, ALU.max)
            dve.wait_ge(step_done, 15)
            nc.vector.tensor_scalar(zq[:], zq[:], 2.0, None, ALU.mult).then_inc(step_done, 1)
            dve.wait_ge(step_done, 16)
            nc.vector.tensor_tensor(tok[:, :, 1], zq[:], z[:], ALU.add).then_inc(rate_done, 1)
            dve.wait_ge(rate_done, 2)
            nc.vector.scalar_tensor_tensor(gdec[:], tok[:, :, 1], -1.0,
                                           rate[:].unsqueeze(1).broadcast_to([P, NT, H]),
                                           ALU.mult, ALU.mult).then_inc(rate_done, 1)
            dve.wait_ge(cum_ready, 1)
            dve.wait_ge(exp_done, 2)
            nc.vector.tensor_tensor(zs[:], ps_g[:, 1], tok[:, :, 0], ALU.add).then_inc(step_done, 1)
            dve.wait_ge(gate_rows_ready, 2)
            for i in range(2):
                nc.vector.tensor_scalar(gneg[:, i], ps_gate[i][:], -1.0, None, ALU.mult)\
                    .then_inc(guard, 1)
            dve.wait_ge(guard, 2)
            for i in range(2):
                nc.vector.tensor_tensor(gmag[:, i], gneg[:, i], ps_gate[i][:], ALU.max)
                nc.vector.tensor_scalar(gates[:, i], ps_gate[i][:], 0.0, 2.0, ALU.is_ge, ALU.mult)\
                    .then_inc(guard, 1)
            dve.wait_ge(guard, 4)
            nc.vector.tensor_scalar(gmag[:], gmag[:], 0.25, None, ALU.max)
            nc.vector.tensor_scalar(gates[:], gates[:], -1.0, None, ALU.add).then_inc(guard, 1)
            dve.wait_ge(guard, 5)
            nc.vector.tensor_tensor(gates[:], gates[:], gmag[:], ALU.mult).then_inc(guard, 1)
            dve.wait_ge(exp_done, 3)
            nc.vector.tensor_tensor(tok[:, :, 2], zs[:], tok[:, :, 1], ALU.mult).then_inc(step_done, 1)

        @block.tensor
        def _(pe):
            pe.wait_ge(siluc_done, 3)

            def mod_columns(m):
                pe.wait_ge(wmod_loaded[m], 16)
                for n in range(KT):
                    for k in range(KT):
                        last = nc.tensor.matmul(ps_mod[:, SLOT[m], n], wmod[:, m, k, n * P:(n + 1) * P],
                                                silu_c[:, k * B:(k + 1) * B], start=k == 0,
                                                stop=k == KT - 1)
                last.then_inc(mod_ready, 1)

            mod_columns(SA)
            mod_columns(CA)
            pe.wait_ge(cst_in_s, 16)
            for t in range(NT):
                norm.tensor_turn(pe, t)
            mod_columns(SB)
            mod_columns(CB)
            pe.wait_ge(win_split, 2)
            for t in range(NT):
                pe.wait_ge(norm.lo_done, t + 1)
                for k in range(KT):
                    cut = slice(t * P, (t + 1) * P)
                    last = three_products(nc.tensor, ps_g[:, 0, t], hT_hi[:, k, cut], hT_lo[:, k, cut],
                                          win_hi[:, k], win_lo[:, k], k == 0, k == KT - 1)
            last.then_inc(z_ready, 1)
            for i, m in enumerate((GA, GB)):
                pe.wait_ge(wmod_loaded[m], 16)
                for k in range(KT):
                    last = nc.tensor.matmul(ps_gate[i][:], silu_c[:, k * B:(k + 1) * B],
                                            wmod[:, m, k], start=k == 0, stop=k == KT - 1)
                last.then_inc(gate_rows_ready, 1)
            pe.wait_ge(rate_done, 3)
            pe.wait_ge(ones_done, 1)
            tri = cst[:, C_TRI:C_TRI + P]
            nc.tensor.matmul(ps_g[:, 0], tri, gdec[:], start=True, stop=True)
            nc.tensor.matmul(ps_g[:, 1], ones[:], gdec[:], start=True, stop=True).then_inc(cum_ready, 1)
            for t in range(NT):
                i, col = t // 4, t % 4 * P
                last = nc.tensor.matmul(ps_gt[i][:, col:col + P], gdec[:, t], tri, start=True, stop=True)
                if t % 4 == 3:
                    last.then_inc(gT_ready, 1)


def block_attention(nc, cst, x1, hT_hi, hT_lo, tok, gnorm, ident, gT_dram,
                    wq_in, wg_in, wkv_in, wo_in):
    with ExitStack() as ctx:
        def sb(name, shape, dt=F32):
            return ctx.enter_context(nc.sbuf_tensor(name, shape, dt))

        def ps(name):
            return ctx.enter_context(nc.psum_tensor(name, [P, HALF], F32))

        def sem(name):
            return ctx.enter_context(nc.semaphore(name))

        wq_hi, wq_lo = (sb(n, [P, GRP, KT, D], F32R) for n in ("wq_hi", "wq_lo"))
        wg_hi, wg_lo = (sb(n, [P, GRP, KT, D], F32R) for n in ("wg_hi", "wg_lo"))
        wkv_hi, wkv_lo = (sb(n, [P, KT, 2 * D], F32R) for n in ("wkv_hi", "wkv_lo"))
        wo_hi, wo_lo = (sb(n, [P, GRP, HID], F32R) for n in ("wo_hi", "wo_lo"))
        raw_q, raw_g = sb("raw_q", [P, KT, D]), sb("raw_g", [P, KT, D])
        raw_kv, raw_o = sb("raw_kv", [P, KT, 2 * D]), sb("raw_o", [P, GRP, HID])
        qT = sb("qT", [P, 2, GRP, HALF])
        sg = sb("sg", [P, 2, GRP, HALF])
        dec = sb("dec", [P, 2, GRP, CPB, CHUNK])
        kr = sb("kr", [P, 2, CPB, D])
        v = sb("v", [P, 2, CPB, D])
        kT = sb("kT", [P, 2, CPB * CHUNK])
        qe = sb("qe", [P, 2, GRP, CHUNK])
        scal = sb("scal", [P, NT, 3, GRP])
        vw = sb("vw", [P, GRP, D])
        state = sb("state", [P, GRP, D])
        prob = sb("prob", [P, GRP, CHUNK])
        sq, sq_hi, sq_lo = sb("sq", [P, HALF]), sb("sq_hi", [P, HALF], F32R), sb("sq_lo", [P, HALF], F32R)
        rms = sb("rms", [P, HALF])
        z = sb("z_att", [P, GRP, CHUNK])
        z_hi, z_lo = sb("z_hi", [P, GRP, CHUNK], F32R), sb("z_lo", [P, GRP, CHUNK], F32R)
        sig = sb("sig", [P, HALF])
        q_cos, q_sin = sb("q_cos", [P, HALF]), sb("q_sin", [P, HALF])
        k_cos, k_sin = sb("k_cos", [P, CPB, D]), sb("k_sin", [P, CPB, D])
        ones = sb("ones_r", [P, P], F32R)
        eps_col = sb("eps_col", [P, 1])
        future = sb("future", [P, CHUNK])
        ps_q, ps_g, ps_kv, ps_s, ps_y, ps_st, ps_ss, ps_o = (
            ps(n) for n in ("ps_q", "ps_gt", "ps_kv", "ps_s", "ps_y", "ps_st", "ps_ss", "ps_o"))

        cosT = cst[:, C_COST:C_COST + L].unsqueeze(1).broadcast_to([P, 2, L])
        sinT = cst[:, C_SINT:C_SINT + L].unsqueeze(1).broadcast_to([P, 2, L])
        cos_k = cst[:, C_COS:C_COS + L].rearrange("p (c d) -> p c d", c=CPB)
        sin_k = cst[:, C_SIN:C_SIN + L].rearrange("p (c d) -> p c d", c=CPB)

        wh_loaded = sem("wh_loaded")
        kv_loaded = sem("kv_loaded")
        wo_loaded = sem("wo_loaded")
        dec_loaded = sem("dec_loaded")
        wh_hi_done = sem("wh_hi_done")
        wh_split = sem("wh_split")
        kv_hi_done = sem("kv_hi_done")
        kv_split = sem("kv_split")
        wo_hi_done = sem("wo_hi_done")
        wo_split = sem("wo_split")
        q_ready = sem("q_ready")
        g_ready = sem("g_ready")
        kv_ready = sem("kv_ready")
        kt_ready = sem("kt_ready")
        s_ready = sem("s_ready")
        y_ready = sem("y_ready")
        st_ready = sem("st_ready")
        ss_ready = sem("ss_ready")
        o_ready = sem("o_ready")
        swap_done = sem("swap_done")
        qsin_done = sem("qsin_done")
        qcos_done = sem("qcos_done")
        rope_done = sem("rope_done")
        esig_done = sem("esig_done")
        cap_done = sem("cap_done")
        lsig_done = sem("lsig_done")
        sig_done = sem("sig_done")
        sg_done = sem("sg_done")
        kparts_done = sem("kparts_done")
        kr_done = sem("kr_done")
        v_done = sem("v_done")
        kT_done = sem("kT_done")
        scal_done = sem("scal_done")
        expg_done = sem("expg_done")
        mask_done = sem("mask_done")
        dec_done = sem("dec_done")
        vw_done = sem("vw_done")
        qe_done = sem("qe_done")
        state_done = sem("state_done")
        prob_done = sem("prob_done")
        sq_done = sem("sq_done")
        sqhi_done = sem("sqhi_done")
        sqlo_done = sem("sqlo_done")
        zz_done = sem("zz_done")
        lnss_done = sem("lnss_done")
        rms_done = sem("rms_done")
        z_done = sem("z_done")
        zhi_done = sem("zhi_done")
        zlo_done = sem("zlo_done")
        zeros_done = sem("zeros_done")
        future_done = sem("future_done")
        ones_done = sem("ones_done_r")
        sums_done = sem("sums_done")
        block = ctx.enter_context(nc.Block())

        def rows_of(t):
            return slice(t % 4 * P, t % 4 * P + P)

        def group_slice(g, b, size):
            g = g + 1 if b == B - 1 else g
            return bass.ds(g * size, size)

        def groups(engine, step):
            with engine.Fori(0, KVH - 1) as g:
                for t in range(NT):
                    step(g, t, True, True, True)
            for t in range(NT):
                step(KVH - 1, t, t < 4, t < NT - 2, False)

        @block.sync
        def _(sp):
            def load_head(g, j, first=False):
                if not first:
                    sp.wait_ge(wh_split, g * 4 + j)
                sp.dma_start(raw_q[:], wq_in[bass.ds(g * 4 + j, 1)].rearrange("o p k d -> (o p) k d"))\
                    .then_inc(wh_loaded, 16)
                sp.dma_start(raw_g[:], wg_in[bass.ds(g * 4 + j, 1)].rearrange("o p k d -> (o p) k d"))\
                    .then_inc(wh_loaded, 16)

            def load_kv(g):
                sp.dma_start(raw_kv[:], wkv_in[bass.ds(g, 1)].rearrange("o p k d -> (o p) k d"))\
                    .then_inc(kv_loaded, 16)

            def load_o(g):
                sp.dma_start(raw_o[:], wo_in[bass.ds(g, 1)].rearrange("o p h n -> (o p) h n"))\
                    .then_inc(wo_loaded, 16)

            def load_dec(g, b):
                bn = (b + 1) % B
                src = gT_dram[group_slice(g, b, GRP), bn * L:(bn + 1) * L]
                sp.dma_start(dec[:, bn % 2].rearrange("p h c i -> p h (c i)"),
                             src.partition_broadcast(P)).then_inc(dec_loaded, 16)

            load_kv(0)
            load_head(0, 0, True)
            load_dec(0, -1)
            for j in range(1, GRP):
                load_head(0, j)
            load_o(0)

            def step(g, t, project, next_batch, next_group):
                if t % 2 == 0 and next_batch:
                    sp.wait_ge(s_ready, g * 8 + (t + 1))
                    load_dec(g, t // 2)
                if next_group and t < GRP:
                    load_head(g + 1, t)
                if next_group and t == 1:
                    sp.wait_ge(wo_split, g + 2)
                    load_o(g + 1)
                if next_group and t == 2:
                    sp.wait_ge(kv_split, g + 1)
                    load_kv(g + 1)

            groups(sp, step)

        @block.tensor
        def _(pe):
            def q_block(g, t, first=False):
                half, j = (t // 4 + 1) % 2, t % 4
                gw = g + 1 if t >= 4 else g
                pe.wait_ge(wh_split, gw * 4 + (j + 1))
                if not first:
                    pe.wait_ge(qcos_done, g * 8 + (t + 4))
                for k in range(KT):
                    cut = slice(half * HALF, (half + 1) * HALF)
                    last = three_products(nc.tensor, ps_q[:], wq_hi[:, j, k], wq_lo[:, j, k],
                                          hT_hi[:, k, cut], hT_lo[:, k, cut], k == 0, k == KT - 1)
                last.then_inc(q_ready, 1)

            def g_block(g, t, k_from, k_to, first=False):
                half, j = (t // 4 + 1) % 2, t % 4
                if k_from == 0 and not first:
                    pe.wait_ge(sg_done, g * 8 + (t + 4))
                for k in range(k_from, k_to):
                    cut = slice(half * HALF, (half + 1) * HALF)
                    last = three_products(nc.tensor, ps_g[:], wg_hi[:, j, k], wg_lo[:, j, k],
                                          hT_hi[:, k, cut], hT_lo[:, k, cut], k == 0, k == KT - 1)
                if k_to == KT:
                    last.then_inc(g_ready, 1)

            def kv_batch(g, b):
                bn = (b + 1) % B
                gw = g + 1 if b == B - 1 else g
                pe.wait_ge(kv_split, gw + 1)
                if b >= 0:
                    pe.wait_ge(kT_done, g * 4 + (b + 1))
                for c in range(CPB):
                    cut = slice((bn * CPB + c) * P, (bn * CPB + c + 1) * P)
                    for k in range(KT):
                        last = three_products(nc.tensor, ps_kv[:, c * 2 * D:(c + 1) * 2 * D],
                                              hT_hi[:, k, cut], hT_lo[:, k, cut],
                                              wkv_hi[:, k], wkv_lo[:, k], k == 0, k == KT - 1)
                last.then_inc(kv_ready, 1)

            def k_turn(g, b):
                pe.wait_ge(kr_done, g * 4 + (b + 2))
                pe.wait_ge(v_done, g * 4 + (b + 2))
                for c in range(CPB):
                    last = nc.tensor.transpose(ps_kv[:, c * P:(c + 1) * P], kr[:, (b + 1) % 2, c], ident)
                last.then_inc(kt_ready, 1)

            def out_product(g, t):
                pe.wait_ge(zhi_done, g * 8 + (t + 1))
                pe.wait_ge(zlo_done, g * 8 + (t + 1))
                if t <= 1:
                    pe.wait_ge(wo_split, g + (t + 1))
                for h in range(GRP):
                    last = three_products(nc.tensor, ps_o[:], z_hi[:, h], z_lo[:, h],
                                          wo_hi[:, h], wo_lo[:, h], h == 0, h == GRP - 1)
                last.then_inc(o_ready, 1)

            kv_batch(0, -1)
            for t in range(-4, 0):
                q_block(0, t, t == -4)
                g_block(0, t, 0, KT, t == -4)
                if t == -4:
                    k_turn(0, -1)
            pe.wait_ge(ones_done, 1)

            def step(g, t, project, next_batch, next_group):
                b, c, half = t // 2, t % 2, t // 4
                pe.wait_ge(kT_done, g * 4 + (b + 1))
                pe.wait_ge(rope_done, g * 8 + (4 * half + 4))
                nc.tensor.matmul(ps_s[:].rearrange("p (h i) -> p h i", h=GRP),
                                 kT[:, b % 2, c * P:(c + 1) * P], qT[:, half, :, rows_of(t)],
                                 start=True, stop=True).then_inc(s_ready, 1)
                if project:
                    q_block(g, t)
                out_product(g, t)
                if c == 1 and next_batch:
                    k_turn(g, b)
                if c == 1:
                    pe.wait_ge(qe_done, g * 4 + (b + 1))
                    pe.wait_ge(state_done, g * 4 + (b + 1))
                    for h in range(GRP):
                        nc.tensor.matmul(ps_y[:, h * P:(h + 1) * P], state[:, h], qe[:, b % 2, h],
                                         start=h == 0, stop=False)
                pe.wait_ge(prob_done, g * 8 + (t + 1))
                nc.tensor.matmul(ps_y[:].rearrange("p (h i) -> p h i", h=GRP), v[:, b % 2, c], prob[:],
                                 start=c == 0, stop=True).then_inc(y_ready, 1)
                if c == 0:
                    pe.wait_ge(vw_done, g * 4 + (b + 1))
                    nc.tensor.matmul(ps_st[:].rearrange("p (h e) -> p h e", h=GRP), kr[:, b % 2, 0],
                                     vw[:], start=True, stop=True).then_inc(st_ready, 1)
                if project:
                    g_block(g, t, 0, KT - 1)
                pe.wait_ge(sqhi_done, g * 8 + (t + 1))
                nc.tensor.matmul(ps_ss[:], ones[:], sq_hi[:], start=True, stop=False)
                pe.wait_ge(sqlo_done, g * 8 + (t + 1))
                nc.tensor.matmul(ps_ss[:], ones[:], sq_lo[:], start=False, stop=True)\
                    .then_inc(ss_ready, 1)
                if project:
                    g_block(g, t, KT - 1, KT)
                if c == 0 and next_batch:
                    kv_batch(g, b)

            groups(pe, step)
            out_product(KVH - 1, NT)

        @block.scalar
        def _(act):
            def swap(g, t, first=False):
                act.wait_ge(q_ready, g * 8 + (t + 5))
                if not first:
                    act.wait_ge(rope_done, g * 8 + (t + 4))
                nc.scalar.activation(q_sin[0:64], ps_q[64:128, :], ACT.Copy)
                nc.scalar.activation(q_sin[64:128], ps_q[0:64, :], ACT.Copy).then_inc(swap_done, 1)

            def exp_gate(g, t):
                act.wait_ge(g_ready, g * 8 + (t + 5))
                nc.scalar.activation(sig[:], ps_g[:], ACT.Exp, scale=-1.0).then_inc(esig_done, 1)

            def sigmoid(g, t):
                act.wait_ge(cap_done, g * 8 + (t + 5))
                nc.scalar.activation(sig[:], sig[:], ACT.Ln, bias=1.0).then_inc(lsig_done, 1)
                act.wait_ge(lsig_done, g * 8 + (t + 5))
                nc.scalar.activation(sig[:], sig[:], ACT.Exp, scale=-1.0).then_inc(sig_done, 1)

            def exp_g(g, b):
                par = (b + 1) % 2
                act.wait_ge(dec_loaded, g * 64 + 16 * (b + 2))
                nc.scalar.activation(qe[:, par], dec[:, par, :, 1], ACT.Exp).then_inc(expg_done, 1)

            def decays(g, b):
                bn = (b + 1) % B
                act.wait_ge(mask_done, g * 4 + (b + 2))
                act.wait_ge(scal_done, g * 4 + (b + 2))
                for h in range(GRP):
                    for c in range(CPB):
                        cell = dec[:, bn % 2, h, c]
                        last = nc.scalar.activation(cell, cell, ACT.Exp,
                                                    bias=scal[:, bn * CPB + c, 0, h:h + 1])
                last.then_inc(dec_done, 1)

            def copy_v(g, b):
                act.wait_ge(kv_ready, g * 4 + (b + 2))
                nc.scalar.activation(v[:, (b + 1) % 2],
                                     ps_kv[:].rearrange("p (c d) -> p c d", c=CPB)[:, :, D:2 * D],
                                     ACT.Copy).then_inc(v_done, 1)

            def copy_kT(g, b):
                act.wait_ge(kt_ready, g * 4 + (b + 2))
                nc.scalar.activation(kT[:, (b + 1) % 2], ps_kv[:, 0:CPB * P], ACT.Copy)\
                    .then_inc(kT_done, 1)

            nc.scalar.preload_act_table_set("natural_log_exp_and_others")
            copy_v(0, -1)
            exp_g(0, -1)
            for t in range(-4, 0):
                swap(0, t, t == -4)
                exp_gate(0, t)
                sigmoid(0, t)
                if t == -4:
                    copy_kT(0, -1)
                    decays(0, -1)
            act.wait_ge(ones_done, 1)

            def step(g, t, project, next_batch, next_group):
                b, c = t // 2, t % 2
                if project:
                    swap(g, t)
                if c == 1 and next_batch:
                    decays(g, b)
                act.wait_ge(y_ready, g * 8 + (t + 1))
                nc.scalar.activation(sq[:], ps_y[:], ACT.Square).then_inc(sq_done, 1)
                nc.scalar.activation(sq_hi[:], ps_y[:], ACT.Square).then_inc(sqhi_done, 1)
                if c == 0:
                    act.wait_ge(st_ready, g * 4 + (b + 1))
                    nc.scalar.activation(state[:].rearrange("p h e -> p (h e)"), ps_st[:], ACT.Copy)\
                        .then_inc(state_done, 1)
                if c == 0 and next_batch:
                    exp_g(g, b)
                if c == 1 and next_batch:
                    copy_kT(g, b)
                act.wait_ge(ss_ready, g * 8 + (t + 1))
                nc.scalar.activation(rms[:], ps_ss[:], ACT.Ln, bias=eps_col[:], scale=1.0 / D)\
                    .then_inc(lnss_done, 1)
                act.wait_ge(lnss_done, g * 8 + (t + 1))
                nc.scalar.activation(rms[:], rms[:], ACT.Exp, scale=-0.5).then_inc(rms_done, 1)
                if project:
                    exp_gate(g, t)
                act.wait_ge(z_done, g * 8 + (t + 1))
                nc.scalar.activation(z_hi[:], z[:], ACT.Copy).then_inc(zhi_done, 1)
                if project:
                    sigmoid(g, t)
                if c == 0 and next_batch:
                    copy_v(g, b)

            groups(act, step)

        @block.vector
        def _(dve):
            def split_head(g, j):
                dve.wait_ge(wh_loaded, g * 128 + 32 * (j + 1))
                split_hi(nc.vector, wq_hi[:, j], raw_q[:])
                split_hi(nc.vector, wg_hi[:, j], raw_g[:]).then_inc(wh_hi_done, 1)
                dve.wait_ge(wh_hi_done, g * 4 + (j + 1))
                split_lo(nc.vector, wq_lo[:, j], raw_q[:], wq_hi[:, j])
                split_lo(nc.vector, wg_lo[:, j], raw_g[:], wg_hi[:, j]).then_inc(wh_split, 1)

            def split_kv(g):
                dve.wait_ge(kv_loaded, g * 16 + 16)
                split_hi(nc.vector, wkv_hi[:], raw_kv[:]).then_inc(kv_hi_done, 1)
                dve.wait_ge(kv_hi_done, g + 1)
                split_lo(nc.vector, wkv_lo[:], raw_kv[:], wkv_hi[:]).then_inc(kv_split, 1)

            def split_o_hi(g):
                dve.wait_ge(wo_loaded, g * 16 + 16)
                split_hi(nc.vector, wo_hi[:], raw_o[:]).then_inc(wo_hi_done, 1)

            def split_o_lo(g):
                dve.wait_ge(wo_hi_done, g + 1)
                split_lo(nc.vector, wo_lo[:], raw_o[:], wo_hi[:]).then_inc(wo_split, 1)

            def copy_scalars(g, b):
                t0 = (b + 1) % B * CPB
                nc.vector.tensor_copy(scal[:, t0:t0 + CPB],
                                      tok[:, t0:t0 + CPB, :, group_slice(g, b, GRP)])\
                    .then_inc(scal_done, 1)

            def rotate_k(g, b):
                ps_k = ps_kv[:].rearrange("p (c d) -> p c d", c=CPB)
                dve.wait_ge(v_done, g * 4 + (b + 2))
                nc.vector.tensor_tensor(k_cos[:], ps_k[:, :, 0:D], cos_k, ALU.mult)
                nc.vector.tensor_tensor(k_sin[:, :, 0:64], ps_k[:, :, 64:128], sin_k[:, :, 0:64],
                                        ALU.mult)
                nc.vector.tensor_tensor(k_sin[:, :, 64:128], ps_k[:, :, 0:64], sin_k[:, :, 64:128],
                                        ALU.mult).then_inc(kparts_done, 1)
                dve.wait_ge(kparts_done, g * 4 + (b + 2))
                nc.vector.tensor_tensor(kr[:, (b + 1) % 2], k_cos[:], k_sin[:], ALU.add)\
                    .then_inc(kr_done, 1)

            def rotate_q_cos(g, t):
                dve.wait_ge(swap_done, g * 8 + (t + 5))
                nc.vector.tensor_tensor(q_cos[:].rearrange("p (b i) -> p b i", b=2),
                                        ps_q[:].rearrange("p (b i) -> p b i", b=2), cosT, ALU.mult)\
                    .then_inc(qcos_done, 1)

            def rotate_q_add(g, t):
                half, j = (t // 4 + 1) % 2, t % 4
                dve.wait_ge(qcos_done, g * 8 + (t + 5))
                dve.wait_ge(qsin_done, g * 8 + (t + 5))
                nc.vector.tensor_tensor(qT[:, half, j], q_cos[:], q_sin[:], ALU.add)\
                    .then_inc(rope_done, 1)

            def cap(g, t):
                dve.wait_ge(esig_done, g * 8 + (t + 5))
                nc.vector.tensor_scalar(sig[:], sig[:], EXP_CAP, None, ALU.min).then_inc(cap_done, 1)

            def gate(g, t):
                half, j = (t // 4 + 1) % 2, t % 4
                dve.wait_ge(sig_done, g * 8 + (t + 5))
                nc.vector.scalar_tensor_tensor(sg[:, half, j], ps_g[:], gnorm[:], sig[:],
                                               ALU.mult, ALU.mult).then_inc(sg_done, 1)

            def add_out(g, t):
                dve.wait_ge(o_ready, g * 8 + (t + 1))
                nc.vector.tensor_tensor(x1[:, (t - 1) % NT], x1[:, (t - 1) % NT], ps_o[:], ALU.add)\
                    .then_inc(sums_done, 1)

            split_kv(0)
            split_head(0, 0)
            copy_scalars(0, -1)
            rotate_k(0, -1)
            split_head(0, 1)
            for t in range(-4, 0):
                rotate_q_cos(0, t)
                rotate_q_add(0, t)
                if t < -2:
                    split_head(0, t + 6)
                cap(0, t)
                gate(0, t)
            dve.wait_ge(zeros_done, 1)

            def step(g, t, project, next_batch, next_group):
                b, c, half = t // 2, t % 2, t // 4
                dve.wait_ge(s_ready, g * 8 + (t + 1))
                dve.wait_ge(dec_done, g * 4 + (b + 1))
                for h in range(GRP):
                    last = nc.vector.scalar_tensor_tensor(
                        prob[:, h], ps_s[:, h * P:(h + 1) * P], scal[:, t, 1, h:h + 1],
                        dec[:, b % 2, h, c], ALU.mult, ALU.mult)
                last.then_inc(prob_done, 1)
                if c == 1 and next_batch:
                    rotate_k(g, b)
                if project:
                    rotate_q_cos(g, t)
                if next_group and 1 <= t <= GRP:
                    split_head(g + 1, t - 1)
                if next_group and t == GRP + 1:
                    split_kv(g + 1)
                if project:
                    rotate_q_add(g, t)
                add_out(g, t)
                dve.wait_ge(sqhi_done, g * 8 + (t + 1))
                split_lo(nc.vector, sq_lo[:], sq[:], sq_hi[:]).then_inc(sqlo_done, 1)
                dve.wait_ge(sg_done, g * 8 + (4 * half + 4))
                nc.vector.tensor_tensor(z[:], ps_y[:].rearrange("p (h i) -> p h i", h=GRP),
                                        sg[:, half, :, rows_of(t)], ALU.mult).then_inc(zz_done, 1)
                if c == 0 and next_batch:
                    copy_scalars(g, b)
                if t == 0:
                    split_o_hi(g)
                dve.wait_ge(zz_done, g * 8 + (t + 1))
                dve.wait_ge(rms_done, g * 8 + (t + 1))
                nc.vector.tensor_tensor(z[:], z[:], rms[:].rearrange("p (h i) -> p h i", h=GRP),
                                        ALU.mult).then_inc(z_done, 1)
                if project:
                    cap(g, t)
                dve.wait_ge(zhi_done, g * 8 + (t + 2))
                split_lo(nc.vector, z_lo[:], z[:], z_hi[:]).then_inc(zlo_done, 1)
                if t == 0:
                    split_o_lo(g)
                if project:
                    gate(g, t)

            groups(dve, step)
            add_out(KVH - 1, NT)

        @block.gpsimd
        def _(pool):
            def mask(g, b):
                cells = dec[:, (b + 1) % 2].rearrange("p h c i -> p (h c) i")
                pool.wait_ge(expg_done, g * 4 + (b + 2))
                nc.gpsimd.tensor_tensor(cells, cells,
                                        future[:].unsqueeze(1).broadcast_to([P, GRP * CPB, CHUNK]),
                                        ALU.add).then_inc(mask_done, 1)

            def rotate_q_sin(g, t):
                pool.wait_ge(swap_done, g * 8 + (t + 5))
                q2 = q_sin[:].rearrange("p (b i) -> p b i", b=2)
                nc.gpsimd.tensor_tensor(q2, q2, sinT, ALU.mult).then_inc(qsin_done, 1)

            def weigh_v(g, b):
                bn = (b + 1) % B
                pool.wait_ge(v_done, g * 4 + (b + 2))
                pool.wait_ge(scal_done, g * 4 + (b + 2))
                nc.gpsimd.tensor_tensor(
                    vw[:], v[:, bn % 2, 0].unsqueeze(1).broadcast_to([P, GRP, D]),
                    scal[:, bn * CPB, 2].unsqueeze(2).broadcast_to([P, GRP, D]), ALU.mult)\
                    .then_inc(vw_done, 1)

            def weigh_q(g, b):
                bn = (b + 1) % B
                pool.wait_ge(rope_done, g * 8 + (4 * ((b + 1) // 2) + 4))
                at = (bn % 2 * CPB + 1) * P
                nc.gpsimd.tensor_tensor(qe[:, bn % 2], qe[:, bn % 2], qT[:, bn // 2, :, at:at + P],
                                        ALU.mult).then_inc(qe_done, 1)

            nc.gpsimd.memset(eps_col[:], EPS)
            nc.gpsimd.memset(future[:], 0.0).then_inc(future_done, 1)
            nc.gpsimd.memset(ones[:].bitcast(F32), 1.0).then_inc(ones_done, 1)
            nc.gpsimd.memset(x1[:], 0.0).then_inc(zeros_done, 1)
            nc.gpsimd.memset(wo_hi[:].bitcast(F32), 0.0)
            nc.gpsimd.memset(wo_lo[:].bitcast(F32), 0.0).then_inc(wo_split, 1)
            nc.gpsimd.memset(z_hi[:].bitcast(F32), 0.0).then_inc(zhi_done, 1)
            nc.gpsimd.memset(z_lo[:].bitcast(F32), 0.0).then_inc(zlo_done, 1)
            pool.wait_ge(future_done, 1)
            nc.gpsimd.affine_select(out=future[:], in_=future[:], compare_op=ALU.is_ge, fill=MASKED,
                                    base=0, pattern=[[1, CHUNK]], channel_multiplier=-1)\
                .then_inc(future_done, 1)
            pool.wait_ge(future_done, 2)
            mask(0, -1)
            for t in range(-4, 0):
                rotate_q_sin(0, t)
                if t == -4:
                    weigh_v(0, -1)
            weigh_q(0, -1)

            def step(g, t, project, next_batch, next_group):
                b, c = t // 2, t % 2
                if project:
                    rotate_q_sin(g, t)
                if c == 1 and next_batch:
                    weigh_v(g, b)
                    weigh_q(g, b)
                if c == 0 and next_batch:
                    mask(g, b)

            groups(pool, step)


def block_ffn(nc, x1, hT_hi, hT_lo, modT, ident, modrow, x_in, wgu_in, wd_in, out):
    with ExitStack() as both:
        def sb2(name, shape, dt=F32):
            return both.enter_context(nc.sbuf_tensor(name, shape, dt))

        a_hi, a_lo = sb2("a_hi", [P, IT, B * L], F32R), sb2("a_lo", [P, IT, B * L], F32R)
        EARLY = 6
        raw_d = sb2("raw_d", [P, EARLY, HID])
        grow = sb2("grow", [P, B, HID])
        d_loaded = both.enter_context(nc.semaphore("d_loaded"))
        gb_loaded = both.enter_context(nc.semaphore("gb_loaded"))

        with ExitStack() as ctx:
            def sb(name, shape, dt=F32):
                return ctx.enter_context(nc.sbuf_tensor(name, shape, dt))

            def sem(name):
                return ctx.enter_context(nc.semaphore(name))

            xt = sb("xt", [P, 2, HID])
            raw = sb("raw_gu", [P, 2, KT, 2 * P])
            w_hi, w_lo = sb("wgu_hi", [P, 2, KT, 2 * P], F32R), sb("wgu_lo", [P, 2, KT, 2 * P], F32R)
            prod = sb("prod", [P, 2, HALF])
            norm = Norm(ctx, nc, "2", x1, hT_hi, hT_lo, modT[:, 2], modT[:, 3], ident)
            ps_g = [ctx.enter_context(nc.psum_tensor(f"ps_fg{i}", [P, HALF], F32)) for i in range(2)]
            ps_u = [ctx.enter_context(nc.psum_tensor(f"ps_fu{i}", [P, HALF], F32)) for i in range(2)]
            ga_loaded = sem("ga_loaded")
            xt_loaded = [sem(f"xt_loaded{i}") for i in range(2)]
            w_loaded = [sem(f"wgu_loaded{i}") for i in range(2)]
            scaled = sem("scaled")
            residual = sem("residual")
            whi_done = sem("whi_done")
            w_split = sem("w_split")
            gate_ready = sem("gate_ready")
            up_ready = sem("up_ready")
            silu_done = sem("silu_done")
            prod_done = sem("prod_done")
            ahi_done = sem("ahi_done")
            alo_done = sem("alo_done")
            block = ctx.enter_context(nc.Block())

            def inner_tiles(engine, step):
                step(0, 0, 0, True, True)
                with engine.Fori(0, (IT - 3) // 2) as i:
                    step(i, 2, 1, True, True)
                    step(i, 2, 2, True, True)
                step(0, 0, IT - 2, False, True)
                step(0, 0, IT - 1, False, False)

            @block.sync
            def _(sp):
                def load_w(i, per, k, parity):
                    sp.dma_start(raw[:, parity], wgu_in[bass.ds(i * per + k, 1)]
                                 .rearrange("o p k n -> (o p) k n")).then_inc(w_loaded[parity], 16)

                sp.dma_start(grow[:].rearrange("p b n -> p (b n)"), modrow[0].partition_broadcast(P))\
                    .then_inc(ga_loaded, 16)
                for t in range(NT):
                    if t >= 2:
                        sp.wait_ge(residual, t - 1)
                    sp.dma_start(xt[:, t % 2], x_in[t]).then_inc(xt_loaded[t % 2], 16)
                    if t == 1:
                        load_w(0, 0, 0, 0)
                        load_w(0, 0, 1, 1)
                sp.wait_ge(scaled, NT)
                sp.dma_start(grow[:].rearrange("p b n -> p (b n)"), modrow[1].partition_broadcast(P))\
                    .then_inc(gb_loaded, 16)
                sp.dma_start(raw_d[:], wd_in[0:EARLY].rearrange("k p n -> p k n")).then_inc(d_loaded, 16)

                def step(i, per, k, prefetch, next_split):
                    if prefetch:
                        sp.wait_ge(w_split, i * per + (k + 1))
                        load_w(i, per, k + 2, k % 2)

                inner_tiles(sp, step)

            @block.tensor
            def _(pe):
                for t in range(NT):
                    norm.tensor_turn(pe, t)

                def product(bank, s, half, u, done):
                    for k in range(KT):
                        cut = slice(half * HALF, (half + 1) * HALF)
                        cols = slice(u * P, (u + 1) * P)
                        last = three_products(nc.tensor, bank[:], w_hi[:, s, k, cols],
                                              w_lo[:, s, k, cols], hT_hi[:, k, cut],
                                              hT_lo[:, k, cut], k == 0, k == KT - 1)
                    last.then_inc(done, 1)

                def step(i, per, k, prefetch, next_split):
                    pe.wait_ge(w_split, i * per + (k + 1))
                    for half in range(2):
                        if k == 0:
                            pe.wait_ge(norm.lo_done, (half + 1) * NT // 2)
                        else:
                            pe.wait_ge(prod_done, i * (2 * per) + (2 * k - 1 + half))
                        product(ps_g[half], k % 2, half, 0, gate_ready)
                        product(ps_u[half], k % 2, half, 1, up_ready)

                inner_tiles(pe, step)

            @block.scalar
            def _(act):
                norm.scalar_rstd(act)
                for t in range(NT):
                    norm.scalar_modulate(act, t)

                def step(i, per, k, prefetch, next_split):
                    for half in range(2):
                        at = i * (2 * per) + (2 * k + half + 1)
                        if k > 0:
                            act.wait_ge(alo_done, i * (2 * per) + (2 * k - 1 + half))
                        act.wait_ge(gate_ready, at)
                        nc.scalar.activation(prod[:, half], ps_g[half][:], ACT.Silu)\
                            .then_inc(silu_done, 1)
                        act.wait_ge(prod_done, at)
                        nc.scalar.activation(
                            a_hi[:, bass.ds(i * per + k, 1), half * HALF:(half + 1) * HALF],
                            prod[:, half].unsqueeze(1), ACT.Copy).then_inc(ahi_done, 1)

                inner_tiles(act, step)

            @block.vector
            def _(dve):
                def split_w(i, per, k):
                    s = k % 2
                    count = 16 * (k // 2 + 1)
                    dve.wait_ge(w_loaded[s], i * (8 * per) + count)
                    split_hi(nc.vector, w_hi[:, s], raw[:, s]).then_inc(whi_done, 1)
                    dve.wait_ge(whi_done, i * per + (k + 1))
                    split_lo(nc.vector, w_lo[:, s], raw[:, s], w_hi[:, s]).then_inc(w_split, 1)

                dve.wait_ge(ga_loaded, 16)
                for t in range(NT):
                    nc.vector.tensor_tensor(x1[:, t], x1[:, t], grow[:, t // CPB], ALU.mult)\
                        .then_inc(scaled, 1)
                for t in range(NT):
                    dve.wait_ge(scaled, t + 1)
                    dve.wait_ge(xt_loaded[t % 2], 16 * (t // 2 + 1))
                    nc.vector.tensor_tensor(x1[:, t], x1[:, t], xt[:, t % 2], ALU.add)\
                        .then_inc(residual, 1)
                    dve.wait_ge(residual, t + 1)
                    norm.vector_stats(dve, t)
                norm.vector_var(dve)
                split_w(0, 0, 0)
                norm.vector_all(dve)

                def step(i, per, k, prefetch, next_split):
                    if next_split:
                        split_w(i, per, k + 1)
                    for half in range(2):
                        at = i * (2 * per) + (2 * k + half + 1)
                        dve.wait_ge(silu_done, at)
                        dve.wait_ge(up_ready, at)
                        nc.vector.tensor_tensor(prod[:, half], ps_u[half][:], prod[:, half], ALU.mult)\
                            .then_inc(prod_done, 1)
                        dve.wait_ge(ahi_done, at)
                        cut = slice(half * HALF, (half + 1) * HALF)
                        split_lo(nc.vector, a_lo[:, bass.ds(i * per + k, 1), cut],
                                 prod[:, half].unsqueeze(1),
                                 a_hi[:, bass.ds(i * per + k, 1), cut]).then_inc(alo_done, 1)

                inner_tiles(dve, step)

        with ExitStack() as ctx:
            def sb(name, shape, dt=F32):
                return ctx.enter_context(nc.sbuf_tensor(name, shape, dt))

            def sem(name):
                return ctx.enter_context(nc.semaphore(name))

            OLD = KT * B * L // HID
            old_hi, old_lo = (h[:].rearrange("p k (m n) -> p (k m) n", n=HID) for h in (hT_hi, hT_lo))
            new_hi, new_lo = (sb(n, [P, IT - OLD, HID], F32R) for n in ("d_hi", "d_lo"))
            raw_d2 = sb("raw_d2", [P, IT - EARLY, HID])
            res = sb("res", [P, 2, HID])
            ps_d = [ctx.enter_context(nc.psum_tensor(f"ps_d{i}", [P, HID], F32)) for i in range(2)]
            d2_loaded = sem("d2_loaded")
            dhi_done = sem("dhi_done")
            d_split = sem("d_split")
            down_ready = sem("down_ready")
            res_scaled = sem("res_scaled")
            res_done = sem("res_done")
            out_stored = [sem(f"out_stored{i}") for i in range(2)]
            block = ctx.enter_context(nc.Block())

            def d_hi(k):
                return old_hi[:, k] if k < OLD else new_hi[:, k - OLD]

            def d_lo(k):
                return old_lo[:, k] if k < OLD else new_lo[:, k - OLD]

            def raw_tile(k):
                return raw_d[:, k] if k < EARLY else raw_d2[:, k - EARLY]

            @block.scalar
            def _(act):
                act.wait_ge(d_loaded, 16)
                for k in range(IT):
                    if k == EARLY:
                        act.wait_ge(d2_loaded, 16)
                    nc.scalar.activation(d_hi(k), raw_tile(k), ACT.Copy).then_inc(dhi_done, 1)

            @block.vector
            def _(dve):
                for k in range(IT):
                    dve.wait_ge(dhi_done, k + 1)
                    split_lo(nc.vector, d_lo(k), raw_tile(k), d_hi(k)).then_inc(d_split, 1)
                dve.wait_ge(gb_loaded, 16)
                for t in range(NT):
                    dve.wait_ge(down_ready, t + 1)
                    if t >= 2:
                        dve.wait_ge(out_stored[t % 2], 16 * (t // 2))
                    nc.vector.tensor_tensor(res[:, t % 2], ps_d[t % 2][:], grow[:, t // CPB], ALU.mult)\
                        .then_inc(res_scaled, 1)
                    dve.wait_ge(res_scaled, t + 1)
                    nc.vector.tensor_tensor(res[:, t % 2], res[:, t % 2], x1[:, t], ALU.add)\
                        .then_inc(res_done, 1)

            @block.tensor
            def _(pe):
                for t in range(NT):
                    if t >= 2:
                        pe.wait_ge(res_scaled, t - 1)
                    cut = slice(t * P, (t + 1) * P)
                    for k in range(IT):
                        if t == 0:
                            pe.wait_ge(d_split, k + 1)
                        last = three_products(nc.tensor, ps_d[t % 2][:], a_hi[:, k, cut], a_lo[:, k, cut],
                                              d_hi(k), d_lo(k), k == 0, k == IT - 1)
                    last.then_inc(down_ready, 1)

            @block.sync
            def _(sp):
                sp.dma_start(raw_d2[:], wd_in[EARLY:IT].rearrange("k p n -> p k n"))\
                    .then_inc(d2_loaded, 16)
                for t in range(NT):
                    sp.wait_ge(res_done, t + 1)
                    sp.dma_start(out[t], res[:, t % 2]).then_inc(out_stored[t % 2], 16)
                for s in range(2):
                    sp.wait_ge(out_stored[s], 16 * (NT // 2))


def constants():
    import numpy as np

    cst = np.zeros((P, C_END), np.float32)
    cst[:, C_ID:C_ID + P] = np.eye(P)
    cst[:, C_TRI:C_TRI + P] = np.triu(np.ones((P, P)))
    inv = (np.float32(1.0) / np.float32(10000.0) ** (np.arange(0, D, 2, dtype=np.float32) / np.float32(D)))
    ang = np.arange(L, dtype=np.float32)[:, None] * inv.astype(np.float32)
    cos = np.concatenate([np.cos(ang)] * 2, axis=1).astype(np.float32)
    sin = np.concatenate([-np.sin(ang), np.sin(ang)], axis=1).astype(np.float32)
    cst[:, C_COST:C_COST + L] = cos.T
    cst[:, C_SINT:C_SINT + L] = sin.T
    cst[:, C_COS:C_COS + L] = cos.reshape(CPB, P, D).transpose(1, 0, 2).reshape(P, L)
    cst[:, C_SIN:C_SIN + L] = sin.reshape(CPB, P, D).transpose(1, 0, 2).reshape(P, L)
    return cst


def kernel(L0_attn_hidden_states, L0_attn_Wq, L0_attn_Wk, L0_attn_Wv, L0_attn_Wo, L0_attn_Wg,
           L0_attn_Win, L0_attn_dt_bias, L0_attn_A_log_bias, L0_attn_gnorm_w, L0_ffn_w_gate,
           L0_ffn_w_up, L0_ffn_w_down, L0_c, L0_wmod):
    import numpy as np
    import concourse.bacc as bacc
    from concourse.bass_utils import run_bass_kernel_spmd

    def f(a):
        return np.asarray(a)

    def heads(w):
        w = f(w)
        return w.reshape(w.shape[0] // D, D, KT, P).transpose(0, 3, 2, 1)

    pad = IT * P - INTER
    wg, wu = (np.pad(f(w), ((0, pad), (0, 0))) for w in (L0_ffn_w_gate, L0_ffn_w_up))
    wd = np.pad(f(L0_ffn_w_down), ((0, 0), (0, pad)))
    arrays = {
        "x_in": f(L0_attn_hidden_states).reshape(NT, P, HID),
        "cT_in": f(L0_c).reshape(B, KT, P).transpose(2, 1, 0).reshape(P, KT * B),
        "wmod_in": f(L0_wmod).reshape(KT, P, 6, HID).transpose(2, 1, 0, 3),
        "wq_in": heads(L0_attn_Wq),
        "wg_in": heads(L0_attn_Wg),
        "wkv_in": np.concatenate([heads(L0_attn_Wk), heads(L0_attn_Wv)], axis=3),
        "wo_in": f(L0_attn_Wo).reshape(HID, KVH, GRP, D).transpose(1, 3, 2, 0),
        "win_in": f(L0_attn_Win).reshape(H, KT, P).transpose(2, 1, 0),
        "rows_in": np.stack([f(L0_attn_dt_bias), f(L0_attn_A_log_bias)]),
        "gnorm_in": f(L0_attn_gnorm_w).reshape(P, 1),
        "wgu_in": np.concatenate([heads(wg), heads(wu)], axis=3),
        "wd_in": wd.T.reshape(IT, P, HID),
        "cst_in": constants(),
    }
    nc = bacc.Bacc("TRN2", target_bir_lowering=False, num_devices=1)
    arrays = {name: np.ascontiguousarray(a) for name, a in arrays.items()}
    args = {name: nc.dram_tensor(name, a.shape, F32, kind="ExternalInput").ap()
            for name, a in arrays.items()}
    out = nc.dram_tensor("out", (NT, P, HID), F32, kind="ExternalOutput").ap()
    build(nc, out=out, **args)
    r = run_bass_kernel_spmd(nc, [arrays], core_ids=[0])
    return r.results[0]["out"].reshape(B, L, HID)
```

```python
from contextlib import ExitStack

import concourse.bass as bass
from concourse import mybir

ALU = mybir.AluOpType
ACT = mybir.ActivationFunctionType
F32 = mybir.dt.float32
F32R = mybir.dt.float32r

P = 128
B, L, HID = 4, 256, 512
H, KVH, D = 32, 8, 128
CHUNK = 128
INTER = 1376
EPS = 1e-5
GRP = H // KVH
KT = HID // P
NT = B * L // P
CPB = L // CHUNK
IT = -(-INTER // P)
HALF = B * L // 2
assert CHUNK == P and D == P and CPB == 2 and HALF == 512 and GRP == 4 and NT == 8

C_ID, C_COST, C_SINT, C_COS, C_SIN, C_TRI, C_END = 0, 128, 384, 640, 896, 1152, 1280
EXP_CAP = 1e18
MASKED = -1e30
SERIES, INNER = (13, 11, 9, 7, 5, 3), 3
CHAIN_ABS = 3
CHAIN_SQUARE = CHAIN_ABS + 4
CHAIN_G = CHAIN_SQUARE + 1 + len(SERIES) + 4
CHAIN_DIFF = CHAIN_G + 1
CHAIN_END = CHAIN_DIFF + 1
GUARD_END = 8
SA, CA, GA, SB, CB, GB = range(6)


def split_hi(engine, hi, full):
    return engine.tensor_copy(hi, full)


def split_lo(engine, lo, full, hi):
    return engine.tensor_tensor(lo, full, hi.bitcast(F32), ALU.subtract)


def three_products(pe, out, w_hi, w_lo, x_hi, x_lo, first, last):
    pe.matmul(out, w_hi, x_hi, start=first, stop=False)
    pe.matmul(out, w_hi, x_lo, start=False, stop=False)
    return pe.matmul(out, w_lo, x_hi, start=False, stop=last)


def build(nc, x_in, cT_in, wmod_in, wq_in, wg_in, wkv_in, wo_in, win_in, rows_in, gnorm_in,
          wgu_in, wd_in, cst_in, out):
    modrow = nc.dram_tensor("modrow", (2, B * HID), F32, kind="Internal").ap()
    gT_dram = nc.dram_tensor("gT_dram", (H, B * L), F32, kind="Internal").ap()

    with ExitStack() as outer:
        def sb(name, shape, dt=F32):
            return outer.enter_context(nc.sbuf_tensor(name, shape, dt))

        cst = sb("cst", [P, C_TRI])
        x1 = sb("x1", [P, NT, HID])
        hT_hi = sb("hT_hi", [P, KT, B * L], F32R)
        hT_lo = sb("hT_lo", [P, KT, B * L], F32R)
        tok = sb("tok", [P, NT, 3, H])
        modT = sb("modT", [P, 4, KT, B])
        gnorm = sb("gnorm", [P, 1])
        ident = cst[:, C_ID:C_ID + P]

        block_attention(nc, cst, x1, hT_hi, hT_lo, tok, modT, gnorm, ident, modrow, gT_dram,
                        x_in, cT_in, wmod_in, wq_in, wg_in, wkv_in, wo_in, win_in, rows_in,
                        gnorm_in, cst_in)
        block_ffn(nc, x1, hT_hi, hT_lo, modT, ident, modrow, x_in, wgu_in, wd_in, out)


class Norm:

    def __init__(self, ctx, nc, tag, x1, hT_hi, hT_lo, shift, scale, ident, banks,
                 in_place, hf):
        def sb(name, shape, dt=F32):
            return ctx.enter_context(nc.sbuf_tensor(name + tag, shape, dt))

        def sem(name):
            return ctx.enter_context(nc.semaphore(name + tag))

        self.nc, self.x1, self.hT_hi, self.hT_lo = nc, x1, hT_hi, hT_lo
        self.shift, self.scale, self.ident = shift, scale, ident
        self.stats = sb("stats", [P, NT, 6])
        self.mv = sb("mv", [P, NT, 2])
        self.var = sb("var", [P, NT])
        self.rstd = sb("rstd", [P, NT])
        self.in_place = in_place
        self.xn = x1 if in_place else sb("xn", [P, 2, HID])
        self.hf = hf
        self.ps = banks
        self.stats_done = sem("stats_done")
        self.mv_done = sem("mv_done")
        self.var_done = sem("var_done")
        self.lnvar_done = sem("lnvar_done")
        self.rstd_done = sem("rstd_done")
        self.xn_done = sem("xn_done")
        self.turned = sem("turned")
        self.hf_done = sem("hf_done")
        self.hi_done = sem("hi_done")
        self.lo_done = sem("lo_done")

    def vector_stats(self, dve, t):
        nc = self.nc
        nc.vector.bn_stats(self.stats[:, t], self.x1[:, t]).then_inc(self.stats_done, 1)
        dve.wait_ge(self.stats_done, t + 1)
        nc.vector.bn_aggr(self.mv[:, t], self.stats[:, t]).then_inc(self.mv_done, 1)

    def half(self, i):
        return slice(i * NT // 2, (i + 1) * NT // 2)

    def vector_var(self, dve, i):
        dve.wait_ge(self.mv_done, (i + 1) * NT // 2)
        self.nc.vector.tensor_scalar(self.var[:, self.half(i)], self.mv[:, self.half(i), 1], EPS, None,
                                     ALU.add).then_inc(self.var_done, 1)

    def scalar_rstd(self, act, i):
        nc, var = self.nc, self.var[:, self.half(i)]
        act.wait_ge(self.var_done, i + 1)
        nc.scalar.activation(var, var, ACT.Ln).then_inc(self.lnvar_done, 1)
        act.wait_ge(self.lnvar_done, i + 1)
        nc.scalar.activation(self.rstd[:, self.half(i)], var, ACT.Exp, scale=-0.5)\
            .then_inc(self.rstd_done, 1)

    def xn_of(self, t):
        return self.xn[:, t if self.in_place else t % 2]

    def vector_normalise(self, dve, t):
        if t % (NT // 2) == 0:
            dve.wait_ge(self.rstd_done, t // (NT // 2) + 1)
        if t >= 2 and not self.in_place:
            dve.wait_ge(self.turned, t - 1)
        self.nc.vector.tensor_scalar(self.xn_of(t), self.x1[:, t], self.mv[:, t, 0:1],
                                     self.rstd[:, t:t + 1], ALU.subtract, ALU.mult)\
            .then_inc(self.xn_done, 1)

    def bank(self, t):
        return self.ps[t % len(self.ps)][:].rearrange("p (k i) -> p k i", k=KT)

    def tensor_turn(self, pe, t):
        pe.wait_ge(self.xn_done, t + 1)
        if t >= len(self.ps):
            pe.wait_ge(self.hf_done, t - len(self.ps) + 1)
        for k in range(KT):
            last = self.nc.tensor.transpose(self.bank(t)[:, k], self.xn_of(t)[:, k * P:(k + 1) * P],
                                            self.ident)
        last.then_inc(self.turned, 1)

    def scalar_modulate(self, act, t):
        b = t // CPB
        act.wait_ge(self.turned, t + 1)
        if t >= 2:
            act.wait_ge(self.lo_done, t - 1)
        for k in range(KT):
            last = self.nc.scalar.activation(self.hf[:, t % 2, k], self.bank(t)[:, k], ACT.Identity,
                                             bias=self.shift[:, k, b:b + 1],
                                             scale=self.scale[:, k, b:b + 1])
        last.then_inc(self.hf_done, 1)

    def vector_split(self, dve, t, with_lo=True):
        hi, lo = self.hT_hi[:, :, t * P:(t + 1) * P], self.hT_lo[:, :, t * P:(t + 1) * P]
        dve.wait_ge(self.hf_done, t + 1)
        split_hi(self.nc.vector, hi, self.hf[:, t % 2]).then_inc(self.hi_done, 1)
        if with_lo:
            dve.wait_ge(self.hi_done, t + 1)
            split_lo(self.nc.vector, lo, self.hf[:, t % 2], hi).then_inc(self.lo_done, 1)

    def pool_split_lo(self, pool, t):
        hi, lo = self.hT_hi[:, :, t * P:(t + 1) * P], self.hT_lo[:, :, t * P:(t + 1) * P]
        pool.wait_ge(self.hi_done, t + 1)
        split_lo(self.nc.gpsimd, lo, self.hf[:, t % 2], hi).then_inc(self.lo_done, 1)

    def vector_all(self, dve):
        for t in range(NT + 1):
            if t < NT:
                self.vector_normalise(dve, t)
            if t >= 1:
                self.vector_split(dve, t - 1)


def block_attention(nc, cst, x1, hT_hi, hT_lo, tok, modT, gnorm, ident, modrow, gT_dram,
                    x_in, cT_in, wmod_in, wq_in, wg_in, wkv_in, wo_in, win_in, rows_in,
                    gnorm_in, cst_in):
    with ExitStack() as ctx:
        def sb(name, shape, dt=F32):
            return ctx.enter_context(nc.sbuf_tensor(name, shape, dt))

        def ps(name):
            return ctx.enter_context(nc.psum_tensor(name, [P, HALF], F32))

        def sem(name):
            return ctx.enter_context(nc.semaphore(name))

        wq_hi, wq_lo = (sb(n, [P, GRP, KT, D], F32R) for n in ("wq_hi", "wq_lo"))
        wg_hi, wg_lo = (sb(n, [P, GRP, KT, D], F32R) for n in ("wg_hi", "wg_lo"))
        wkv_hi, wkv_lo = (sb(n, [P, KT, 2 * D], F32R) for n in ("wkv_hi", "wkv_lo"))
        wo_hi, wo_lo = (sb(n, [P, GRP, HID], F32R) for n in ("wo_hi", "wo_lo"))
        raw_q, raw_g = sb("raw_q", [P, KT, D]), sb("raw_g", [P, KT, D])
        raw_kv, raw_o = sb("raw_kv", [P, KT, 2 * D]), sb("raw_o", [P, GRP, HID])
        qT = sb("qT", [P, 2, GRP, HALF])
        sg = sb("sg", [P, 2, GRP, HALF])
        dec = sb("dec", [P, 2, GRP, CPB, CHUNK])
        kr = sb("kr", [P, 2, CPB, D])
        v = sb("v", [P, 2, CPB, D])
        kT = sb("kT", [P, 2, CPB * CHUNK])
        qe = sb("qe", [P, 2, GRP, CHUNK])
        scal = sb("scal", [P, NT, 3, GRP])
        vw = sb("vw", [P, GRP, D])
        state = sb("state", [P, GRP, D])
        prob = sb("prob", [P, GRP, CHUNK])
        sq, sq_hi, sq_lo = sb("sq", [P, HALF]), sb("sq_hi", [P, HALF], F32R), sb("sq_lo", [P, HALF], F32R)
        rms = sb("rms", [P, HALF])
        z = sb("z_att", [P, GRP, CHUNK])
        z_hi, z_lo = sb("z_hi", [P, GRP, CHUNK], F32R), sb("z_lo", [P, GRP, CHUNK], F32R)
        sig = sb("sig", [P, HALF])
        q_cos, q_sin = sb("q_cos", [P, HALF]), sb("q_sin", [P, HALF])
        k_cos, k_sin = sb("k_cos", [P, CPB, D]), sb("k_sin", [P, CPB, D])
        ones = sb("ones_r", [P, P], F32R)
        eps_col = sb("eps_col", [P, 1])
        future = sb("future", [P, CHUNK])
        ps_q, ps_g, ps_kv, ps_s, ps_y, ps_st, ps_ss, ps_o = (
            ps(n) for n in ("ps_q", "ps_gt", "ps_kv", "ps_s", "ps_y", "ps_st", "ps_ss", "ps_o"))

        silu_c = sb("silu_c", [P, KT * B])
        win, win_hi, win_lo = (w[:].rearrange("p (k h) -> p k h", k=KT) for w in (q_cos, sq_hi, sq_lo))
        rows = prob[:, 1, 0:2 * H].rearrange("p (r h) -> p r h", r=2)
        rate = prob[:, 1, 2 * H:3 * H]
        cT, sig_c = (prob[:, 2, i * KT * B:(i + 1) * KT * B] for i in range(2))
        z1, za, zs, zs2, zq, gdec = (
            raw_o[:, i // 2, i % 2 * NT * H:(i % 2 + 1) * NT * H].rearrange("p (t h) -> p t h", h=H)
            for i in range(6))
        zT = gT = [sq[0:H], rms[0:H]]
        tri = state[:, 0]
        hf = dec[:, 1].rearrange("p (s h) c i -> p s (h c) i", s=2)
        wmod = {SA: qT[:, 1], CA: sg[:, 1]}
        mod_rows = sg[0:B, 0, 0:2]
        ps_rows = {SA: ps_q[0:B], CA: ps_g[0:B]}
        ps_modT = ps_o[:, 0:2 * KT * B].rearrange("p (m k b) -> p m k b", m=2, k=KT)
        ps_z, ps_glast = (ps_o[:, i * NT * H:(i + 1) * NT * H].rearrange("p (t h) -> p t h", h=H)
                          for i in range(2))
        ps_zT = ps_gT = [ps_st, ps_ss]
        wmod[GA] = raw_o
        wmod[GB] = [raw_kv[:, 0:2].rearrange("p k d -> p (k d)"),
                    raw_kv[:, 2:4].rearrange("p k d -> p (k d)"),
                    raw_q[:].rearrange("p k d -> p (k d)"), raw_g[:].rearrange("p k d -> p (k d)")]
        wmod[SB], wmod[CB] = qT[:, 0], sg[:, 0]
        late_rows = dec[0:B, 0].rearrange("p h c i -> p (h c i)")\
            .rearrange("p (m n) -> p m n", m=2)
        gates, gmag = [q_cos[0:B], q_sin[0:B]], sig[0:B]
        ps_rows.update({GA: ps_q[0:B], GB: ps_g[0:B], SB: ps_kv[0:B], CB: ps_st[0:B]})
        ps_late_modT = ps_q[:, 0:2 * KT * B].rearrange("p (m k b) -> p m k b", m=2, k=KT)
        norm = Norm(ctx, nc, "1", x1, hT_hi, hT_lo, modT[:, 0], modT[:, 1], ident,
                    [ps_s, ps_y, ps_st, ps_ss], True, hf)

        cosT = cst[:, C_COST:C_COST + L].unsqueeze(1).broadcast_to([P, 2, L])
        sinT = cst[:, C_SINT:C_SINT + L].unsqueeze(1).broadcast_to([P, 2, L])
        cos_k = cst[:, C_COS:C_COS + L].rearrange("p (c d) -> p c d", c=CPB)
        sin_k = cst[:, C_SIN:C_SIN + L].rearrange("p (c d) -> p c d", c=CPB)

        wh_loaded = sem("wh_loaded")
        kv_loaded = sem("kv_loaded")
        wo_loaded = sem("wo_loaded")
        dec_loaded = sem("dec_loaded")
        wh_hi_done = sem("wh_hi_done")
        wh_split = sem("wh_split")
        kv_hi_done = sem("kv_hi_done")
        kv_split = sem("kv_split")
        wo_hi_done = sem("wo_hi_done")
        wo_split = sem("wo_split")
        q_ready = sem("q_ready")
        g_ready = sem("g_ready")
        kv_ready = sem("kv_ready")
        kt_ready = sem("kt_ready")
        s_ready = sem("s_ready")
        y_ready = sem("y_ready")
        st_ready = sem("st_ready")
        ss_ready = sem("ss_ready")
        o_ready = sem("o_ready")
        swap_done = sem("swap_done")
        qsin_done = sem("qsin_done")
        qcos_done = sem("qcos_done")
        rope_done = sem("rope_done")
        esig_done = sem("esig_done")
        cap_done = sem("cap_done")
        lsig_done = sem("lsig_done")
        sig_done = sem("sig_done")
        sg_done = sem("sg_done")
        kparts_done = sem("kparts_done")
        kr_done = sem("kr_done")
        v_done = sem("v_done")
        kT_done = sem("kT_done")
        scal_done = sem("scal_done")
        expg_done = sem("expg_done")
        mask_done = sem("mask_done")
        dec_done = sem("dec_done")
        vw_done = sem("vw_done")
        qe_done = sem("qe_done")
        state_done = sem("state_done")
        prob_done = sem("prob_done")
        sq_done = sem("sq_done")
        sqhi_done = sem("sqhi_done")
        sqlo_done = sem("sqlo_done")
        zz_done = sem("zz_done")
        lnss_done = sem("lnss_done")
        rms_done = sem("rms_done")
        z_done = sem("z_done")
        zhi_done = sem("zhi_done")
        zlo_done = sem("zlo_done")
        zeros_done = sem("zeros_done")
        future_done = sem("future_done")
        ones_done = sem("ones_done_r")
        sums_done = sem("sums_done")
        c_loaded = sem("c_loaded")
        x_loaded = [sem(f"x_loaded{i}") for i in range(2)]
        mod_loaded = [sem(f"mod_loaded{i}") for i in range(6)]
        cst_loaded = sem("cst_loaded")
        small_loaded = sem("small_loaded")
        sigc_done = sem("sigc_done")
        siluc_done = sem("siluc_done")
        rows_ready = sem("rows_ready")
        rows_copied = sem("rows_copied")
        mod_turned = sem("mod_turned")
        modT_done = sem("modT_done")
        win_split = sem("win_split")
        rate_done = sem("rate_done")
        zT_ready = sem("zT_ready")
        zT_copied = sem("zT_copied")
        z_ready = sem("z_ready")
        chain = sem("chain")
        exp_done = sem("exp_done")
        cum_ready = sem("cum_ready")
        gT_ready = sem("gT_ready")
        gT_copied = sem("gT_copied")
        gT_stored = sem("gT_stored")
        gates_ready = sem("gates_ready")
        guard = sem("guard")
        rows_stored = sem("rows_stored")
        block = ctx.enter_context(nc.Block())

        def rows_of(t):
            return slice(t % 4 * P, t % 4 * P + P)

        def group_slice(g, b, size):
            g = g + 1 if b == B - 1 else g
            return bass.ds(g * size, size)

        def groups(engine, step):
            with engine.Fori(0, KVH - 1) as g:
                for t in range(NT):
                    step(g, t, True, True, True)
            for t in range(NT):
                step(KVH - 1, t, t < 4, t < NT - 2, False)

        @block.sync
        def _(sp):
            def load_mod(m):
                if m == GB:
                    for k in range(KT):
                        sp.dma_start(wmod[m][k], wmod_in[m][:, k]).then_inc(mod_loaded[m], 16)
                else:
                    sp.dma_start(wmod[m][:], wmod_in[m]).then_inc(mod_loaded[m], 16)

            def load_head(g, j, first=False):
                if not first:
                    sp.wait_ge(wh_split, g * 4 + j)
                sp.dma_start(raw_q[:], wq_in[bass.ds(g * 4 + j, 1)].rearrange("o p k d -> (o p) k d"))\
                    .then_inc(wh_loaded, 16)
                sp.dma_start(raw_g[:], wg_in[bass.ds(g * 4 + j, 1)].rearrange("o p k d -> (o p) k d"))\
                    .then_inc(wh_loaded, 16)

            def load_kv(g):
                sp.dma_start(raw_kv[:], wkv_in[bass.ds(g, 1)].rearrange("o p k d -> (o p) k d"))\
                    .then_inc(kv_loaded, 16)

            def load_o(g):
                sp.dma_start(raw_o[:], wo_in[bass.ds(g, 1)].rearrange("o p h n -> (o p) h n"))\
                    .then_inc(wo_loaded, 16)

            def load_dec(g, b):
                bn = (b + 1) % B
                src = gT_dram[group_slice(g, b, GRP), bn * L:(bn + 1) * L]
                sp.dma_start(dec[:, bn % 2].rearrange("p h c i -> p h (c i)"),
                             src.partition_broadcast(P)).then_inc(dec_loaded, 16)

            sp.dma_start(cT, cT_in).then_inc(c_loaded, 16)
            for half, m in enumerate((SA, CA)):
                load_mod(m)
                a = half * NT // 2
                sp.dma_start(x1[:, a:a + NT // 2], x_in[a:a + NT // 2].rearrange("t p n -> p t n"))\
                    .then_inc(x_loaded[half], 16)
            load_kv(0)
            load_head(0, 0, True)
            for j in range(1, GRP):
                load_head(0, j)
            sp.wait_ge(gT_copied, 2)
            for i in range(2):
                sp.dma_start(gT_dram[:, i * HALF:(i + 1) * HALF], gT[i]).then_inc(gT_stored, 16)
            sp.wait_ge(gT_stored, 32)
            load_dec(0, -1)
            sp.wait_ge(chain, CHAIN_END)
            load_o(0)

            def step(g, t, project, next_batch, next_group):
                if t % 2 == 0 and next_batch:
                    sp.wait_ge(prob_done, g * 8 + (t + 1))
                    load_dec(g, t // 2)
                if next_group and t < GRP:
                    load_head(g + 1, t)
                if next_group and t == 1:
                    sp.wait_ge(wo_split, g + 2)
                    load_o(g + 1)
                if next_group and t == 2:
                    sp.wait_ge(kv_split, g + 1)
                    load_kv(g + 1)

                if not next_group and t == 1:
                    sp.wait_ge(wo_split, KVH + 1)
                    load_mod(GA)
                    load_mod(GB)
                if not next_group and t == 4:
                    sp.wait_ge(zz_done, g * 8 + 4)
                    load_mod(SB)
                    load_mod(CB)

            groups(sp, step)
            sp.wait_ge(guard, GUARD_END)
            for i in range(2):
                sp.dma_start(modrow[i].rearrange("(b n) -> b n", b=B), gates[i])\
                    .then_inc(rows_stored, 16)
            sp.wait_ge(rows_stored, 32)

        @block.tensor
        def _(pe):
            def q_block(g, t, first=False):
                half, j = (t // 4 + 1) % 2, t % 4
                gw = g + 1 if t >= 4 else g
                pe.wait_ge(wh_split, gw * 4 + (j + 1))
                if not first:
                    pe.wait_ge(qcos_done, g * 8 + (t + 4))
                for k in range(KT):
                    cut = slice(half * HALF, (half + 1) * HALF)
                    last = three_products(nc.tensor, ps_q[:], wq_hi[:, j, k], wq_lo[:, j, k],
                                          hT_hi[:, k, cut], hT_lo[:, k, cut], k == 0, k == KT - 1)
                last.then_inc(q_ready, 1)

            def g_block(g, t, k_from, k_to, first=False):
                half, j = (t // 4 + 1) % 2, t % 4
                if k_from == 0 and not first:
                    pe.wait_ge(sg_done, g * 8 + (t + 4))
                for k in range(k_from, k_to):
                    cut = slice(half * HALF, (half + 1) * HALF)
                    last = three_products(nc.tensor, ps_g[:], wg_hi[:, j, k], wg_lo[:, j, k],
                                          hT_hi[:, k, cut], hT_lo[:, k, cut], k == 0, k == KT - 1)
                if k_to == KT:
                    last.then_inc(g_ready, 1)

            def kv_batch(g, b):
                bn = (b + 1) % B
                gw = g + 1 if b == B - 1 else g
                pe.wait_ge(kv_split, gw + 1)
                if b >= 0:
                    pe.wait_ge(kT_done, g * 4 + (b + 1))
                for c in range(CPB):
                    cut = slice((bn * CPB + c) * P, (bn * CPB + c + 1) * P)
                    for k in range(KT):
                        last = three_products(nc.tensor, ps_kv[:, c * 2 * D:(c + 1) * 2 * D],
                                              hT_hi[:, k, cut], hT_lo[:, k, cut],
                                              wkv_hi[:, k], wkv_lo[:, k], k == 0, k == KT - 1)
                last.then_inc(kv_ready, 1)

            def k_turn(g, b):
                pe.wait_ge(kr_done, g * 4 + (b + 2))
                pe.wait_ge(v_done, g * 4 + (b + 2))
                for c in range(CPB):
                    last = nc.tensor.transpose(ps_kv[:, c * P:(c + 1) * P], kr[:, (b + 1) % 2, c], ident)
                last.then_inc(kt_ready, 1)

            def out_product(g, t):
                pe.wait_ge(zhi_done, g * 8 + (t + 1))
                pe.wait_ge(zlo_done, g * 8 + (t + 1))
                if t <= 1:
                    pe.wait_ge(wo_split, g + (t + 1))
                for h in range(GRP):
                    last = three_products(nc.tensor, ps_o[:], z_hi[:, h], z_lo[:, h],
                                          wo_hi[:, h], wo_lo[:, h], h == 0, h == GRP - 1)
                last.then_inc(o_ready, 1)

            def weights(m, k):
                return wmod[m][k] if m == GB else wmod[m][:, k]

            def mod_row(m):
                pe.wait_ge(mod_loaded[m], 16 * KT if m == GB else 16)
                for k in range(KT):
                    last = nc.tensor.matmul(ps_rows[m], silu_c[:, k * B:(k + 1) * B], weights(m, k),
                                            start=k == 0, stop=k == KT - 1)
                last.then_inc(rows_ready, 1)

            def mod_turn(dest, source, count):
                pe.wait_ge(rows_copied, count)
                for i in range(2):
                    for k in range(KT):
                        last = nc.tensor.transpose(dest[:, i, k], source[:, i, k * P:(k + 1) * P],
                                                   ident[0:B, 0:B])
                last.then_inc(mod_turned, 1)

            def softplus_argument():
                for i in range(2):
                    for k in range(KT):
                        cut = slice(i * HALF, (i + 1) * HALF)
                        last = three_products(nc.tensor, ps_zT[i][:], win_hi[:, k], win_lo[:, k],
                                              hT_hi[:, k, cut], hT_lo[:, k, cut], k == 0, k == KT - 1)
                    last.then_inc(zT_ready, 1)

            def softplus_turn():
                for t in range(NT):
                    if t % 4 == 0:
                        pe.wait_ge(zT_copied, t // 4 + 1)
                    last = nc.tensor.transpose(ps_z[:, t], zT[t // 4][:, t % 4 * P:(t % 4 + 1) * P],
                                               ident[0:H, 0:H])
                last.then_inc(z_ready, 1)

            def cumulative():
                pe.wait_ge(chain, CHAIN_G)
                pe.wait_ge(small_loaded, 64)
                nc.tensor.matmul(ps_z, tri, gdec, start=True, stop=True)
                nc.tensor.matmul(ps_glast, ones[:].bitcast(F32), gdec, start=True, stop=True)\
                    .then_inc(cum_ready, 1)
                for t in range(NT):
                    i, col = t // 4, t % 4 * P
                    last = nc.tensor.matmul(ps_gT[i][0:H, col:col + P], gdec[:, t], tri,
                                            start=True, stop=True)
                    if t % 4 == 3:
                        last.then_inc(gT_ready, 1)

            pe.wait_ge(siluc_done, 3)
            mod_row(SA)
            mod_row(CA)
            pe.wait_ge(cst_loaded, 16)
            norm.tensor_turn(pe, 0)
            mod_turn(ps_modT, mod_rows, 2)
            for t in range(1, 6):
                norm.tensor_turn(pe, t)
            pe.wait_ge(norm.lo_done, CPB)
            kv_batch(0, -1)
            norm.tensor_turn(pe, 6)
            norm.tensor_turn(pe, 7)
            pe.wait_ge(norm.lo_done, NT // 2)
            q_block(0, -4, True)
            g_block(0, -4, 0, KT, True)
            k_turn(0, -1)
            pe.wait_ge(win_split, 2)
            pe.wait_ge(norm.lo_done, NT)
            softplus_argument()
            q_block(0, -3)
            softplus_turn()
            g_block(0, -3, 0, KT)
            q_block(0, -2)
            g_block(0, -2, 0, KT)
            pe.wait_ge(ones_done, 1)
            cumulative()
            q_block(0, -1)
            g_block(0, -1, 0, KT)

            def step(g, t, project, next_batch, next_group):
                b, c, half = t // 2, t % 2, t // 4
                pe.wait_ge(kT_done, g * 4 + (b + 1))
                pe.wait_ge(rope_done, g * 8 + (4 * half + 4))
                nc.tensor.matmul(ps_s[:].rearrange("p (h i) -> p h i", h=GRP),
                                 kT[:, b % 2, c * P:(c + 1) * P], qT[:, half, :, rows_of(t)],
                                 start=True, stop=True).then_inc(s_ready, 1)
                if project:
                    q_block(g, t)
                out_product(g, t)
                if c == 1 and next_batch:
                    k_turn(g, b)
                if c == 1:
                    pe.wait_ge(qe_done, g * 4 + (b + 1))
                    pe.wait_ge(state_done, g * 4 + (b + 1))
                    for h in range(GRP):
                        nc.tensor.matmul(ps_y[:, h * P:(h + 1) * P], state[:, h], qe[:, b % 2, h],
                                         start=h == 0, stop=False)
                pe.wait_ge(prob_done, g * 8 + (t + 1))
                nc.tensor.matmul(ps_y[:].rearrange("p (h i) -> p h i", h=GRP), v[:, b % 2, c], prob[:],
                                 start=c == 0, stop=True).then_inc(y_ready, 1)
                if c == 0:
                    pe.wait_ge(vw_done, g * 4 + (b + 1))
                    nc.tensor.matmul(ps_st[:].rearrange("p (h e) -> p h e", h=GRP), kr[:, b % 2, 0],
                                     vw[:], start=True, stop=True).then_inc(st_ready, 1)
                if project:
                    g_block(g, t, 0, KT - 1)
                if not next_group and t == 5:
                    mod_row(GA)
                    mod_row(GB)
                if not next_group and t == 6:
                    mod_row(SB)
                    pe.wait_ge(state_done, KVH * B)
                    mod_row(CB)
                pe.wait_ge(sqhi_done, g * 8 + (t + 1))
                nc.tensor.matmul(ps_ss[:], ones[:], sq_hi[:], start=True, stop=False)
                pe.wait_ge(sqlo_done, g * 8 + (t + 1))
                nc.tensor.matmul(ps_ss[:], ones[:], sq_lo[:], start=False, stop=True)\
                    .then_inc(ss_ready, 1)
                if project:
                    g_block(g, t, KT - 1, KT)
                if c == 0 and next_batch:
                    kv_batch(g, b)

            groups(pe, step)
            out_product(KVH - 1, NT)
            pe.wait_ge(guard, 2)
            mod_turn(ps_late_modT, late_rows, 4)

        @block.scalar
        def _(act):
            def swap(g, t, first=False):
                act.wait_ge(q_ready, g * 8 + (t + 5))
                if not first:
                    act.wait_ge(rope_done, g * 8 + (t + 4))
                nc.scalar.activation(q_sin[0:64], ps_q[64:128, :], ACT.Copy)
                nc.scalar.activation(q_sin[64:128], ps_q[0:64, :], ACT.Copy).then_inc(swap_done, 1)

            def exp_gate(g, t):
                act.wait_ge(g_ready, g * 8 + (t + 5))
                nc.scalar.activation(sig[:], ps_g[:], ACT.Exp, scale=-1.0).then_inc(esig_done, 1)

            def sigmoid(g, t):
                act.wait_ge(cap_done, g * 8 + (t + 5))
                nc.scalar.activation(sig[:], sig[:], ACT.Ln, bias=1.0).then_inc(lsig_done, 1)
                act.wait_ge(lsig_done, g * 8 + (t + 5))
                nc.scalar.activation(sig[:], sig[:], ACT.Exp, scale=-1.0).then_inc(sig_done, 1)

            def exp_g(g, b):
                par = (b + 1) % 2
                act.wait_ge(dec_loaded, g * 64 + 16 * (b + 2))
                nc.scalar.activation(qe[:, par], dec[:, par, :, 1], ACT.Exp).then_inc(expg_done, 1)

            def decays(g, b):
                bn = (b + 1) % B
                act.wait_ge(mask_done, g * 4 + (b + 2))
                act.wait_ge(scal_done, g * 4 + (b + 2))
                for h in range(GRP):
                    for c in range(CPB):
                        cell = dec[:, bn % 2, h, c]
                        last = nc.scalar.activation(cell, cell, ACT.Exp,
                                                    bias=scal[:, bn * CPB + c, 0, h:h + 1])
                last.then_inc(dec_done, 1)

            def copy_v(g, b):
                act.wait_ge(kv_ready, g * 4 + (b + 2))
                nc.scalar.activation(v[:, (b + 1) % 2],
                                     ps_kv[:].rearrange("p (c d) -> p c d", c=CPB)[:, :, D:2 * D],
                                     ACT.Copy).then_inc(v_done, 1)

            def copy_kT(g, b):
                act.wait_ge(kt_ready, g * 4 + (b + 2))
                nc.scalar.activation(kT[:, (b + 1) % 2], ps_kv[:, 0:CPB * P], ACT.Copy)\
                    .then_inc(kT_done, 1)

            act.dma_start(cst[:], cst_in[:, 0:C_TRI]).then_inc(cst_loaded, 16)
            act.dma_start(tri, cst_in[:, C_TRI:C_END]).then_inc(small_loaded, 16)
            act.dma_start(win, win_in).then_inc(small_loaded, 16)
            act.dma_start(rows, rows_in.partition_broadcast(P)).then_inc(small_loaded, 16)
            act.dma_start(gnorm[:], gnorm_in).then_inc(small_loaded, 16)
            nc.scalar.preload_act_table_set("natural_log_exp_and_others")
            act.wait_ge(c_loaded, 16)
            nc.scalar.activation(sig_c, cT, ACT.Exp, scale=-1.0).then_inc(sigc_done, 1)
            norm.scalar_rstd(act, 0)
            for i, m in enumerate((SA, CA)):
                act.wait_ge(rows_ready, i + 1)
                nc.scalar.activation(mod_rows[:, i], ps_rows[m], ACT.Copy).then_inc(rows_copied, 1)
            act.wait_ge(small_loaded, 64)
            nc.scalar.activation(rate, rows[:, 1], ACT.Exp).then_inc(rate_done, 1)
            norm.scalar_rstd(act, 1)
            act.wait_ge(modT_done, 2)
            for t in range(NT):
                norm.scalar_modulate(act, t)
            for t in range(-4, 0):
                if t == -4:
                    copy_v(0, -1)
                swap(0, t, t == -4)
                exp_gate(0, t)
                if t == -2:
                    act.wait_ge(cum_ready, 1)
                    nc.scalar.activation(tok[:, :, 0], ps_z, ACT.Copy, scale=-1.0).then_inc(exp_done, 1)
                    for i in range(2):
                        act.wait_ge(gT_ready, i + 1)
                        nc.scalar.activation(gT[i], ps_gT[i][0:H], ACT.Copy).then_inc(gT_copied, 1)
                sigmoid(0, t)
                if t == -4:
                    copy_kT(0, -1)
                    for i in range(2):
                        act.wait_ge(zT_ready, i + 1)
                        nc.scalar.activation(zT[i], ps_zT[i][0:H], ACT.Copy).then_inc(zT_copied, 1)
                    act.wait_ge(chain, CHAIN_ABS)
                    nc.scalar.activation(za, za, ACT.Exp, scale=-1.0).then_inc(exp_done, 1)
                if t == -2:
                    act.wait_ge(chain, CHAIN_DIFF)
                    nc.scalar.activation(zs, zs, ACT.Exp).then_inc(exp_done, 1)
            exp_g(0, -1)
            decays(0, -1)
            act.wait_ge(ones_done, 1)

            def step(g, t, project, next_batch, next_group):
                b, c = t // 2, t % 2
                if project:
                    swap(g, t)
                if c == 1 and next_batch:
                    decays(g, b)
                act.wait_ge(y_ready, g * 8 + (t + 1))
                nc.scalar.activation(sq[:], ps_y[:], ACT.Square).then_inc(sq_done, 1)
                nc.scalar.activation(sq_hi[:], ps_y[:], ACT.Square).then_inc(sqhi_done, 1)
                if c == 0:
                    act.wait_ge(st_ready, g * 4 + (b + 1))
                    nc.scalar.activation(state[:].rearrange("p h e -> p (h e)"), ps_st[:], ACT.Copy)\
                        .then_inc(state_done, 1)
                if c == 0 and next_batch:
                    exp_g(g, b)
                if c == 1 and next_batch:
                    copy_kT(g, b)
                act.wait_ge(ss_ready, g * 8 + (t + 1))
                nc.scalar.activation(rms[:], ps_ss[:], ACT.Ln, bias=eps_col[:], scale=1.0 / D)\
                    .then_inc(lnss_done, 1)
                act.wait_ge(lnss_done, g * 8 + (t + 1))
                nc.scalar.activation(rms[:], rms[:], ACT.Exp, scale=-0.5).then_inc(rms_done, 1)
                if project:
                    exp_gate(g, t)
                act.wait_ge(z_done, g * 8 + (t + 1))
                nc.scalar.activation(z_hi[:], z[:], ACT.Copy).then_inc(zhi_done, 1)
                if project:
                    sigmoid(g, t)
                if c == 0 and next_batch:
                    copy_v(g, b)
                if not next_group and t == 6:
                    for i, m in enumerate((SB, CB)):
                        act.wait_ge(rows_ready, 5 + i)
                        nc.scalar.activation(late_rows[:, i], ps_rows[m], ACT.Copy)\
                            .then_inc(rows_copied, 1)

            groups(act, step)

        @block.vector
        def _(dve):
            def split_head(g, j):
                dve.wait_ge(wh_loaded, g * 128 + 32 * (j + 1))
                split_hi(nc.vector, wq_hi[:, j], raw_q[:])
                split_hi(nc.vector, wg_hi[:, j], raw_g[:]).then_inc(wh_hi_done, 1)
                dve.wait_ge(wh_hi_done, g * 4 + (j + 1))
                split_lo(nc.vector, wq_lo[:, j], raw_q[:], wq_hi[:, j])
                split_lo(nc.vector, wg_lo[:, j], raw_g[:], wg_hi[:, j]).then_inc(wh_split, 1)

            def split_kv(g):
                dve.wait_ge(kv_loaded, g * 16 + 16)
                split_hi(nc.vector, wkv_hi[:], raw_kv[:]).then_inc(kv_hi_done, 1)
                dve.wait_ge(kv_hi_done, g + 1)
                split_lo(nc.vector, wkv_lo[:], raw_kv[:], wkv_hi[:]).then_inc(kv_split, 1)

            def split_o_hi(g):
                dve.wait_ge(wo_loaded, g * 16 + 16)
                split_hi(nc.vector, wo_hi[:], raw_o[:]).then_inc(wo_hi_done, 1)

            def split_o_lo(g):
                dve.wait_ge(wo_hi_done, g + 1)
                split_lo(nc.vector, wo_lo[:], raw_o[:], wo_hi[:]).then_inc(wo_split, 1)

            def copy_scalars(g, b, first=False):
                t0 = (b + 1) % B * CPB
                if first:
                    dve.wait_ge(chain, CHAIN_END)
                nc.vector.tensor_copy(scal[:, t0:t0 + CPB],
                                      tok[:, t0:t0 + CPB, :, group_slice(g, b, GRP)])\
                    .then_inc(scal_done, 1)

            def rotate_k(g, b):
                ps_k = ps_kv[:].rearrange("p (c d) -> p c d", c=CPB)
                dve.wait_ge(v_done, g * 4 + (b + 2))
                nc.vector.tensor_tensor(k_cos[:], ps_k[:, :, 0:D], cos_k, ALU.mult)
                nc.vector.tensor_tensor(k_sin[:, :, 0:64], ps_k[:, :, 64:128], sin_k[:, :, 0:64],
                                        ALU.mult)
                nc.vector.tensor_tensor(k_sin[:, :, 64:128], ps_k[:, :, 0:64], sin_k[:, :, 64:128],
                                        ALU.mult).then_inc(kparts_done, 1)
                dve.wait_ge(kparts_done, g * 4 + (b + 2))
                nc.vector.tensor_tensor(kr[:, (b + 1) % 2], k_cos[:], k_sin[:], ALU.add)\
                    .then_inc(kr_done, 1)

            def rotate_q_cos(g, t):
                dve.wait_ge(swap_done, g * 8 + (t + 5))
                nc.vector.tensor_tensor(q_cos[:].rearrange("p (b i) -> p b i", b=2),
                                        ps_q[:].rearrange("p (b i) -> p b i", b=2), cosT, ALU.mult)\
                    .then_inc(qcos_done, 1)

            def rotate_q_add(g, t):
                half, j = (t // 4 + 1) % 2, t % 4
                dve.wait_ge(qcos_done, g * 8 + (t + 5))
                dve.wait_ge(qsin_done, g * 8 + (t + 5))
                nc.vector.tensor_tensor(qT[:, half, j], q_cos[:], q_sin[:], ALU.add)\
                    .then_inc(rope_done, 1)

            def cap(g, t):
                dve.wait_ge(esig_done, g * 8 + (t + 5))
                nc.vector.tensor_scalar(sig[:], sig[:], EXP_CAP, None, ALU.min).then_inc(cap_done, 1)

            def gate(g, t):
                half, j = (t // 4 + 1) % 2, t % 4
                dve.wait_ge(sig_done, g * 8 + (t + 5))
                nc.vector.scalar_tensor_tensor(sg[:, half, j], ps_g[:], gnorm[:], sig[:],
                                               ALU.mult, ALU.mult).then_inc(sg_done, 1)

            def add_out(g, t):
                dve.wait_ge(o_ready, g * 8 + (t + 1))
                nc.vector.tensor_tensor(x1[:, (t - 1) % NT], x1[:, (t - 1) % NT], ps_o[:], ALU.add)\
                    .then_inc(sums_done, 1)

            def softplus_before_exp():
                dve.wait_ge(z_ready, 1)
                nc.vector.tensor_tensor(z1, ps_z, rows[:, 0].unsqueeze(1).broadcast_to([P, NT, H]),
                                        ALU.add).then_inc(chain, 1)
                dve.wait_ge(chain, 1)
                nc.vector.tensor_scalar(za, z1, -1.0, None, ALU.mult).then_inc(chain, 1)
                dve.wait_ge(chain, 2)
                nc.vector.tensor_tensor(za, za, z1, ALU.max).then_inc(chain, 1)

            def softplus_argument_of_series():
                dve.wait_ge(exp_done, 1)
                nc.vector.tensor_scalar(zs2, za, 2.0, None, ALU.add).then_inc(chain, 1)
                dve.wait_ge(chain, CHAIN_ABS + 1)
                nc.vector.reciprocal(zs, zs2).then_inc(chain, 1)
                dve.wait_ge(chain, CHAIN_ABS + 2)
                nc.vector.tensor_tensor(zs, zs, za, ALU.mult).then_inc(chain, 1)
                dve.wait_ge(chain, CHAIN_ABS + 3)
                nc.vector.tensor_tensor(zs2, zs, zs, ALU.mult).then_inc(chain, 1)

            def softplus_series(part):
                if part == 0:
                    dve.wait_ge(chain, CHAIN_SQUARE)
                    nc.vector.tensor_scalar(zq, zs2, 1.0 / 15, None, ALU.mult).then_inc(chain, 1)
                    dve.wait_ge(chain, CHAIN_SQUARE + 1)
                for n in range(INNER) if part == 0 else range(INNER, len(SERIES)):
                    odd = SERIES[n]
                    nc.vector.scalar_tensor_tensor(zq, zq, 1.0 / odd, zs2, ALU.add, ALU.mult)\
                        .then_inc(chain, 1)
                    dve.wait_ge(chain, CHAIN_SQUARE + 2 + n)

            def decay_rates():
                nc.vector.scalar_tensor_tensor(zq, zq, 1.0, zs, ALU.add, ALU.mult).then_inc(chain, 1)
                nc.vector.tensor_scalar(z1, z1, 0.0, None, ALU.max).then_inc(chain, 1)
                dve.wait_ge(chain, CHAIN_G - 2)
                nc.vector.scalar_tensor_tensor(tok[:, :, 1], zq, 2.0, z1, ALU.mult, ALU.add)\
                    .then_inc(chain, 1)
                dve.wait_ge(chain, CHAIN_G - 1)
                dve.wait_ge(rate_done, 1)
                nc.vector.scalar_tensor_tensor(gdec, tok[:, :, 1], -1.0,
                                               rate.unsqueeze(1).broadcast_to([P, NT, H]),
                                               ALU.mult, ALU.mult).then_inc(chain, 1)

            def chunk_end():
                dve.wait_ge(cum_ready, 1)
                dve.wait_ge(exp_done, 2)
                nc.vector.tensor_tensor(zs, ps_glast, tok[:, :, 0], ALU.add).then_inc(chain, 1)

            def state_weight():
                dve.wait_ge(exp_done, 3)
                nc.vector.tensor_tensor(tok[:, :, 2], zs, tok[:, :, 1], ALU.mult).then_inc(chain, 1)

            def guard_gates():
                dve.wait_ge(rows_ready, 4)
                ga_gb = (ps_rows[GA], ps_rows[GB])
                for i, row in enumerate(ga_gb):
                    nc.vector.tensor_scalar(gmag, row, -1.0, None, ALU.mult).then_inc(guard, 1)
                    dve.wait_ge(guard, 4 * i + 1)
                    nc.vector.tensor_tensor(gmag, gmag, row, ALU.max)
                    nc.vector.tensor_scalar(gates[i], row, 0.0, 2.0, ALU.is_ge, ALU.mult)\
                        .then_inc(guard, 1)
                    dve.wait_ge(guard, 4 * i + 2)
                    nc.vector.tensor_scalar(gates[i], gates[i], -1.0, None, ALU.add).then_inc(guard, 1)
                    dve.wait_ge(guard, 4 * i + 3)
                    nc.vector.scalar_tensor_tensor(gates[i], gmag, 0.25, gates[i], ALU.max, ALU.mult)\
                        .then_inc(guard, 1)
                    dve.wait_ge(guard, 4 * i + 4)

            dve.wait_ge(sigc_done, 1)
            nc.vector.tensor_scalar(sig_c, sig_c, 1.0, None, ALU.add).then_inc(siluc_done, 1)
            dve.wait_ge(siluc_done, 1)
            nc.vector.reciprocal(silu_c[:], sig_c).then_inc(siluc_done, 1)
            dve.wait_ge(siluc_done, 2)
            nc.vector.tensor_tensor(silu_c[:], silu_c[:], cT, ALU.mult).then_inc(siluc_done, 1)
            for half in range(2):
                dve.wait_ge(x_loaded[half], 16)
                for t in range(half * NT // 2, (half + 1) * NT // 2):
                    norm.vector_stats(dve, t)
                norm.vector_var(dve, half)
                if half == 1:
                    dve.wait_ge(mod_turned, 1)
                    nc.vector.tensor_copy(modT[:, 0], ps_modT[:, 0]).then_inc(modT_done, 1)
                    nc.vector.tensor_scalar(modT[:, 1], ps_modT[:, 1], 1.0, None, ALU.add)\
                        .then_inc(modT_done, 1)
                for t in range(half * NT // 2, (half + 1) * NT // 2):
                    norm.vector_normalise(dve, t)
            norm.vector_split(dve, 0, False)
            split_kv(0)
            norm.vector_split(dve, 1, False)
            split_head(0, 0)
            for t in range(2, NT):
                norm.vector_split(dve, t, False)
                if t == 4:
                    dve.wait_ge(small_loaded, 64)
                    split_hi(nc.vector, win_hi, win).then_inc(win_split, 1)
                    dve.wait_ge(win_split, 1)
                    split_lo(nc.vector, win_lo, win, win_hi).then_inc(win_split, 1)
            rotate_k(0, -1)
            for t in range(-4, 0):
                rotate_q_cos(0, t)
                if t == -4:
                    rotate_q_add(0, t)
                    split_head(0, 1)
                if t == -3:
                    softplus_argument_of_series()
                    rotate_q_add(0, t)
                if t >= -2:
                    rotate_q_add(0, t)
                cap(0, t)
                if t == -3:
                    softplus_series(0)
                gate(0, t)
                if t == -4:
                    split_head(0, 2)
                    softplus_before_exp()
                if t == -3:
                    softplus_series(1)
                    decay_rates()
                    split_head(0, 3)
                if t == -2:
                    chunk_end()
            state_weight()
            copy_scalars(0, -1, True)
            dve.wait_ge(zeros_done, 1)

            def step(g, t, project, next_batch, next_group):
                b, c, half = t // 2, t % 2, t // 4
                dve.wait_ge(s_ready, g * 8 + (t + 1))
                dve.wait_ge(dec_done, g * 4 + (b + 1))
                for h in range(GRP):
                    last = nc.vector.scalar_tensor_tensor(
                        prob[:, h], ps_s[:, h * P:(h + 1) * P], scal[:, t, 1, h:h + 1],
                        dec[:, b % 2, h, c], ALU.mult, ALU.mult)
                last.then_inc(prob_done, 1)
                if c == 1 and next_batch:
                    rotate_k(g, b)
                if project:
                    rotate_q_cos(g, t)
                if next_group and 1 <= t <= GRP:
                    split_head(g + 1, t - 1)
                if next_group and t == GRP + 1:
                    split_kv(g + 1)
                if project:
                    rotate_q_add(g, t)
                add_out(g, t)
                dve.wait_ge(sqhi_done, g * 8 + (t + 1))
                split_lo(nc.vector, sq_lo[:], sq[:], sq_hi[:]).then_inc(sqlo_done, 1)
                dve.wait_ge(sg_done, g * 8 + (4 * half + 4))
                nc.vector.tensor_tensor(z[:], ps_y[:].rearrange("p (h i) -> p h i", h=GRP),
                                        sg[:, half, :, rows_of(t)], ALU.mult).then_inc(zz_done, 1)
                if c == 0 and next_batch:
                    copy_scalars(g, b)
                if t == 0:
                    split_o_hi(g)
                dve.wait_ge(zz_done, g * 8 + (t + 1))
                dve.wait_ge(rms_done, g * 8 + (t + 1))
                nc.vector.tensor_tensor(z[:], z[:], rms[:].rearrange("p (h i) -> p h i", h=GRP),
                                        ALU.mult).then_inc(z_done, 1)
                if project:
                    cap(g, t)
                dve.wait_ge(zhi_done, g * 8 + (t + 2))
                split_lo(nc.vector, z_lo[:], z[:], z_hi[:]).then_inc(zlo_done, 1)
                if t == 0:
                    split_o_lo(g)
                if project:
                    gate(g, t)
                if not next_group and t == 6:
                    guard_gates()

            groups(dve, step)
            add_out(KVH - 1, NT)
            dve.wait_ge(mod_turned, 2)
            nc.vector.tensor_copy(modT[:, 2], ps_late_modT[:, 0])
            nc.vector.tensor_scalar(modT[:, 3], ps_late_modT[:, 1], 1.0, None, ALU.add)

        @block.gpsimd
        def _(pool):
            def mask(g, b):
                cells = dec[:, (b + 1) % 2].rearrange("p h c i -> p (h c) i")
                pool.wait_ge(expg_done, g * 4 + (b + 2))
                nc.gpsimd.tensor_tensor(cells, cells,
                                        future[:].unsqueeze(1).broadcast_to([P, GRP * CPB, CHUNK]),
                                        ALU.add).then_inc(mask_done, 1)

            def rotate_q_sin(g, t):
                pool.wait_ge(swap_done, g * 8 + (t + 5))
                q2 = q_sin[:].rearrange("p (b i) -> p b i", b=2)
                nc.gpsimd.tensor_tensor(q2, q2, sinT, ALU.mult).then_inc(qsin_done, 1)

            def weigh_v(g, b):
                bn = (b + 1) % B
                pool.wait_ge(v_done, g * 4 + (b + 2))
                pool.wait_ge(scal_done, g * 4 + (b + 2))
                nc.gpsimd.tensor_tensor(
                    vw[:], v[:, bn % 2, 0].unsqueeze(1).broadcast_to([P, GRP, D]),
                    scal[:, bn * CPB, 2].unsqueeze(2).broadcast_to([P, GRP, D]), ALU.mult)\
                    .then_inc(vw_done, 1)

            def weigh_q(g, b):
                bn = (b + 1) % B
                pool.wait_ge(rope_done, g * 8 + (4 * ((b + 1) // 2) + 4))
                at = (bn % 2 * CPB + 1) * P
                nc.gpsimd.tensor_tensor(qe[:, bn % 2], qe[:, bn % 2], qT[:, bn // 2, :, at:at + P],
                                        ALU.mult).then_inc(qe_done, 1)

            nc.gpsimd.memset(eps_col[:], EPS)
            nc.gpsimd.memset(future[:], 0.0).then_inc(future_done, 1)
            nc.gpsimd.memset(ones[:].bitcast(F32), 1.0).then_inc(ones_done, 1)
            nc.gpsimd.memset(wo_hi[:].bitcast(F32), 0.0)
            nc.gpsimd.memset(wo_lo[:].bitcast(F32), 0.0).then_inc(wo_split, 1)
            nc.gpsimd.memset(z_hi[:].bitcast(F32), 0.0).then_inc(zhi_done, 1)
            nc.gpsimd.memset(z_lo[:].bitcast(F32), 0.0).then_inc(zlo_done, 1)
            pool.wait_ge(future_done, 1)
            nc.gpsimd.affine_select(out=future[:], in_=future[:], compare_op=ALU.is_ge, fill=MASKED,
                                    base=0, pattern=[[1, CHUNK]], channel_multiplier=-1)\
                .then_inc(future_done, 1)
            for t in range(NT):
                norm.pool_split_lo(pool, t)
            for t in range(-4, 0):
                rotate_q_sin(0, t)
                if t == -4:
                    pool.wait_ge(norm.turned, NT)
                    nc.gpsimd.memset(x1[:], 0.0).then_inc(zeros_done, 1)
            pool.wait_ge(future_done, 2)
            mask(0, -1)
            weigh_v(0, -1)
            weigh_q(0, -1)

            def step(g, t, project, next_batch, next_group):
                b, c = t // 2, t % 2
                if project:
                    rotate_q_sin(g, t)
                if c == 1 and next_batch:
                    weigh_v(g, b)
                    weigh_q(g, b)
                if c == 0 and next_batch:
                    mask(g, b)

            groups(pool, step)


def block_ffn(nc, x1, hT_hi, hT_lo, modT, ident, modrow, x_in, wgu_in, wd_in, out):
    with ExitStack() as both:
        def sb2(name, shape, dt=F32):
            return both.enter_context(nc.sbuf_tensor(name, shape, dt))

        a_hi, a_lo = sb2("a_hi", [P, IT, B * L], F32R), sb2("a_lo", [P, IT, B * L], F32R)
        EARLY = 6
        raw_d = sb2("raw_d", [P, EARLY, HID])
        grow = sb2("grow", [P, B, HID])
        d_loaded = both.enter_context(nc.semaphore("d_loaded"))
        gb_loaded = both.enter_context(nc.semaphore("gb_loaded"))

        with ExitStack() as ctx:
            def sb(name, shape, dt=F32):
                return ctx.enter_context(nc.sbuf_tensor(name, shape, dt))

            def sem(name):
                return ctx.enter_context(nc.semaphore(name))

            xt = sb("xt", [P, 2, HID])
            raw = sb("raw_gu", [P, 2, KT, 2 * P])
            w_hi, w_lo = sb("wgu_hi", [P, 2, KT, 2 * P], F32R), sb("wgu_lo", [P, 2, KT, 2 * P], F32R)
            prod = sb("prod", [P, 2, HALF])
            norm = Norm(ctx, nc, "2", x1, hT_hi, hT_lo, modT[:, 2], modT[:, 3], ident,
                        [ctx.enter_context(nc.psum_tensor(f"ps_ln{i}", [P, HID], F32))
                         for i in range(2)], False, sb("hf", [P, 2, KT, P]))
            ps_g = [ctx.enter_context(nc.psum_tensor(f"ps_fg{i}", [P, HALF], F32)) for i in range(2)]
            ps_u = [ctx.enter_context(nc.psum_tensor(f"ps_fu{i}", [P, HALF], F32)) for i in range(2)]
            ga_loaded = sem("ga_loaded")
            xt_loaded = [sem(f"xt_loaded{i}") for i in range(2)]
            w_loaded = [sem(f"wgu_loaded{i}") for i in range(2)]
            scaled = sem("scaled")
            residual = sem("residual")
            whi_done = sem("whi_done")
            w_split = sem("w_split")
            gate_ready = sem("gate_ready")
            up_ready = sem("up_ready")
            silu_done = sem("silu_done")
            prod_done = sem("prod_done")
            ahi_done = sem("ahi_done")
            alo_done = sem("alo_done")
            block = ctx.enter_context(nc.Block())

            def inner_tiles(engine, step):
                step(0, 0, 0, True, True)
                with engine.Fori(0, (IT - 3) // 2) as i:
                    step(i, 2, 1, True, True)
                    step(i, 2, 2, True, True)
                step(0, 0, IT - 2, False, True)
                step(0, 0, IT - 1, False, False)

            @block.sync
            def _(sp):
                def load_w(i, per, k, parity):
                    sp.dma_start(raw[:, parity], wgu_in[bass.ds(i * per + k, 1)]
                                 .rearrange("o p k n -> (o p) k n")).then_inc(w_loaded[parity], 16)

                sp.dma_start(grow[:].rearrange("p b n -> p (b n)"), modrow[0].partition_broadcast(P))\
                    .then_inc(ga_loaded, 16)
                for t in range(NT):
                    if t >= 2:
                        sp.wait_ge(residual, t - 1)
                    sp.dma_start(xt[:, t % 2], x_in[t]).then_inc(xt_loaded[t % 2], 16)
                    if t == 1:
                        load_w(0, 0, 0, 0)
                        load_w(0, 0, 1, 1)
                sp.wait_ge(scaled, NT)
                sp.dma_start(grow[:].rearrange("p b n -> p (b n)"), modrow[1].partition_broadcast(P))\
                    .then_inc(gb_loaded, 16)
                sp.dma_start(raw_d[:], wd_in[0:EARLY].rearrange("k p n -> p k n")).then_inc(d_loaded, 16)

                def step(i, per, k, prefetch, next_split):
                    if prefetch:
                        sp.wait_ge(w_split, i * per + (k + 1))
                        load_w(i, per, k + 2, k % 2)

                inner_tiles(sp, step)

            @block.tensor
            def _(pe):
                for t in range(NT):
                    norm.tensor_turn(pe, t)

                def product(bank, s, half, u, done):
                    for k in range(KT):
                        cut = slice(half * HALF, (half + 1) * HALF)
                        cols = slice(u * P, (u + 1) * P)
                        last = three_products(nc.tensor, bank[:], w_hi[:, s, k, cols],
                                              w_lo[:, s, k, cols], hT_hi[:, k, cut],
                                              hT_lo[:, k, cut], k == 0, k == KT - 1)
                    last.then_inc(done, 1)

                def step(i, per, k, prefetch, next_split):
                    pe.wait_ge(w_split, i * per + (k + 1))
                    for half in range(2):
                        if k == 0:
                            pe.wait_ge(norm.lo_done, (half + 1) * NT // 2)
                        else:
                            pe.wait_ge(prod_done, i * (2 * per) + (2 * k - 1 + half))
                        product(ps_g[half], k % 2, half, 0, gate_ready)
                        product(ps_u[half], k % 2, half, 1, up_ready)

                inner_tiles(pe, step)

            @block.scalar
            def _(act):
                norm.scalar_rstd(act, 0)
                norm.scalar_rstd(act, 1)
                for t in range(NT):
                    norm.scalar_modulate(act, t)

                def step(i, per, k, prefetch, next_split):
                    for half in range(2):
                        at = i * (2 * per) + (2 * k + half + 1)
                        if k > 0:
                            act.wait_ge(alo_done, i * (2 * per) + (2 * k - 1 + half))
                        act.wait_ge(gate_ready, at)
                        nc.scalar.activation(prod[:, half], ps_g[half][:], ACT.Silu)\
                            .then_inc(silu_done, 1)
                        act.wait_ge(prod_done, at)
                        nc.scalar.activation(
                            a_hi[:, bass.ds(i * per + k, 1), half * HALF:(half + 1) * HALF],
                            prod[:, half].unsqueeze(1), ACT.Copy).then_inc(ahi_done, 1)

                inner_tiles(act, step)

            @block.vector
            def _(dve):
                def split_w(i, per, k):
                    s = k % 2
                    count = 16 * (k // 2 + 1)
                    dve.wait_ge(w_loaded[s], i * (8 * per) + count)
                    split_hi(nc.vector, w_hi[:, s], raw[:, s]).then_inc(whi_done, 1)
                    dve.wait_ge(whi_done, i * per + (k + 1))
                    split_lo(nc.vector, w_lo[:, s], raw[:, s], w_hi[:, s]).then_inc(w_split, 1)

                dve.wait_ge(ga_loaded, 16)
                for t in range(NT):
                    nc.vector.tensor_tensor(x1[:, t], x1[:, t], grow[:, t // CPB], ALU.mult)\
                        .then_inc(scaled, 1)
                for t in range(NT):
                    dve.wait_ge(scaled, t + 1)
                    dve.wait_ge(xt_loaded[t % 2], 16 * (t // 2 + 1))
                    nc.vector.tensor_tensor(x1[:, t], x1[:, t], xt[:, t % 2], ALU.add)\
                        .then_inc(residual, 1)
                    dve.wait_ge(residual, t + 1)
                    norm.vector_stats(dve, t)
                norm.vector_var(dve, 0)
                norm.vector_var(dve, 1)
                split_w(0, 0, 0)
                norm.vector_all(dve)

                def step(i, per, k, prefetch, next_split):
                    if next_split:
                        split_w(i, per, k + 1)
                    for half in range(2):
                        at = i * (2 * per) + (2 * k + half + 1)
                        dve.wait_ge(silu_done, at)
                        dve.wait_ge(up_ready, at)
                        nc.vector.tensor_tensor(prod[:, half], ps_u[half][:], prod[:, half], ALU.mult)\
                            .then_inc(prod_done, 1)
                        dve.wait_ge(ahi_done, at)
                        cut = slice(half * HALF, (half + 1) * HALF)
                        split_lo(nc.vector, a_lo[:, bass.ds(i * per + k, 1), cut],
                                 prod[:, half].unsqueeze(1),
                                 a_hi[:, bass.ds(i * per + k, 1), cut]).then_inc(alo_done, 1)

                inner_tiles(dve, step)

        with ExitStack() as ctx:
            def sb(name, shape, dt=F32):
                return ctx.enter_context(nc.sbuf_tensor(name, shape, dt))

            def sem(name):
                return ctx.enter_context(nc.semaphore(name))

            OLD = KT * B * L // HID
            old_hi, old_lo = (h[:].rearrange("p k (m n) -> p (k m) n", n=HID) for h in (hT_hi, hT_lo))
            new_hi, new_lo = (sb(n, [P, IT - OLD, HID], F32R) for n in ("d_hi", "d_lo"))
            raw_d2 = sb("raw_d2", [P, IT - EARLY, HID])
            res = sb("res", [P, 2, HID])
            ps_d = [ctx.enter_context(nc.psum_tensor(f"ps_d{i}", [P, HID], F32)) for i in range(2)]
            d2_loaded = sem("d2_loaded")
            dhi_done = sem("dhi_done")
            d_split = sem("d_split")
            down_ready = sem("down_ready")
            res_scaled = sem("res_scaled")
            res_done = sem("res_done")
            out_stored = [sem(f"out_stored{i}") for i in range(2)]
            block = ctx.enter_context(nc.Block())

            def d_hi(k):
                return old_hi[:, k] if k < OLD else new_hi[:, k - OLD]

            def d_lo(k):
                return old_lo[:, k] if k < OLD else new_lo[:, k - OLD]

            def raw_tile(k):
                return raw_d[:, k] if k < EARLY else raw_d2[:, k - EARLY]

            @block.scalar
            def _(act):
                act.wait_ge(d_loaded, 16)
                for k in range(IT):
                    if k == EARLY:
                        act.wait_ge(d2_loaded, 16)
                    nc.scalar.activation(d_hi(k), raw_tile(k), ACT.Copy).then_inc(dhi_done, 1)

            @block.vector
            def _(dve):
                for k in range(IT):
                    dve.wait_ge(dhi_done, k + 1)
                    split_lo(nc.vector, d_lo(k), raw_tile(k), d_hi(k)).then_inc(d_split, 1)
                dve.wait_ge(gb_loaded, 16)
                for t in range(NT):
                    dve.wait_ge(down_ready, t + 1)
                    if t >= 2:
                        dve.wait_ge(out_stored[t % 2], 16 * (t // 2))
                    nc.vector.tensor_tensor(res[:, t % 2], ps_d[t % 2][:], grow[:, t // CPB], ALU.mult)\
                        .then_inc(res_scaled, 1)
                    dve.wait_ge(res_scaled, t + 1)
                    nc.vector.tensor_tensor(res[:, t % 2], res[:, t % 2], x1[:, t], ALU.add)\
                        .then_inc(res_done, 1)

            @block.tensor
            def _(pe):
                for t in range(NT):
                    if t >= 2:
                        pe.wait_ge(res_scaled, t - 1)
                    cut = slice(t * P, (t + 1) * P)
                    for k in range(IT):
                        if t == 0:
                            pe.wait_ge(d_split, k + 1)
                        last = three_products(nc.tensor, ps_d[t % 2][:], a_hi[:, k, cut], a_lo[:, k, cut],
                                              d_hi(k), d_lo(k), k == 0, k == IT - 1)
                    last.then_inc(down_ready, 1)

            @block.sync
            def _(sp):
                sp.dma_start(raw_d2[:], wd_in[EARLY:IT].rearrange("k p n -> p k n"))\
                    .then_inc(d2_loaded, 16)
                for t in range(NT):
                    sp.wait_ge(res_done, t + 1)
                    sp.dma_start(out[t], res[:, t % 2]).then_inc(out_stored[t % 2], 16)
                for s in range(2):
                    sp.wait_ge(out_stored[s], 16 * (NT // 2))


def constants():
    import numpy as np

    cst = np.zeros((P, C_END), np.float32)
    cst[:, C_ID:C_ID + P] = np.eye(P)
    cst[:, C_TRI:C_TRI + P] = np.triu(np.ones((P, P)))
    inv = (np.float32(1.0) / np.float32(10000.0) ** (np.arange(0, D, 2, dtype=np.float32) / np.float32(D)))
    ang = np.arange(L, dtype=np.float32)[:, None] * inv.astype(np.float32)
    cos = np.concatenate([np.cos(ang)] * 2, axis=1).astype(np.float32)
    sin = np.concatenate([-np.sin(ang), np.sin(ang)], axis=1).astype(np.float32)
    cst[:, C_COST:C_COST + L] = cos.T
    cst[:, C_SINT:C_SINT + L] = sin.T
    cst[:, C_COS:C_COS + L] = cos.reshape(CPB, P, D).transpose(1, 0, 2).reshape(P, L)
    cst[:, C_SIN:C_SIN + L] = sin.reshape(CPB, P, D).transpose(1, 0, 2).reshape(P, L)
    return cst


def kernel(L0_attn_hidden_states, L0_attn_Wq, L0_attn_Wk, L0_attn_Wv, L0_attn_Wo, L0_attn_Wg,
           L0_attn_Win, L0_attn_dt_bias, L0_attn_A_log_bias, L0_attn_gnorm_w, L0_ffn_w_gate,
           L0_ffn_w_up, L0_ffn_w_down, L0_c, L0_wmod):
    import numpy as np
    import concourse.bacc as bacc
    from concourse.bass_utils import run_bass_kernel_spmd

    def f(a):
        return np.asarray(a)

    def heads(w):
        w = f(w)
        return w.reshape(w.shape[0] // D, D, KT, P).transpose(0, 3, 2, 1)

    pad = IT * P - INTER
    wg, wu = (np.pad(f(w), ((0, pad), (0, 0))) for w in (L0_ffn_w_gate, L0_ffn_w_up))
    wd = np.pad(f(L0_ffn_w_down), ((0, 0), (0, pad)))
    arrays = {
        "x_in": f(L0_attn_hidden_states).reshape(NT, P, HID),
        "cT_in": f(L0_c).reshape(B, KT, P).transpose(2, 1, 0).reshape(P, KT * B),
        "wmod_in": f(L0_wmod).reshape(KT, P, 6, HID).transpose(2, 1, 0, 3),
        "wq_in": heads(L0_attn_Wq),
        "wg_in": heads(L0_attn_Wg),
        "wkv_in": np.concatenate([heads(L0_attn_Wk), heads(L0_attn_Wv)], axis=3),
        "wo_in": f(L0_attn_Wo).reshape(HID, KVH, GRP, D).transpose(1, 3, 2, 0),
        "win_in": np.pad(f(L0_attn_Win).reshape(H, KT, P).transpose(2, 1, 0),
                         ((0, 0), (0, 0), (0, P - H))),
        "rows_in": np.stack([f(L0_attn_dt_bias), f(L0_attn_A_log_bias)]),
        "gnorm_in": f(L0_attn_gnorm_w).reshape(P, 1),
        "wgu_in": np.concatenate([heads(wg), heads(wu)], axis=3),
        "wd_in": wd.T.reshape(IT, P, HID),
        "cst_in": constants(),
    }
    nc = bacc.Bacc("TRN2", target_bir_lowering=False, num_devices=1)
    arrays = {name: np.ascontiguousarray(a) for name, a in arrays.items()}
    args = {name: nc.dram_tensor(name, a.shape, F32, kind="ExternalInput").ap()
            for name, a in arrays.items()}
    out = nc.dram_tensor("out", (NT, P, HID), F32, kind="ExternalOutput").ap()
    build(nc, out=out, **args)
    r = run_bass_kernel_spmd(nc, [arrays], core_ids=[0])
    return r.results[0]["out"].reshape(B, L, HID)
```

```python
from contextlib import ExitStack

import concourse.bass as bass
from concourse import mybir

ALU = mybir.AluOpType
ACT = mybir.ActivationFunctionType
F32 = mybir.dt.float32
F32R = mybir.dt.float32r

P = 128
B, L, HID = 4, 256, 512
H, KVH, D = 32, 8, 128
CHUNK = 128
INTER = 1376
EPS = 1e-5
GRP = H // KVH
KT = HID // P
NT = B * L // P
CPB = L // CHUNK
IT = -(-INTER // P)
HALF = B * L // 2
assert CHUNK == P and D == P and CPB == 2 and HALF == 512 and GRP == 4 and NT == 8

C_ID, C_COST, C_SINT, C_COS, C_SIN, C_TRI, C_END = 0, 128, 384, 640, 896, 1152, 1280
EXP_CAP = 1e18
MASKED = -1e30
POOL_TILES = 7
SERIES, INNER = (13, 11, 9, 7, 5, 3), 3
CHAIN_ABS = 3
CHAIN_SQUARE = CHAIN_ABS + 4
CHAIN_G = CHAIN_SQUARE + 1 + len(SERIES) + 4
CHAIN_DIFF = CHAIN_G + 1
CHAIN_END = CHAIN_DIFF + 1
GUARD_END = 4
SA, CA, GA, SB, CB, GB = range(6)


def split_hi(engine, hi, full):
    return engine.tensor_copy(hi, full)


def split_lo(engine, lo, full, hi):
    return engine.tensor_tensor(lo, full, hi.bitcast(F32), ALU.subtract)


def three_products(pe, out, w_hi, w_lo, x_hi, x_lo, first, last):
    pe.matmul(out, w_hi, x_hi, start=first, stop=False)
    pe.matmul(out, w_hi, x_lo, start=False, stop=False)
    return pe.matmul(out, w_lo, x_hi, start=False, stop=last)


def build(nc, x_in, cT_in, wmod_in, wq_in, wg_in, wkv_in, wo_in, win_in, rows_in, gnorm_in,
          wgu_in, wd_in, cst_in, out):
    modrow = nc.dram_tensor("modrow", (2, B * HID), F32, kind="Internal").ap()
    gT_dram = nc.dram_tensor("gT_dram", (H, B * L), F32, kind="Internal").ap()

    with ExitStack() as outer:
        def sb(name, shape, dt=F32):
            return outer.enter_context(nc.sbuf_tensor(name, shape, dt))

        cst = sb("cst", [P, C_TRI])
        x1 = sb("x1", [P, NT, HID])
        hT_hi = sb("hT_hi", [P, KT, B * L], F32R)
        hT_lo = sb("hT_lo", [P, KT, B * L], F32R)
        tok = sb("tok", [P, NT, 3, H])
        modT = sb("modT", [P, 4, KT, B])
        gnorm = sb("gnorm", [P, 1])
        raw_pair = sb("raw_pair", [P, KT, 2 * P])
        norm_rows = [sb("stats", [P, NT, 6]), sb("mv", [P, NT, 2]), sb("var", [P, NT]),
                     sb("rstd", [P, NT])]
        ident = cst[:, C_ID:C_ID + P]

        block_attention(nc, cst, x1, hT_hi, hT_lo, tok, modT, gnorm, ident, modrow, gT_dram,
                        x_in, cT_in, wmod_in, wq_in, wg_in, wkv_in, wo_in, win_in, rows_in,
                        gnorm_in, cst_in, wgu_in, norm_rows, raw_pair)
        block_ffn(nc, x1, hT_hi, hT_lo, modT, ident, modrow, wgu_in, wd_in, out, norm_rows,
                  raw_pair)


class Norm:

    def __init__(self, ctx, nc, tag, rows, x1, hT_hi, hT_lo, shift, scale, ident, banks,
                 in_place, hf, rows_given=False):
        def sb(name, shape, dt=F32):
            return ctx.enter_context(nc.sbuf_tensor(name + tag, shape, dt))

        def sem(name):
            return ctx.enter_context(nc.semaphore(name + tag))

        self.nc, self.x1, self.hT_hi, self.hT_lo = nc, x1, hT_hi, hT_lo
        self.shift, self.scale, self.ident = shift, scale, ident
        self.stats, self.mv, self.var, self.rstd = rows
        self.rows_given = rows_given
        self.in_place = in_place
        self.xn = x1 if in_place else sb("xn", [P, 4, HID])
        self.hf = hf
        self.hf_slots = hf.shape[1] if hf is not None else 0
        self.ps = banks
        self.stats_done = sem("stats_done")
        self.mv_done = sem("mv_done")
        self.var_done = sem("var_done")
        self.lnvar_done = sem("lnvar_done")
        self.rstd_done = sem("rstd_done")
        self.xn_done = sem("xn_done")
        self.turned = sem("turned")
        self.hf_done = sem("hf_done")
        self.hi_done = sem("hi_done")
        self.lo_done = sem("lo_done")

    def vector_stats(self, dve, t):
        nc = self.nc
        nc.vector.bn_stats(self.stats[:, t], self.x1[:, t]).then_inc(self.stats_done, 1)
        dve.wait_ge(self.stats_done, t + 1)
        nc.vector.bn_aggr(self.mv[:, t], self.stats[:, t]).then_inc(self.mv_done, 1)

    def half(self, i):
        return slice(i * NT // 2, (i + 1) * NT // 2)

    def vector_var(self, dve, i):
        dve.wait_ge(self.mv_done, (i + 1) * NT // 2)
        self.nc.vector.tensor_scalar(self.var[:, self.half(i)], self.mv[:, self.half(i), 1], EPS, None,
                                     ALU.add).then_inc(self.var_done, 1)

    def scalar_rstd(self, act, i):
        nc, var = self.nc, self.var[:, self.half(i)]
        act.wait_ge(self.var_done, i + 1)
        nc.scalar.activation(var, var, ACT.Ln).then_inc(self.lnvar_done, 1)
        act.wait_ge(self.lnvar_done, i + 1)
        nc.scalar.activation(self.rstd[:, self.half(i)], var, ACT.Exp, scale=-0.5)\
            .then_inc(self.rstd_done, 1)

    def xn_of(self, t):
        return self.xn[:, t if self.in_place else t % 4]

    def vector_normalise(self, dve, t):
        if t % (NT // 2) == 0 and not self.rows_given:
            dve.wait_ge(self.rstd_done, t // (NT // 2) + 1)
        if t >= 4 and not self.in_place:
            dve.wait_ge(self.turned, t - 3)
        self.nc.vector.tensor_scalar(self.xn_of(t), self.x1[:, t], self.mv[:, t, 0:1],
                                     self.rstd[:, t:t + 1], ALU.subtract, ALU.mult)\
            .then_inc(self.xn_done, 1)

    def bank(self, t):
        return self.ps[t % len(self.ps)][:].rearrange("p (k i) -> p k i", k=KT)

    def tensor_turn(self, pe, t):
        pe.wait_ge(self.xn_done, t + 1)
        if t >= len(self.ps):
            pe.wait_ge(self.hf_done, t - len(self.ps) + 1)
        for k in range(KT):
            last = self.nc.tensor.transpose(self.bank(t)[:, k], self.xn_of(t)[:, k * P:(k + 1) * P],
                                            self.ident)
        last.then_inc(self.turned, 1)

    def scalar_modulate(self, act, t):
        b = t // CPB
        act.wait_ge(self.turned, t + 1)
        if t >= self.hf_slots:
            act.wait_ge(self.lo_done, t - self.hf_slots + 1)
        for k in range(KT):
            last = self.nc.scalar.activation(self.hf[:, t % self.hf_slots, k], self.bank(t)[:, k], ACT.Identity,
                                             bias=self.shift[:, k, b:b + 1],
                                             scale=self.scale[:, k, b:b + 1])
        last.then_inc(self.hf_done, 1)

    def vector_split(self, dve, t, with_lo=True):
        hi, lo = self.hT_hi[:, :, t * P:(t + 1) * P], self.hT_lo[:, :, t * P:(t + 1) * P]
        dve.wait_ge(self.hf_done, t + 1)
        split_hi(self.nc.vector, hi, self.hf[:, t % self.hf_slots]).then_inc(self.hi_done, 1)
        if with_lo:
            dve.wait_ge(self.hi_done, t + 1)
            split_lo(self.nc.vector, lo, self.hf[:, t % self.hf_slots], hi).then_inc(self.lo_done, 1)

    def pool_split_lo(self, pool, t):
        hi, lo = self.hT_hi[:, :, t * P:(t + 1) * P], self.hT_lo[:, :, t * P:(t + 1) * P]
        pool.wait_ge(self.hi_done, t + 1)
        split_lo(self.nc.gpsimd, lo, self.hf[:, t % self.hf_slots], hi).then_inc(self.lo_done, 1)


def block_attention(nc, cst, x1, hT_hi, hT_lo, tok, modT, gnorm, ident, modrow, gT_dram,
                    x_in, cT_in, wmod_in, wq_in, wg_in, wkv_in, wo_in, win_in, rows_in,
                    gnorm_in, cst_in, wgu_in, norm_rows, raw_pair):
    with ExitStack() as ctx:
        def sb(name, shape, dt=F32):
            return ctx.enter_context(nc.sbuf_tensor(name, shape, dt))

        def ps(name):
            return ctx.enter_context(nc.psum_tensor(name, [P, HALF], F32))

        def sem(name):
            return ctx.enter_context(nc.semaphore(name))

        wq_hi, wq_lo = (sb(n, [P, GRP, KT, D], F32R) for n in ("wq_hi", "wq_lo"))
        wg_hi, wg_lo = (sb(n, [P, GRP, KT, D], F32R) for n in ("wg_hi", "wg_lo"))
        wkv_hi, wkv_lo = (sb(n, [P, KT, 2 * D], F32R) for n in ("wkv_hi", "wkv_lo"))
        wo_hi, wo_lo = (sb(n, [P, GRP, HID], F32R) for n in ("wo_hi", "wo_lo"))
        raw_q, raw_g = sb("raw_q", [P, KT, D]), sb("raw_g", [P, KT, D])
        raw_kv, raw_o = raw_pair, sb("raw_o", [P, GRP, HID])
        qT = sb("qT", [P, 2, GRP, HALF])
        sg = sb("sg", [P, 2, GRP, HALF])
        dec = sb("dec", [P, 2, GRP, CPB, CHUNK])
        v_hi, v_lo = sb("v_hi", [P, 2, CPB, D], F32R), sb("v_lo", [P, 2, CPB, D], F32R)
        kT = sb("kT", [P, 2, CPB * CHUNK])
        qe = sb("qe", [P, 2, GRP, CHUNK])
        scal = sb("scal", [P, NT, 3, GRP])
        kr = sb("kr", [P, CPB, D])
        v = sb("v", [P, CPB, D])
        vw = sb("vw", [P, GRP, D])
        state = sb("state", [P, GRP, D])
        work = sb("work", [P, GRP, CHUNK])
        prob, z = work, work
        sq = work[:].rearrange("p h i -> p (h i)")
        prob_hi, prob_lo = (sb(n, [P, GRP, CHUNK], F32R) for n in ("prob_hi", "prob_lo"))
        sq_hi, sq_lo = sb("sq_hi", [P, HALF], F32R), sb("sq_lo", [P, HALF], F32R)
        rms = sb("rms", [P, HALF])
        z_hi, z_lo = sb("z_hi", [P, GRP, CHUNK], F32R), sb("z_lo", [P, GRP, CHUNK], F32R)
        sig = sb("sig", [P, HALF])
        q_cos, q_sin = sb("q_cos", [P, HALF]), sb("q_sin", [P, HALF])
        k_cos, k_sin = (q_cos[:, i * CPB * D:(i + 1) * CPB * D].rearrange("p (c d) -> p c d", c=CPB)
                        for i in range(2))
        prob_tail = sig[:].rearrange("p (h i) -> p h i", h=GRP)
        ones = sb("ones_r", [P, P], F32R)
        eps_col = sb("eps_col", [P, 1])
        future = sb("future", [P, CHUNK])
        ps_q, ps_g, ps_kv, ps_s, ps_y, ps_st, ps_ss, ps_o = (
            ps(n) for n in ("ps_q", "ps_gt", "ps_kv", "ps_s", "ps_y", "ps_st", "ps_ss", "ps_o"))

        silu_c = sb("silu_c", [P, KT * B])
        win, win_hi, win_lo = (w[:].rearrange("p (k h) -> p k h", k=KT) for w in (q_cos, sq_hi, sq_lo))
        rows = vw[:, 1, 0:2 * H].rearrange("p (r h) -> p r h", r=2)
        rate = vw[:, 1, 2 * H:3 * H]
        cT, sig_c = (vw[:, 2, i * KT * B:(i + 1) * KT * B] for i in range(2))
        z1, za, zs, zs2, zq, gdec = (
            raw_o[:, i // 2, i % 2 * NT * H:(i % 2 + 1) * NT * H].rearrange("p (t h) -> p t h", h=H)
            for i in range(6))
        zT = gT = [sq[0:H], rms[0:H]]
        tri = state[:, 0]
        hf = dec[:, 1].rearrange("p (s h) c i -> p s (h c) i", s=2)
        wmod = {SA: qT[:, 1], CA: sg[:, 1]}
        mod_rows = sg[0:B, 0, 0:2]
        ps_rows = {SA: ps_q[0:B], CA: ps_g[0:B]}
        ps_modT = ps_o[:, 0:2 * KT * B].rearrange("p (m k b) -> p m k b", m=2, k=KT)
        ps_z, ps_glast = (ps_o[:, i * NT * H:(i + 1) * NT * H].rearrange("p (t h) -> p t h", h=H)
                          for i in range(2))
        ps_zT = ps_gT = [ps_st, ps_ss]
        wmod[GA] = raw_o
        wmod[GB] = [raw_kv[:, 0:2].rearrange("p k d -> p (k d)"),
                    raw_kv[:, 2:4].rearrange("p k d -> p (k d)"),
                    raw_q[:].rearrange("p k d -> p (k d)"), raw_g[:].rearrange("p k d -> p (k d)")]
        wmod[CB], wmod[SB] = qT[:, 0], sg[:, 0]
        late_rows = dec[0:B, 0].rearrange("p h c i -> p (h c i)")\
            .rearrange("p (m n) -> p m n", m=2)
        gates = [q_sin[0:B], tok[0:B].rearrange("p t r h -> p (t r h)")[:, 0:HID]]
        gmag = q_cos[0:B]
        ps_rows.update({GA: ps_q[0:B], GB: ps_g[0:B], SB: ps_kv[0:B], CB: ps_q[0:B]})
        ps_late_modT = ps_q[:, 0:2 * KT * B].rearrange("p (m k b) -> p m k b", m=2, k=KT)
        grow, x_again = raw_o, [qT[:, 0], sg[:, 0]]
        norm = Norm(ctx, nc, "1", norm_rows, x1, hT_hi, hT_lo, modT[:, 0], modT[:, 1], ident,
                    [ps_s, ps_y, ps_st, ps_ss], True, hf)
        norm2 = Norm(ctx, nc, "2", norm_rows, x1, None, None, None, None, None, None, True, None)

        cosT = cst[:, C_COST:C_COST + L].unsqueeze(1).broadcast_to([P, 2, L])
        sinT = cst[:, C_SINT:C_SINT + L].unsqueeze(1).broadcast_to([P, 2, L])
        cos_k = cst[:, C_COS:C_COS + L].rearrange("p (c d) -> p c d", c=CPB)
        sin_k = cst[:, C_SIN:C_SIN + L].rearrange("p (c d) -> p c d", c=CPB)

        wh_loaded = sem("wh_loaded")
        kv_loaded = sem("kv_loaded")
        wo_loaded = sem("wo_loaded")
        dec_loaded = sem("dec_loaded")
        wh_hi_done = sem("wh_hi_done")
        wh_split = sem("wh_split")
        kv_hi_done = sem("kv_hi_done")
        kv_split = sem("kv_split")
        wo_hi_done = sem("wo_hi_done")
        wo_split = sem("wo_split")
        q_ready = sem("q_ready")
        g_ready = sem("g_ready")
        kv_ready = sem("kv_ready")
        kt_ready = sem("kt_ready")
        s_ready = sem("s_ready")
        y_ready = sem("y_ready")
        st_ready = sem("st_ready")
        ss_ready = sem("ss_ready")
        o_ready = sem("o_ready")
        swap_done = sem("swap_done")
        qsin_done = sem("qsin_done")
        qcos_done = sem("qcos_done")
        rope_done = sem("rope_done")
        esig_done = sem("esig_done")
        cap_done = sem("cap_done")
        lsig_done = sem("lsig_done")
        sig_done = sem("sig_done")
        sg_done = sem("sg_done")
        kparts_done = sem("kparts_done")
        kr_done = sem("kr_done")
        v_done = sem("v_done")
        kT_done = sem("kT_done")
        scal_done = sem("scal_done")
        expg_done = sem("expg_done")
        mask_done = sem("mask_done")
        dec_done = sem("dec_done")
        vw_done = sem("vw_done")
        qe_done = sem("qe_done")
        state_done = sem("state_done")
        prob_done = sem("prob_done")
        phi_done = sem("phi_done")
        plo_done = sem("plo_done")
        vlo_done = sem("vlo_done")
        sq_done = sem("sq_done")
        sqhi_done = sem("sqhi_done")
        sqlo_done = sem("sqlo_done")
        zz_done = sem("zz_done")
        lnss_done = sem("lnss_done")
        rms_done = sem("rms_done")
        z_done = sem("z_done")
        zhi_done = sem("zhi_done")
        zlo_done = sem("zlo_done")
        zeros_done = sem("zeros_done")
        future_done = sem("future_done")
        ones_done = sem("ones_done_r")
        sums_done = sem("sums_done")
        c_loaded = sem("c_loaded")
        x_loaded = [sem(f"x_loaded{i}") for i in range(2)]
        mod_loaded = [sem(f"mod_loaded{i}") for i in range(6)]
        cst_loaded = sem("cst_loaded")
        tables_loaded = sem("tables_loaded")
        small_loaded = sem("small_loaded")
        sigc_done = sem("sigc_done")
        siluc_done = sem("siluc_done")
        rows_ready = sem("rows_ready")
        rows_copied = sem("rows_copied")
        mod_turned = sem("mod_turned")
        modT_done = sem("modT_done")
        win_split = sem("win_split")
        rate_done = sem("rate_done")
        zT_ready = sem("zT_ready")
        zT_copied = sem("zT_copied")
        z_ready = sem("z_ready")
        chain = sem("chain")
        exp_done = sem("exp_done")
        cum_ready = sem("cum_ready")
        gT_ready = sem("gT_ready")
        gT_copied = sem("gT_copied")
        gT_stored = sem("gT_stored")
        gates_ready = sem("gates_ready")
        guard = sem("guard")
        rows_stored = sem("rows_stored")
        ga_loaded = sem("ga_loaded")
        w0_loaded = sem("w0_loaded")
        xa_loaded = [sem(f"xa_loaded{i}") for i in range(2)]
        scaled = [sem(f"scaled_{n}") for n in ("pool", "dve")]
        residual = [sem(f"residual_{n}") for n in ("pool", "dve")]
        block = ctx.enter_context(nc.Block())

        def rows_of(t):
            return slice(t % 4 * P, t % 4 * P + P)

        def group_slice(g, b, size):
            g = g + 1 if b == B - 1 else g
            return bass.ds(g * size, size)

        def groups(engine, step, tail):
            with engine.Fori(0, KVH - 1) as g:
                for t in range(NT):
                    step(g, t, True, True, True)
            for t in range(NT):
                if t < 4:
                    step(KVH - 1, t, True, True, False)
                else:
                    tail(KVH - 1, t)

        def scale_sum(engine, who, t):
            engine.tensor_tensor(x1[:, t], x1[:, t], grow[:, t // CPB], ALU.mult)\
                .then_inc(scaled[who], 1)

        def add_x(engine, queue, who, t, n):
            queue.wait_ge(scaled[who], n + 1)
            queue.wait_ge(xa_loaded[t // 4], 16)
            engine.tensor_tensor(x1[:, t], x1[:, t], x_again[t // 4][:, t % 4], ALU.add)\
                .then_inc(residual[who], 1)

        @block.sync
        def _(sp):
            def load_mod(m):
                if m == GB:
                    for k in range(KT):
                        sp.dma_start(wmod[m][k], wmod_in[m][:, k]).then_inc(mod_loaded[m], 16)
                else:
                    sp.dma_start(wmod[m][:], wmod_in[m]).then_inc(mod_loaded[m], 16)

            def load_head(g, j, first=False):
                if not first:
                    sp.wait_ge(wh_split, g * 4 + j)
                sp.dma_start(raw_q[:], wq_in[bass.ds(g * 4 + j, 1)].rearrange("o p k d -> (o p) k d"))\
                    .then_inc(wh_loaded, 16)
                sp.dma_start(raw_g[:], wg_in[bass.ds(g * 4 + j, 1)].rearrange("o p k d -> (o p) k d"))\
                    .then_inc(wh_loaded, 16)

            def load_kv(g):
                sp.dma_start(raw_kv[:], wkv_in[bass.ds(g, 1)].rearrange("o p k d -> (o p) k d"))\
                    .then_inc(kv_loaded, 16)

            def load_o(g):
                sp.dma_start(raw_o[:], wo_in[bass.ds(g, 1)].rearrange("o p h n -> (o p) h n"))\
                    .then_inc(wo_loaded, 16)

            def load_dec(g, b):
                bn = (b + 1) % B
                src = gT_dram[group_slice(g, b, GRP), bn * L:(bn + 1) * L]
                sp.dma_start(dec[:, bn % 2].rearrange("p h c i -> p h (c i)"),
                             src.partition_broadcast(P)).then_inc(dec_loaded, 16)

            sp.dma_start(cT, cT_in).then_inc(c_loaded, 16)
            for half, m in enumerate((SA, CA)):
                load_mod(m)
                a = half * NT // 2
                sp.dma_start(x1[:, a:a + NT // 2], x_in[a:a + NT // 2].rearrange("t p n -> p t n"))\
                    .then_inc(x_loaded[half], 16)
            load_kv(0)
            load_head(0, 0, True)
            sp.dma_start(cst[:, C_COST:C_TRI], cst_in[:, C_COST:C_TRI]).then_inc(tables_loaded, 16)
            for j in range(1, GRP):
                load_head(0, j)
            for i in range(2):
                sp.wait_ge(gT_copied, i + 1)
                sp.dma_start(gT_dram[:, i * HALF:(i + 1) * HALF], gT[i]).then_inc(gT_stored, 16)
                sp.wait_ge(gT_stored, 16 * (i + 1))
                if i == 0:
                    load_dec(0, -1)
            sp.wait_ge(chain, CHAIN_END)
            load_o(0)

            def step(g, t, project, next_batch, next_group):
                if t % 2 == 0 and next_batch:
                    sp.wait_ge(prob_done, g * 8 + (t + 1))
                    load_dec(g, t // 2)
                if next_group and t < GRP:
                    load_head(g + 1, t)
                if next_group and t == 1:
                    sp.wait_ge(wo_split, g + 2)
                    load_o(g + 1)
                if next_group and t == 2:
                    sp.wait_ge(kv_split, g + 1)
                    load_kv(g + 1)

                if not next_group and t == 1:
                    sp.wait_ge(wo_split, KVH + 1)
                    load_mod(GA)
                    load_mod(GB)

            def tail(g, t):
                if t == 4:
                    step(g, t, False, True, False)
                    sp.wait_ge(zz_done, g * 8 + 4)
                    load_mod(CB)
                    load_mod(SB)

            groups(sp, step, tail)
            def store_gate(i):
                sp.wait_ge(guard, GUARD_END * (i + 1))
                sp.dma_start(modrow[i].rearrange("(b n) -> b n", b=B), gates[i])\
                    .then_inc(rows_stored, 16)

            store_gate(0)
            sp.wait_ge(rows_stored, 16)
            sp.dma_start(grow[:].rearrange("p b n -> p (b n)"),
                         modrow[0].partition_broadcast(P)).then_inc(ga_loaded, 16)
            for i in range(2):
                sp.wait_ge(rows_ready, 4 + i)
                a = i * NT // 2
                sp.dma_start(x_again[i], x_in[a:a + NT // 2].rearrange("t p n -> p t n"))\
                    .then_inc(xa_loaded[i], 16)
            sp.wait_ge(rows_ready, 6)
            sp.dma_start(raw_pair[:], wgu_in[0]).then_inc(w0_loaded, 16)
            store_gate(1)
            sp.wait_ge(rows_stored, 32)
            sp.wait_ge(w0_loaded, 16)

        @block.tensor
        def _(pe):
            def q_block(g, t, first=False):
                half, j = (t // 4 + 1) % 2, t % 4
                gw = g + 1 if t >= 4 else g
                pe.wait_ge(wh_split, gw * 4 + (j + 1))
                if not first:
                    pe.wait_ge(qcos_done, g * 8 + (t + 4))
                for k in range(KT):
                    cut = slice(half * HALF, (half + 1) * HALF)
                    last = three_products(nc.tensor, ps_q[:], wq_hi[:, j, k], wq_lo[:, j, k],
                                          hT_hi[:, k, cut], hT_lo[:, k, cut], k == 0, k == KT - 1)
                last.then_inc(q_ready, 1)

            def g_block(g, t, k_from, k_to, first=False):
                half, j = (t // 4 + 1) % 2, t % 4
                if k_from == 0 and not first:
                    pe.wait_ge(sg_done, g * 8 + (t + 4))
                for k in range(k_from, k_to):
                    cut = slice(half * HALF, (half + 1) * HALF)
                    last = three_products(nc.tensor, ps_g[:], wg_hi[:, j, k], wg_lo[:, j, k],
                                          hT_hi[:, k, cut], hT_lo[:, k, cut], k == 0, k == KT - 1)
                if k_to == KT:
                    last.then_inc(g_ready, 1)

            def kv_batch(g, b):
                bn = (b + 1) % B
                gw = g + 1 if b == B - 1 else g
                pe.wait_ge(kv_split, gw + 1)
                if b >= 0:
                    pe.wait_ge(kT_done, g * 4 + (b + 1))
                for c in range(CPB):
                    cut = slice((bn * CPB + c) * P, (bn * CPB + c + 1) * P)
                    for k in range(KT):
                        last = three_products(nc.tensor, ps_kv[:, c * 2 * D:(c + 1) * 2 * D],
                                              hT_hi[:, k, cut], hT_lo[:, k, cut],
                                              wkv_hi[:, k], wkv_lo[:, k], k == 0, k == KT - 1)
                last.then_inc(kv_ready, 1)

            def k_turn(g, b):
                pe.wait_ge(kr_done, g * 4 + (b + 2))
                pe.wait_ge(v_done, g * 4 + (b + 2))
                for c in range(CPB):
                    last = nc.tensor.transpose(ps_kv[:, c * P:(c + 1) * P], kr[:, c], ident)
                last.then_inc(kt_ready, 1)

            def out_product(g, t):
                pe.wait_ge(zhi_done, g * 8 + (t + 1))
                pe.wait_ge(zlo_done, g * 8 + (t + 1))
                if t <= 1:
                    pe.wait_ge(wo_split, g + (t + 1))
                for h in range(GRP):
                    last = three_products(nc.tensor, ps_o[:], z_hi[:, h], z_lo[:, h],
                                          wo_hi[:, h], wo_lo[:, h], h == 0, h == GRP - 1)
                last.then_inc(o_ready, 1)

            def weights(m, k):
                return wmod[m][k] if m == GB else wmod[m][:, k]

            def mod_row(m):
                pe.wait_ge(mod_loaded[m], 16 * KT if m == GB else 16)
                for k in range(KT):
                    last = nc.tensor.matmul(ps_rows[m], silu_c[:, k * B:(k + 1) * B], weights(m, k),
                                            start=k == 0, stop=k == KT - 1)
                last.then_inc(rows_ready, 1)

            def mod_turn(dest, source, count):
                pe.wait_ge(rows_copied, count)
                for i in range(2):
                    for k in range(KT):
                        last = nc.tensor.transpose(dest[:, i, k], source[:, i, k * P:(k + 1) * P],
                                                   ident[0:B, 0:B])
                last.then_inc(mod_turned, 1)

            def softplus_argument():
                for i in range(2):
                    for k in range(KT):
                        cut = slice(i * HALF, (i + 1) * HALF)
                        last = three_products(nc.tensor, ps_zT[i][:], win_hi[:, k], win_lo[:, k],
                                              hT_hi[:, k, cut], hT_lo[:, k, cut], k == 0, k == KT - 1)
                    last.then_inc(zT_ready, 1)

            def softplus_turn():
                for t in range(NT):
                    if t % 4 == 0:
                        pe.wait_ge(zT_copied, t // 4 + 1)
                    last = nc.tensor.transpose(ps_z[:, t], zT[t // 4][:, t % 4 * P:(t % 4 + 1) * P],
                                               ident[0:H, 0:H])
                last.then_inc(z_ready, 1)

            def cumulative():
                pe.wait_ge(chain, CHAIN_G)
                pe.wait_ge(small_loaded, 64)

                def turned(i):
                    for t in range(4 * i, 4 * i + 4):
                        last = nc.tensor.matmul(ps_gT[i][0:H, t % 4 * P:(t % 4 + 1) * P], gdec[:, t],
                                                tri, start=True, stop=True)
                    last.then_inc(gT_ready, 1)

                turned(0)
                nc.tensor.matmul(ps_z, tri, gdec, start=True, stop=True)
                nc.tensor.matmul(ps_glast, ones[:].bitcast(F32), gdec, start=True, stop=True)\
                    .then_inc(cum_ready, 1)
                turned(1)

            pe.wait_ge(siluc_done, 3)
            mod_row(SA)
            mod_row(CA)
            pe.wait_ge(cst_loaded, 16)
            norm.tensor_turn(pe, 0)
            mod_turn(ps_modT, mod_rows, 2)
            for t in range(1, 6):
                norm.tensor_turn(pe, t)
            pe.wait_ge(norm.lo_done, CPB)
            kv_batch(0, -1)
            norm.tensor_turn(pe, 6)
            norm.tensor_turn(pe, 7)
            pe.wait_ge(norm.lo_done, NT // 2)
            q_block(0, -4, True)
            g_block(0, -4, 0, KT, True)
            k_turn(0, -1)
            pe.wait_ge(win_split, 2)
            pe.wait_ge(norm.lo_done, NT)
            softplus_argument()
            q_block(0, -3)
            softplus_turn()
            g_block(0, -3, 0, KT)
            q_block(0, -2)
            g_block(0, -2, 0, KT)
            pe.wait_ge(ones_done, 1)
            cumulative()
            q_block(0, -1)
            g_block(0, -1, 0, KT)

            def scores(g, t):
                b, c, half = t // 2, t % 2, t // 4
                pe.wait_ge(kT_done, g * 4 + (b + 1))
                pe.wait_ge(rope_done, g * 8 + (4 * half + 4))
                nc.tensor.matmul(ps_s[:].rearrange("p (h i) -> p h i", h=GRP),
                                 kT[:, b % 2, c * P:(c + 1) * P], qT[:, half, :, rows_of(t)],
                                 start=True, stop=True).then_inc(s_ready, 1)

            def y_product(g, t):
                b, c = t // 2, t % 2
                if c == 1:
                    pe.wait_ge(qe_done, g * 4 + (b + 1))
                    pe.wait_ge(state_done, g * 4 + (b + 1))
                    for h in range(GRP):
                        nc.tensor.matmul(ps_y[:, h * P:(h + 1) * P], state[:, h], qe[:, b % 2, h],
                                         start=h == 0, stop=False)
                pe.wait_ge(vlo_done, g * 4 + (b + 1))
                pe.wait_ge(plo_done, g * 8 + (t + 1))
                p_hi, p_lo = (p[:].rearrange("p h i -> p (h i)") for p in (prob_hi, prob_lo))
                three_products(nc.tensor, ps_y[:], v_hi[:, b % 2, c], v_lo[:, b % 2, c], p_hi, p_lo,
                               c == 0, True).then_inc(y_ready, 1)

            def chunk_state(g, b):
                pe.wait_ge(vw_done, g * 4 + (b + 1))
                nc.tensor.matmul(ps_st[:].rearrange("p (h e) -> p h e", h=GRP), kr[:, 0],
                                 vw[:], start=True, stop=True).then_inc(st_ready, 1)

            def square_sum(g, t):
                pe.wait_ge(sqhi_done, g * 8 + (t + 1))
                nc.tensor.matmul(ps_ss[:], ones[:], sq_hi[:], start=True, stop=False)
                pe.wait_ge(sqlo_done, g * 8 + (t + 1))
                nc.tensor.matmul(ps_ss[:], ones[:], sq_lo[:], start=False, stop=True)\
                    .then_inc(ss_ready, 1)

            def step(g, t, project, next_batch, next_group):
                b, c = t // 2, t % 2
                scores(g, t)
                if project:
                    q_block(g, t)
                out_product(g, t)
                if c == 1 and next_batch:
                    k_turn(g, b)
                y_product(g, t)
                if c == 0:
                    chunk_state(g, b)
                if project:
                    g_block(g, t, 0, KT - 1)
                square_sum(g, t)
                if project:
                    g_block(g, t, KT - 1, KT)
                if c == 0 and next_batch:
                    kv_batch(g, b)

            def tail(g, t):
                b, c = t // 2, t % 2
                if t == 4:
                    scores(g, t)
                    mod_row(GA)
                    out_product(g, t)
                if c == 1:
                    pe.wait_ge(prob_done, g * 8 + (t + 1))
                y_product(g, t)
                if c == 0:
                    chunk_state(g, b)
                    scores(g, t + 1)
                if t == 4:
                    kv_batch(g, b)
                else:
                    pe.wait_ge(lnss_done, g * 8 + t)
                if t == 5:
                    k_turn(g, b)
                    pe.wait_ge(guard, 2)
                    mod_row(CB)
                if t == 7:
                    mod_row(GB)
                square_sum(g, t)
                if t == 5:
                    scores(g, t + 1)
                if t > 4:
                    out_product(g, t)
                if t == 5:
                    mod_row(SB)
                if t == 7:
                    mod_turn(ps_late_modT, late_rows, 4)

            groups(pe, step, tail)
            out_product(KVH - 1, NT)

        @block.scalar
        def _(act):
            def swap(g, t, first=False):
                act.wait_ge(q_ready, g * 8 + (t + 5))
                if not first:
                    act.wait_ge(rope_done, g * 8 + (t + 4))
                nc.scalar.activation(q_sin[0:64], ps_q[64:128, :], ACT.Copy)
                nc.scalar.activation(q_sin[64:128], ps_q[0:64, :], ACT.Copy).then_inc(swap_done, 1)

            def exp_gate(g, t):
                act.wait_ge(g_ready, g * 8 + (t + 5))
                nc.scalar.activation(sig[:], ps_g[:], ACT.Exp, scale=-1.0).then_inc(esig_done, 1)

            def sigmoid(g, t):
                act.wait_ge(cap_done, g * 8 + (t + 5))
                nc.scalar.activation(sig[:], sig[:], ACT.Ln, bias=1.0).then_inc(lsig_done, 1)
                act.wait_ge(lsig_done, g * 8 + (t + 5))
                nc.scalar.activation(sig[:], sig[:], ACT.Exp, scale=-1.0).then_inc(sig_done, 1)

            def exp_g(g, b):
                par = (b + 1) % 2
                act.wait_ge(dec_loaded, g * 64 + 16 * (b + 2))
                nc.scalar.activation(qe[:, par], dec[:, par, :, 1], ACT.Exp).then_inc(expg_done, 1)

            def decays(g, t):
                bn, c = t // 2 % B, t % 2
                if c == 0:
                    act.wait_ge(mask_done, g * 4 + (t // 2 + 1))
                    act.wait_ge(scal_done, g * 4 + (t // 2 + 1))
                for h in range(GRP):
                    cell = dec[:, bn % 2, h, c]
                    last = nc.scalar.activation(cell, cell, ACT.Exp,
                                                bias=scal[:, bn * CPB + c, 0, h:h + 1])
                last.then_inc(dec_done, 1)

            def copy_v(g, b):
                act.wait_ge(kv_ready, g * 4 + (b + 2))
                if b >= 0:
                    act.wait_ge(vw_done, g * 4 + (b + 1))
                ps_v = ps_kv[:].rearrange("p (c d) -> p c d", c=CPB)[:, :, D:2 * D]
                nc.scalar.activation(v[:], ps_v, ACT.Copy)
                nc.scalar.activation(v_hi[:, (b + 1) % 2], ps_v, ACT.Copy).then_inc(v_done, 1)

            def copy_kT(g, b):
                act.wait_ge(kt_ready, g * 4 + (b + 2))
                nc.scalar.activation(kT[:, (b + 1) % 2], ps_kv[:, 0:CPB * P], ACT.Copy)\
                    .then_inc(kT_done, 1)

            nc.scalar.preload_act_table_set("natural_log_exp_and_others")
            act.dma_start(ident, cst_in[:, C_ID:C_COST]).then_inc(cst_loaded, 16)
            act.dma_start(tri, cst_in[:, C_TRI:C_END]).then_inc(small_loaded, 16)
            act.dma_start(win, win_in).then_inc(small_loaded, 16)
            act.dma_start(rows, rows_in.partition_broadcast(P)).then_inc(small_loaded, 16)
            act.dma_start(gnorm[:], gnorm_in).then_inc(small_loaded, 16)
            act.wait_ge(c_loaded, 16)
            nc.scalar.activation(sig_c, cT, ACT.Exp, scale=-1.0).then_inc(sigc_done, 1)
            norm.scalar_rstd(act, 0)
            for i, m in enumerate((SA, CA)):
                act.wait_ge(rows_ready, i + 1)
                nc.scalar.activation(mod_rows[:, i], ps_rows[m], ACT.Copy).then_inc(rows_copied, 1)
            act.wait_ge(small_loaded, 64)
            nc.scalar.activation(rate, rows[:, 1], ACT.Exp).then_inc(rate_done, 1)
            act.wait_ge(modT_done, 2)
            for t in range(NT):
                if t == 1:
                    norm.scalar_rstd(act, 1)
                norm.scalar_modulate(act, t)
            for t in range(-4, 0):
                if t == -4:
                    copy_v(0, -1)
                swap(0, t, t == -4)
                if t == -1:
                    exp_g(0, -1)
                exp_gate(0, t)
                if t == -2:
                    for i in range(2):
                        act.wait_ge(gT_ready, i + 1)
                        nc.scalar.activation(gT[i], ps_gT[i][0:H], ACT.Copy).then_inc(gT_copied, 1)
                        if i == 0:
                            act.wait_ge(cum_ready, 1)
                            nc.scalar.activation(tok[:, :, 0], ps_z, ACT.Copy, scale=-1.0)\
                                .then_inc(exp_done, 1)
                if t == -1:
                    decays(0, 0)
                sigmoid(0, t)
                if t == -4:
                    copy_kT(0, -1)
                    for i in range(2):
                        act.wait_ge(zT_ready, i + 1)
                        nc.scalar.activation(zT[i], ps_zT[i][0:H], ACT.Copy).then_inc(zT_copied, 1)
                    act.wait_ge(chain, CHAIN_ABS)
                    nc.scalar.activation(za, za, ACT.Exp, scale=-1.0).then_inc(exp_done, 1)
                if t == -2:
                    act.wait_ge(chain, CHAIN_DIFF)
                    nc.scalar.activation(zs, zs, ACT.Exp).then_inc(exp_done, 1)
            act.wait_ge(gT_stored, 32)
            act.wait_ge(ones_done, 1)

            def squares(g, t, tail=False):
                if tail:
                    act.wait_ge(zlo_done, g * 8 + (t + 1))
                act.wait_ge(y_ready, g * 8 + (t + 1))
                nc.scalar.activation(sq, ps_y[:], ACT.Square).then_inc(sq_done, 1)
                nc.scalar.activation(sq_hi[:], ps_y[:], ACT.Square).then_inc(sqhi_done, 1)

            def copy_state(g, b):
                act.wait_ge(st_ready, g * 4 + (b + 1))
                nc.scalar.activation(state[:].rearrange("p h e -> p (h e)"), ps_st[:], ACT.Copy)\
                    .then_inc(state_done, 1)

            def inverse_rms(g, t):
                act.wait_ge(ss_ready, g * 8 + (t + 1))
                nc.scalar.activation(rms[:], ps_ss[:], ACT.Ln, bias=eps_col[:], scale=1.0 / D)\
                    .then_inc(lnss_done, 1)
                act.wait_ge(lnss_done, g * 8 + (t + 1))
                nc.scalar.activation(rms[:], rms[:], ACT.Exp, scale=-0.5).then_inc(rms_done, 1)

            def split_prob_hi(g, t):
                act.wait_ge(prob_done, g * 8 + (t + 1))
                nc.scalar.activation(prob_hi[:], prob[:], ACT.Copy).then_inc(phi_done, 1)

            def split_z_hi(g, t):
                act.wait_ge(z_done, g * 8 + (t + 1))
                nc.scalar.activation(z_hi[:], z[:], ACT.Copy).then_inc(zhi_done, 1)

            def step(g, t, project, next_batch, next_group):
                b, c = t // 2, t % 2
                split_prob_hi(g, t)
                swap(g, t)
                squares(g, t)
                if c == 0:
                    copy_state(g, b)
                else:
                    copy_kT(g, b)
                decays(g, t + 1)
                inverse_rms(g, t)
                exp_gate(g, t)
                split_z_hi(g, t)
                sigmoid(g, t)
                if c == 0:
                    copy_v(g, b)
                    exp_g(g, b)

            def tail(g, t):
                b, c = t // 2, t % 2
                if c == 0:
                    decays(g, t + 1)
                squares(g, t, True)
                if t == 5:
                    copy_kT(g, b)
                    decays(g, t + 1)
                if c == 0:
                    copy_state(g, b)
                if t == 4:
                    copy_v(g, b)
                    exp_g(g, b)
                inverse_rms(g, t)
                act.wait_ge(o_ready, g * 8 + (t + 1))
                split_z_hi(g, t)
                if t == 6:
                    for i, m in enumerate((CB, SB)):
                        act.wait_ge(rows_ready, 4 + i)
                        nc.scalar.activation(late_rows[:, 1 - i], ps_rows[m], ACT.Copy)\
                            .then_inc(rows_copied, 1)

            groups(act, step, tail)
            norm2.scalar_rstd(act, 0)
            norm2.scalar_rstd(act, 1)

        @block.vector
        def _(dve):
            def split_head_hi(g, j):
                dve.wait_ge(wh_loaded, g * 128 + 32 * (j + 1))
                split_hi(nc.vector, wq_hi[:, j], raw_q[:])
                split_hi(nc.vector, wg_hi[:, j], raw_g[:]).then_inc(wh_hi_done, 1)

            def split_head_lo_g(g, j):
                dve.wait_ge(wh_hi_done, g * 4 + (j + 1))
                split_lo(nc.vector, wg_lo[:, j], raw_g[:], wg_hi[:, j])

            def split_head_lo_q(g, j):
                split_lo(nc.vector, wq_lo[:, j], raw_q[:], wq_hi[:, j]).then_inc(wh_split, 1)

            def split_head(g, j):
                split_head_hi(g, j)
                split_head_lo_g(g, j)
                split_head_lo_q(g, j)

            def split_kv_hi(g):
                dve.wait_ge(kv_loaded, g * 16 + 16)
                split_hi(nc.vector, wkv_hi[:], raw_kv[:]).then_inc(kv_hi_done, 1)

            def split_kv_lo(g):
                dve.wait_ge(kv_hi_done, g + 1)
                split_lo(nc.vector, wkv_lo[:], raw_kv[:], wkv_hi[:]).then_inc(kv_split, 1)

            def split_o_hi(g):
                dve.wait_ge(wo_loaded, g * 16 + 16)
                split_hi(nc.vector, wo_hi[:], raw_o[:]).then_inc(wo_hi_done, 1)

            def split_o_lo(g):
                dve.wait_ge(wo_hi_done, g + 1)
                split_lo(nc.vector, wo_lo[:], raw_o[:], wo_hi[:]).then_inc(wo_split, 1)

            def copy_scalars(g, b, first=False):
                t0 = (b + 1) % B * CPB
                if first:
                    dve.wait_ge(chain, CHAIN_END)
                nc.vector.tensor_copy(scal[:, t0:t0 + CPB],
                                      tok[:, t0:t0 + CPB, :, group_slice(g, b, GRP)])\
                    .then_inc(scal_done, 1)

            def rotate_k(g, b, t=0):
                ps_k = ps_kv[:].rearrange("p (c d) -> p c d", c=CPB)
                dve.wait_ge(v_done, g * 4 + (b + 2))
                if b >= 0:
                    dve.wait_ge(rope_done, g * 8 + min(t + 4, NT))
                nc.vector.tensor_tensor(k_cos, ps_k[:, :, 0:D], cos_k, ALU.mult)
                nc.vector.tensor_tensor(k_sin[:, :, 0:64], ps_k[:, :, 64:128], sin_k[:, :, 0:64],
                                        ALU.mult)
                nc.vector.tensor_tensor(k_sin[:, :, 64:128], ps_k[:, :, 0:64], sin_k[:, :, 64:128],
                                        ALU.mult).then_inc(kparts_done, 1)
                dve.wait_ge(kparts_done, g * 4 + (b + 2))
                nc.vector.tensor_tensor(kr[:], k_cos, k_sin, ALU.add)\
                    .then_inc(kr_done, 1)

            def rotate_q_cos(g, t):
                if t % 2 == 1 or t == -4:
                    dve.wait_ge(kr_done, g * 4 + (max(t, -2) // 2 + 2))
                dve.wait_ge(swap_done, g * 8 + (t + 5))
                nc.vector.tensor_tensor(q_cos[:].rearrange("p (b i) -> p b i", b=2),
                                        ps_q[:].rearrange("p (b i) -> p b i", b=2), cosT, ALU.mult)\
                    .then_inc(qcos_done, 1)

            def rotate_q_add(g, t):
                half, j = (t // 4 + 1) % 2, t % 4
                dve.wait_ge(qcos_done, g * 8 + (t + 5))
                dve.wait_ge(qsin_done, g * 8 + (t + 5))
                nc.vector.tensor_tensor(qT[:, half, j], q_cos[:], q_sin[:], ALU.add)\
                    .then_inc(rope_done, 1)

            def cap(g, t):
                dve.wait_ge(esig_done, g * 8 + (t + 5))
                nc.vector.tensor_scalar(sig[:], sig[:], EXP_CAP, None, ALU.min).then_inc(cap_done, 1)

            def gate(g, t):
                half, j = (t // 4 + 1) % 2, t % 4
                dve.wait_ge(sig_done, g * 8 + (t + 5))
                nc.vector.scalar_tensor_tensor(sg[:, half, j], ps_g[:], gnorm[:], sig[:],
                                               ALU.mult, ALU.mult).then_inc(sg_done, 1)

            def add_out(g, t):
                dve.wait_ge(o_ready, g * 8 + (t + 1))
                nc.vector.tensor_tensor(x1[:, (t - 1) % NT], x1[:, (t - 1) % NT], ps_o[:], ALU.add)\
                    .then_inc(sums_done, 1)

            def softplus_before_exp():
                dve.wait_ge(z_ready, 1)
                nc.vector.tensor_tensor(z1, ps_z, rows[:, 0].unsqueeze(1).broadcast_to([P, NT, H]),
                                        ALU.add).then_inc(chain, 1)
                dve.wait_ge(chain, 1)
                nc.vector.tensor_scalar(za, z1, -1.0, None, ALU.mult).then_inc(chain, 1)
                dve.wait_ge(chain, 2)
                nc.vector.tensor_tensor(za, za, z1, ALU.max).then_inc(chain, 1)

            def softplus_argument_of_series():
                dve.wait_ge(exp_done, 1)
                nc.vector.tensor_scalar(zs2, za, 2.0, None, ALU.add).then_inc(chain, 1)
                dve.wait_ge(chain, CHAIN_ABS + 1)
                nc.vector.reciprocal(zs, zs2).then_inc(chain, 1)
                dve.wait_ge(chain, CHAIN_ABS + 2)
                nc.vector.tensor_tensor(zs, zs, za, ALU.mult).then_inc(chain, 1)
                dve.wait_ge(chain, CHAIN_ABS + 3)
                nc.vector.tensor_tensor(zs2, zs, zs, ALU.mult).then_inc(chain, 1)

            def softplus_series(part):
                if part == 0:
                    dve.wait_ge(chain, CHAIN_SQUARE)
                    nc.vector.tensor_scalar(zq, zs2, 1.0 / 15, None, ALU.mult).then_inc(chain, 1)
                    dve.wait_ge(chain, CHAIN_SQUARE + 1)
                for n in range(INNER) if part == 0 else range(INNER, len(SERIES)):
                    odd = SERIES[n]
                    nc.vector.scalar_tensor_tensor(zq, zq, 1.0 / odd, zs2, ALU.add, ALU.mult)\
                        .then_inc(chain, 1)
                    dve.wait_ge(chain, CHAIN_SQUARE + 2 + n)

            def decay_rates():
                nc.vector.scalar_tensor_tensor(zq, zq, 1.0, zs, ALU.add, ALU.mult).then_inc(chain, 1)
                nc.vector.tensor_scalar(z1, z1, 0.0, None, ALU.max).then_inc(chain, 1)
                dve.wait_ge(chain, CHAIN_G - 2)
                nc.vector.scalar_tensor_tensor(tok[:, :, 1], zq, 2.0, z1, ALU.mult, ALU.add)\
                    .then_inc(chain, 1)
                dve.wait_ge(chain, CHAIN_G - 1)
                dve.wait_ge(rate_done, 1)
                nc.vector.scalar_tensor_tensor(gdec, tok[:, :, 1], -1.0,
                                               rate.unsqueeze(1).broadcast_to([P, NT, H]),
                                               ALU.mult, ALU.mult).then_inc(chain, 1)

            def chunk_end():
                dve.wait_ge(cum_ready, 1)
                dve.wait_ge(exp_done, 2)
                nc.vector.tensor_tensor(zs, ps_glast, tok[:, :, 0], ALU.add).then_inc(chain, 1)

            def state_weight():
                dve.wait_ge(exp_done, 3)
                nc.vector.tensor_tensor(tok[:, :, 2], zs, tok[:, :, 1], ALU.mult).then_inc(chain, 1)

            def guard_gate(i):
                row = ps_rows[(GA, GB)[i]]
                dve.wait_ge(rows_ready, 3 if i == 0 else 6)
                if i == 0:
                    dve.wait_ge(rope_done, H * 2)
                else:
                    dve.wait_ge(guard, GUARD_END)
                nc.vector.tensor_scalar(gmag, row, -1.0, None, ALU.mult).then_inc(guard, 1)
                dve.wait_ge(guard, GUARD_END * i + 1)
                nc.vector.tensor_tensor(gmag, gmag, row, ALU.max)
                nc.vector.tensor_scalar(gates[i], row, 0.0, 2.0, ALU.is_ge, ALU.mult).then_inc(guard, 1)
                dve.wait_ge(guard, GUARD_END * i + 2)
                nc.vector.tensor_scalar(gates[i], gates[i], -1.0, None, ALU.add).then_inc(guard, 1)
                dve.wait_ge(guard, GUARD_END * i + 3)
                nc.vector.scalar_tensor_tensor(gates[i], gmag, 0.25, gates[i], ALU.max, ALU.mult)\
                    .then_inc(guard, 1)

            dve.wait_ge(sigc_done, 1)
            nc.vector.tensor_scalar(sig_c, sig_c, 1.0, None, ALU.add).then_inc(siluc_done, 1)
            dve.wait_ge(siluc_done, 1)
            nc.vector.reciprocal(silu_c[:], sig_c).then_inc(siluc_done, 1)
            dve.wait_ge(siluc_done, 2)
            nc.vector.tensor_tensor(silu_c[:], silu_c[:], cT, ALU.mult).then_inc(siluc_done, 1)
            dve.wait_ge(x_loaded[0], 16)
            for t in range(4):
                norm.vector_stats(dve, t)
            norm.vector_var(dve, 0)
            for t in range(4):
                norm.vector_normalise(dve, t)
            dve.wait_ge(x_loaded[1], 16)
            norm.vector_stats(dve, 4)
            norm.vector_stats(dve, 5)
            dve.wait_ge(mod_turned, 1)
            nc.vector.tensor_copy(modT[:, 0], ps_modT[:, 0]).then_inc(modT_done, 1)
            nc.vector.tensor_scalar(modT[:, 1], ps_modT[:, 1], 1.0, None, ALU.add).then_inc(modT_done, 1)
            norm.vector_stats(dve, 6)
            norm.vector_stats(dve, 7)
            norm.vector_var(dve, 1)
            norm.vector_split(dve, 0, False)
            split_kv_hi(0)
            split_kv_lo(0)
            norm.vector_split(dve, 1, False)
            norm.vector_normalise(dve, 4)
            norm.vector_normalise(dve, 5)
            norm.vector_split(dve, 2, False)
            norm.vector_normalise(dve, 6)
            norm.vector_normalise(dve, 7)
            norm.vector_split(dve, 3, False)
            split_head(0, 0)
            for t in range(4, NT):
                norm.vector_split(dve, t, False)
                if t == 4:
                    dve.wait_ge(small_loaded, 64)
                    split_hi(nc.vector, win_hi, win).then_inc(win_split, 1)
                    dve.wait_ge(win_split, 1)
                    split_lo(nc.vector, win_lo, win, win_hi).then_inc(win_split, 1)
            dve.wait_ge(tables_loaded, 16)
            dve.wait_ge(win_split, 2)
            rotate_k(0, -1)
            for t in range(-4, 0):
                rotate_q_cos(0, t)
                if t == -4:
                    rotate_q_add(0, t)
                    split_head(0, 1)
                if t == -3:
                    softplus_argument_of_series()
                    rotate_q_add(0, t)
                if t == -1:
                    dve.wait_ge(expg_done, 1)
                    dve.wait_ge(future_done, 2)
                    cells = dec[:, 0].rearrange("p h c i -> p (h c) i")
                    nc.vector.tensor_tensor(cells, cells,
                                            future[:].unsqueeze(1).broadcast_to([P, GRP * CPB, CHUNK]),
                                            ALU.add).then_inc(mask_done, 1)
                    state_weight()
                    copy_scalars(0, -1, True)
                if t >= -2:
                    rotate_q_add(0, t)
                cap(0, t)
                if t == -3:
                    softplus_series(0)
                if t < -1:
                    gate(0, t)
                if t == -4:
                    split_head(0, 2)
                    softplus_before_exp()
                if t == -3:
                    softplus_series(1)
                    decay_rates()
                    split_head(0, 3)
                if t == -2:
                    chunk_end()
            dve.wait_ge(zeros_done, 1)

            def probabilities(g, t, tail=False):
                b, c = t // 2, t % 2
                early = tail and t > 4
                dest = prob_tail if tail else prob
                if early:
                    dve.wait_ge(plo_done, g * 8 + t)
                elif tail:
                    dve.wait_ge(sg_done, g * 8 + 8)
                else:
                    dve.wait_ge(zlo_done, g * 8 + (t + 1))
                dve.wait_ge(s_ready, g * 8 + (t + 1))
                dve.wait_ge(dec_done, g * 8 + (t + 1))
                for h in range(GRP):
                    last = nc.vector.scalar_tensor_tensor(
                        dest[:, h], ps_s[:, h * P:(h + 1) * P], scal[:, t, 1, h:h + 1],
                        dec[:, b % 2, h, c], ALU.mult, ALU.mult)
                last.then_inc(prob_done, 1)

            def split_prob_lo(g, t, tail=False):
                if tail:
                    dve.wait_ge(prob_done, g * 8 + (t + 1))
                    split_hi(nc.vector, prob_hi[:], prob_tail).then_inc(phi_done, 1)
                dve.wait_ge(phi_done, g * 8 + (t + 1))
                split_lo(nc.vector, prob_lo[:], prob_tail if tail else prob[:], prob_hi[:])\
                    .then_inc(plo_done, 1)

            def gated_y(g, t):
                half = t // 4
                dve.wait_ge(sqhi_done, g * 8 + (t + 1))
                split_lo(nc.vector, sq_lo[:], sq, sq_hi[:]).then_inc(sqlo_done, 1)
                dve.wait_ge(sqlo_done, g * 8 + (t + 1))
                dve.wait_ge(sg_done, g * 8 + (4 * half + 4))
                nc.vector.tensor_tensor(z[:], ps_y[:].rearrange("p (h i) -> p h i", h=GRP),
                                        sg[:, half, :, rows_of(t)], ALU.mult).then_inc(zz_done, 1)

            def normed_z(g, t):
                dve.wait_ge(zz_done, g * 8 + (t + 1))
                dve.wait_ge(rms_done, g * 8 + (t + 1))
                nc.vector.tensor_tensor(z[:], z[:], rms[:].rearrange("p (h i) -> p h i", h=GRP),
                                        ALU.mult).then_inc(z_done, 1)

            def split_z_lo(g, t):
                dve.wait_ge(zhi_done, g * 8 + (t + 2))
                split_lo(nc.vector, z_lo[:], z[:], z_hi[:]).then_inc(zlo_done, 1)

            def step(g, t, project, next_batch, next_group):
                b, c = t // 2, t % 2
                heads, keys = next_group and 1 <= t <= GRP, next_group and t == GRP + 1
                probabilities(g, t)
                if c == 1:
                    rotate_k(g, b, t)
                gate(g, t - 1)
                split_prob_lo(g, t)
                rotate_q_cos(g, t)
                if heads:
                    split_head_hi(g + 1, t - 1)
                if keys:
                    split_kv_hi(g + 1)
                rotate_q_add(g, t)
                add_out(g, t)
                gated_y(g, t)
                if heads:
                    split_head_lo_g(g + 1, t - 1)
                if keys:
                    split_kv_lo(g + 1)
                if c == 0:
                    copy_scalars(g, b)
                if t == 0:
                    split_o_hi(g)
                normed_z(g, t)
                cap(g, t)
                if heads:
                    split_head_lo_q(g + 1, t - 1)
                split_z_lo(g, t)
                if t == 0:
                    split_o_lo(g)

            def tail(g, t):
                b, c = t // 2, t % 2
                if t == 4:
                    gate(g, t - 1)
                    probabilities(g, t, True)
                    split_prob_lo(g, t, True)
                    add_out(g, t)
                    guard_gate(0)
                gated_y(g, t)
                if t == 4:
                    copy_scalars(g, b)
                if t < NT - 1 and t != 5:
                    probabilities(g, t + 1, True)
                    split_prob_lo(g, t + 1, True)
                if t == 4:
                    dve.wait_ge(guard, GUARD_END)
                    rotate_k(g, b, t)
                if t == 7:
                    guard_gate(1)
                normed_z(g, t)
                if t > 4:
                    add_out(g, t)
                split_z_lo(g, t)
                if t == 5:
                    probabilities(g, t + 1, True)
                    split_prob_lo(g, t + 1, True)
                if t == 6:
                    for tile in range(3):
                        stats_of(tile)
                if t == 7:
                    stats_of(3)
                    norm2.vector_var(dve, 0)
                    stats_of(4)
                    stats_of(5)

            def stats_of(tile):
                if tile < POOL_TILES:
                    dve.wait_ge(residual[0], tile + 1)
                else:
                    dve.wait_ge(residual[1], tile - POOL_TILES + 1)
                norm2.vector_stats(dve, tile)

            groups(dve, step, tail)
            dve.wait_ge(ga_loaded, 16)
            dve.wait_ge(mod_turned, 2)
            nc.vector.tensor_copy(modT[:, 2], ps_late_modT[:, 0])
            nc.vector.tensor_scalar(modT[:, 3], ps_late_modT[:, 1], 1.0, None, ALU.add)
            stats_of(NT - 2)
            add_out(KVH - 1, NT)
            dve.wait_ge(sums_done, KVH * NT + 1)
            scale_sum(nc.vector, 1, NT - 1)
            add_x(nc.vector, dve, 1, NT - 1, 0)
            stats_of(NT - 1)
            norm2.vector_var(dve, 1)

        @block.gpsimd
        def _(pool):
            def mask(g, b):
                cells = dec[:, (b + 1) % 2].rearrange("p h c i -> p (h c) i")
                pool.wait_ge(expg_done, g * 4 + (b + 2))
                nc.gpsimd.tensor_tensor(cells, cells,
                                        future[:].unsqueeze(1).broadcast_to([P, GRP * CPB, CHUNK]),
                                        ALU.add).then_inc(mask_done, 1)

            def rotate_q_sin(g, t):
                pool.wait_ge(swap_done, g * 8 + (t + 5))
                q2 = q_sin[:].rearrange("p (b i) -> p b i", b=2)
                nc.gpsimd.tensor_tensor(q2, q2, sinT, ALU.mult).then_inc(qsin_done, 1)

            def weigh_v(g, b):
                bn = (b + 1) % B
                pool.wait_ge(v_done, g * 4 + (b + 2))
                split_lo(nc.gpsimd, v_lo[:, bn % 2], v[:], v_hi[:, bn % 2]).then_inc(vlo_done, 1)
                pool.wait_ge(scal_done, g * 4 + (b + 2))
                nc.gpsimd.tensor_tensor(
                    vw[:], v[:, 0].unsqueeze(1).broadcast_to([P, GRP, D]),
                    scal[:, bn * CPB, 2].unsqueeze(2).broadcast_to([P, GRP, D]), ALU.mult)\
                    .then_inc(vw_done, 1)

            def weigh_q(g, b):
                bn = (b + 1) % B
                pool.wait_ge(rope_done, g * 8 + (4 * ((b + 1) // 2) + 4))
                at = (bn % 2 * CPB + 1) * P
                nc.gpsimd.tensor_tensor(qe[:, bn % 2], qe[:, bn % 2], qT[:, bn // 2, :, at:at + P],
                                        ALU.mult).then_inc(qe_done, 1)

            nc.gpsimd.memset(eps_col[:], EPS)
            nc.gpsimd.memset(future[:], 0.0).then_inc(future_done, 1)
            nc.gpsimd.memset(ones[:].bitcast(F32), 1.0).then_inc(ones_done, 1)
            nc.gpsimd.memset(wo_hi[:].bitcast(F32), 0.0)
            nc.gpsimd.memset(wo_lo[:].bitcast(F32), 0.0).then_inc(wo_split, 1)
            nc.gpsimd.memset(z_hi[:].bitcast(F32), 0.0).then_inc(zhi_done, 1)
            nc.gpsimd.memset(z_lo[:].bitcast(F32), 0.0).then_inc(zlo_done, 1)
            pool.wait_ge(future_done, 1)
            nc.gpsimd.affine_select(out=future[:], in_=future[:], compare_op=ALU.is_ge, fill=MASKED,
                                    base=0, pattern=[[1, CHUNK]], channel_multiplier=-1)\
                .then_inc(future_done, 1)
            for t in range(NT):
                norm.pool_split_lo(pool, t)
            pool.wait_ge(tables_loaded, 16)
            for t in range(-4, 0):
                rotate_q_sin(0, t)
                if t == -4:
                    pool.wait_ge(norm.turned, NT)
                    nc.gpsimd.memset(x1[:], 0.0).then_inc(zeros_done, 1)
            weigh_v(0, -1)
            weigh_q(0, -1)

            def step(g, t, project, next_batch, next_group):
                b, c = t // 2, t % 2
                if project:
                    rotate_q_sin(g, t)
                if c == 1 and next_batch:
                    weigh_v(g, b)
                    weigh_q(g, b)
                if c == 0 and next_batch:
                    mask(g, b)

            def tail(g, t):
                if t < NT - 2:
                    step(g, t, False, True, False)

            groups(pool, step, tail)
            def scale_tile(t):
                pool.wait_ge(sums_done, KVH * NT - (NT - 1) + t + 1)
                scale_sum(nc.gpsimd, 0, t)

            pool.wait_ge(ga_loaded, 16)
            for t in range(5):
                scale_tile(t)
            for t in range(4):
                add_x(nc.gpsimd, pool, 0, t, t)
            scale_tile(5)
            add_x(nc.gpsimd, pool, 0, 4, 4)
            add_x(nc.gpsimd, pool, 0, 5, 5)
            scale_tile(6)
            add_x(nc.gpsimd, pool, 0, 6, 6)


def block_ffn(nc, x1, hT_hi, hT_lo, modT, ident, modrow, wgu_in, wd_in, out, norm_rows,
              raw_pair):
    with ExitStack() as both:
        def sb2(name, shape, dt=F32):
            return both.enter_context(nc.sbuf_tensor(name, shape, dt))

        a_hi, a_lo = sb2("a_hi", [P, IT, B * L], F32R), sb2("a_lo", [P, IT, B * L], F32R)
        EARLY, MORE = 4, 4
        raw_d = sb2("raw_d", [P, EARLY, HID])
        raw_gu = sb2("raw_gu", [P, KT, 2 * P])
        d0_hi, d0_lo = sb2("d0_hi", [P, HID], F32R), sb2("d0_lo", [P, HID], F32R)
        grow = sb2("grow", [P, B, HID])
        d_loaded = both.enter_context(nc.semaphore("d_loaded"))
        dm_loaded = both.enter_context(nc.semaphore("dm_loaded"))
        gb_loaded = both.enter_context(nc.semaphore("gb_loaded"))

        with ExitStack() as ctx:
            def sb(name, shape, dt=F32):
                return ctx.enter_context(nc.sbuf_tensor(name, shape, dt))

            def sem(name):
                return ctx.enter_context(nc.semaphore(name))

            raw = [raw_pair, raw_gu]
            w_hi, w_lo = sb("wgu_hi", [P, 2, KT, 2 * P], F32R), sb("wgu_lo", [P, 2, KT, 2 * P], F32R)
            prod = sb("prod", [P, 2, HALF])
            norm = Norm(ctx, nc, "2b", norm_rows, x1, hT_hi, hT_lo, modT[:, 2], modT[:, 3], ident,
                        [ctx.enter_context(nc.psum_tensor(f"ps_ln{i}", [P, HID], F32))
                         for i in range(4)], False, sb("hf", [P, 3, KT, P]), True)
            ps_g = [ctx.enter_context(nc.psum_tensor(f"ps_fg{i}", [P, HALF], F32)) for i in range(2)]
            ps_u = [ctx.enter_context(nc.psum_tensor(f"ps_fu{i}", [P, HALF], F32)) for i in range(2)]
            w_loaded = [sem(f"wgu_loaded{i}") for i in range(2)]
            d0_done = sem("d0_done")
            whi_done = sem("whi_done")
            w_split = sem("w_split")
            gate_ready = sem("gate_ready")
            up_ready = sem("up_ready")
            silu_done = sem("silu_done")
            prod_done = sem("prod_done")
            ahi_done = sem("ahi_done")
            alo_done = sem("alo_done")
            block = ctx.enter_context(nc.Block())

            def inner_tiles(engine, step):
                step(0, 0, 0, True, True)
                with engine.Fori(0, (IT - 3) // 2) as i:
                    step(i, 2, 1, True, True)
                    step(i, 2, 2, True, True)
                step(0, 0, IT - 2, False, True)
                step(0, 0, IT - 1, False, False)

            @block.gpsimd
            def _(pool):
                pool.wait_ge(whi_done, 1)
                split_lo(nc.gpsimd, w_lo[:, 0], raw[0][:], w_hi[:, 0]).then_inc(w_split, 1)

            @block.sync
            def _(sp):
                def load_w(i, per, k, parity):
                    sp.dma_start(raw[parity][:], wgu_in[bass.ds(i * per + k, 1)]
                                 .rearrange("o p k n -> (o p) k n")).then_inc(w_loaded[parity], 16)

                load_w(0, 0, 1, 1)
                sp.dma_start(grow[:].rearrange("p b n -> p (b n)"), modrow[1].partition_broadcast(P))\
                    .then_inc(gb_loaded, 16)
                sp.dma_start(raw_d[:], wd_in[0:EARLY].rearrange("k p n -> p k n")).then_inc(d_loaded, 16)

                def step(i, per, k, prefetch, next_split):
                    if prefetch:
                        sp.wait_ge(w_split, i * per + (k + 1))
                        load_w(i, per, k + 2, k % 2)

                inner_tiles(sp, step)
                sp.wait_ge(w_split, IT - 1)
                for i, dest in enumerate((raw_gu, raw_pair)):
                    if i == 1:
                        sp.wait_ge(w_split, IT)
                    at = EARLY + 2 * i
                    sp.dma_start(dest[:].rearrange("p (m k) n -> p m (k n)", m=2),
                                 wd_in[at:at + 2].rearrange("k p n -> p k n")).then_inc(dm_loaded, 16)

            @block.tensor
            def _(pe):
                for t in range(NT - 4):
                    norm.tensor_turn(pe, t)

                def product(bank, s, half, u, done, part=0, parts=1):
                    size = HALF // parts
                    at = half * HALF + part * size
                    for k in range(KT):
                        cut = slice(at, at + size)
                        cols = slice(u * P, (u + 1) * P)
                        last = three_products(nc.tensor, bank[:, part * size:(part + 1) * size],
                                              w_hi[:, s, k, cols], w_lo[:, s, k, cols],
                                              hT_hi[:, k, cut], hT_lo[:, k, cut], k == 0, k == KT - 1)
                    if part == parts - 1:
                        last.then_inc(done, 1)

                def step(i, per, k, prefetch, next_split):
                    pe.wait_ge(w_split, i * per + (k + 1))
                    for half in range(2):
                        if k == 0:
                            for part in range(2):
                                pe.wait_ge(norm.lo_done, 4 * half + 2 * (part + 1))
                                for u, (bank, done) in enumerate(((ps_g, gate_ready), (ps_u, up_ready))):
                                    if half == 0:
                                        norm.tensor_turn(pe, NT // 2 + 2 * part + u)
                                    product(bank[half], 0, half, u, done, part, 2)
                            continue
                        pe.wait_ge(prod_done, i * (2 * per) + (2 * k - 1 + half))
                        product(ps_g[half], k % 2, half, 0, gate_ready)
                        product(ps_u[half], k % 2, half, 1, up_ready)

                inner_tiles(pe, step)

            @block.scalar
            def _(act):
                for t in range(NT):
                    norm.scalar_modulate(act, t)

                def step(i, per, k, prefetch, next_split):
                    for half in range(2):
                        at = i * (2 * per) + (2 * k + half + 1)
                        if k > 0:
                            act.wait_ge(alo_done, i * (2 * per) + (2 * k - 1 + half))
                        act.wait_ge(gate_ready, at)
                        nc.scalar.activation(prod[:, half], ps_g[half][:], ACT.Silu)\
                            .then_inc(silu_done, 1)
                        act.wait_ge(prod_done, at)
                        nc.scalar.activation(
                            a_hi[:, bass.ds(i * per + k, 1), half * HALF:(half + 1) * HALF],
                            prod[:, half].unsqueeze(1), ACT.Copy).then_inc(ahi_done, 1)

                inner_tiles(act, step)

            @block.vector
            def _(dve):
                def split_w(i, per, k):
                    s = k % 2
                    dve.wait_ge(w_loaded[s], i * (8 * per) + 16 * (k // 2 + s))
                    split_hi(nc.vector, w_hi[:, s], raw[s][:]).then_inc(whi_done, 1)
                    dve.wait_ge(whi_done, i * per + (k + 1))
                    split_lo(nc.vector, w_lo[:, s], raw[s][:], w_hi[:, s]).then_inc(w_split, 1)

                for t in range(4):
                    norm.vector_normalise(dve, t)
                split_hi(nc.vector, w_hi[:, 0], raw[0][:]).then_inc(whi_done, 1)
                for t in range(NT):
                    norm.vector_split(dve, t)
                    if t + 4 < NT:
                        norm.vector_normalise(dve, t + 4)

                def step(i, per, k, prefetch, next_split):
                    if next_split:
                        split_w(i, per, k + 1)
                    for half in range(2):
                        at = i * (2 * per) + (2 * k + half + 1)
                        dve.wait_ge(silu_done, at)
                        dve.wait_ge(up_ready, at)
                        nc.vector.tensor_tensor(prod[:, half], ps_u[half][:], prod[:, half], ALU.mult)\
                            .then_inc(prod_done, 1)
                        dve.wait_ge(ahi_done, at)
                        cut = slice(half * HALF, (half + 1) * HALF)
                        split_lo(nc.vector, a_lo[:, bass.ds(i * per + k, 1), cut],
                                 prod[:, half].unsqueeze(1),
                                 a_hi[:, bass.ds(i * per + k, 1), cut]).then_inc(alo_done, 1)

                inner_tiles(dve, step)
                dve.wait_ge(d_loaded, 16)
                split_hi(nc.vector, d0_hi[:], raw_d[:, 0]).then_inc(d0_done, 1)
                dve.wait_ge(d0_done, 1)
                split_lo(nc.vector, d0_lo[:], raw_d[:, 0], d0_hi[:])

        with ExitStack() as ctx:
            def sb(name, shape, dt=F32):
                return ctx.enter_context(nc.sbuf_tensor(name, shape, dt))

            def sem(name):
                return ctx.enter_context(nc.semaphore(name))

            OLD = KT * B * L // HID
            old_hi, old_lo = (h[:].rearrange("p k (m n) -> p (k m) n", n=HID) for h in (hT_hi, hT_lo))
            new_hi, new_lo = (sb(n, [P, IT - OLD - 1, HID], F32R) for n in ("d_hi", "d_lo"))
            raw_d2 = sb("raw_d2", [P, IT - EARLY - MORE, HID])
            res = sb("res", [P, 2, HID])
            ps_d = [ctx.enter_context(nc.psum_tensor(f"ps_d{i}", [P, HID], F32)) for i in range(2)]
            d2_loaded = sem("d2_loaded")
            dhi_done = sem("dhi_done")
            d_split = sem("d_split")
            down_ready = sem("down_ready")
            res_scaled = sem("res_scaled")
            res_done = sem("res_done")
            out_stored = [sem(f"out_stored{i}") for i in range(2)]
            block = ctx.enter_context(nc.Block())

            def d_tile(k, first, old, new):
                return first[:] if k == 0 else old[:, k - 1] if k <= OLD else new[:, k - 1 - OLD]

            def d_hi(k):
                return d_tile(k, d0_hi, old_hi, new_hi)

            def d_lo(k):
                return d_tile(k, d0_lo, old_lo, new_lo)

            def raw_tile(k):
                if k < EARLY:
                    return raw_d[:, k]
                if k < EARLY + MORE:
                    pair = (raw_gu, raw_pair)[(k - EARLY) // 2]
                    return pair[:].rearrange("p (m k) n -> p m (k n)", m=2)[:, (k - EARLY) % 2]
                return raw_d2[:, k - EARLY - MORE]

            @block.scalar
            def _(act):
                for k in range(1, IT):
                    if k == EARLY:
                        act.wait_ge(dm_loaded, 32)
                    if k == EARLY + MORE:
                        act.wait_ge(d2_loaded, 16)
                    nc.scalar.activation(d_hi(k), raw_tile(k), ACT.Copy).then_inc(dhi_done, 1)

            @block.vector
            def _(dve):
                for k in range(1, IT):
                    dve.wait_ge(dhi_done, k)
                    split_lo(nc.vector, d_lo(k), raw_tile(k), d_hi(k)).then_inc(d_split, 1)
                dve.wait_ge(gb_loaded, 16)
                for t in range(NT):
                    dve.wait_ge(down_ready, t + 1)
                    if t >= 2:
                        dve.wait_ge(out_stored[t % 2], 16 * (t // 2))
                    nc.vector.tensor_tensor(res[:, t % 2], ps_d[t % 2][:], grow[:, t // CPB], ALU.mult)\
                        .then_inc(res_scaled, 1)
                    dve.wait_ge(res_scaled, t + 1)
                    nc.vector.tensor_tensor(res[:, t % 2], res[:, t % 2], x1[:, t], ALU.add)\
                        .then_inc(res_done, 1)

            @block.tensor
            def _(pe):
                def product(t, k):
                    cut = slice(t * P, (t + 1) * P)
                    last = three_products(nc.tensor, ps_d[t % 2][:], a_hi[:, k, cut], a_lo[:, k, cut],
                                          d_hi(k), d_lo(k), k == 0, k == IT - 1)
                    if k == IT - 1:
                        last.then_inc(down_ready, 1)

                for k in range(IT):
                    if k > 0:
                        pe.wait_ge(d_split, k)
                    product(0, k)
                    product(1, k)
                for t in range(2, NT):
                    pe.wait_ge(res_scaled, t - 1)
                    for k in range(IT):
                        product(t, k)

            @block.sync
            def _(sp):
                sp.dma_start(raw_d2[:], wd_in[EARLY + MORE:IT].rearrange("k p n -> p k n"))\
                    .then_inc(d2_loaded, 16)
                for t in range(NT):
                    sp.wait_ge(res_done, t + 1)
                    sp.dma_start(out[t], res[:, t % 2]).then_inc(out_stored[t % 2], 16)
                for s in range(2):
                    sp.wait_ge(out_stored[s], 16 * (NT // 2))


def constants():
    import numpy as np

    cst = np.zeros((P, C_END), np.float32)
    cst[:, C_ID:C_ID + P] = np.eye(P)
    cst[:, C_TRI:C_TRI + P] = np.triu(np.ones((P, P)))
    inv = (np.float32(1.0) / np.float32(10000.0) ** (np.arange(0, D, 2, dtype=np.float32) / np.float32(D)))
    ang = np.arange(L, dtype=np.float32)[:, None] * inv.astype(np.float32)
    cos = np.concatenate([np.cos(ang)] * 2, axis=1).astype(np.float32)
    sin = np.concatenate([-np.sin(ang), np.sin(ang)], axis=1).astype(np.float32)
    cst[:, C_COST:C_COST + L] = cos.T
    cst[:, C_SINT:C_SINT + L] = sin.T
    cst[:, C_COS:C_COS + L] = cos.reshape(CPB, P, D).transpose(1, 0, 2).reshape(P, L)
    cst[:, C_SIN:C_SIN + L] = sin.reshape(CPB, P, D).transpose(1, 0, 2).reshape(P, L)
    return cst


def kernel(L0_attn_hidden_states, L0_attn_Wq, L0_attn_Wk, L0_attn_Wv, L0_attn_Wo, L0_attn_Wg,
           L0_attn_Win, L0_attn_dt_bias, L0_attn_A_log_bias, L0_attn_gnorm_w, L0_ffn_w_gate,
           L0_ffn_w_up, L0_ffn_w_down, L0_c, L0_wmod):
    import numpy as np
    import concourse.bacc as bacc
    from concourse.bass_utils import run_bass_kernel_spmd

    def f(a):
        return np.asarray(a)

    def heads(w):
        w = f(w)
        return w.reshape(w.shape[0] // D, D, KT, P).transpose(0, 3, 2, 1)

    pad = IT * P - INTER
    wg, wu = (np.pad(f(w), ((0, pad), (0, 0))) for w in (L0_ffn_w_gate, L0_ffn_w_up))
    wd = np.pad(f(L0_ffn_w_down), ((0, 0), (0, pad)))
    arrays = {
        "x_in": f(L0_attn_hidden_states).reshape(NT, P, HID),
        "cT_in": f(L0_c).reshape(B, KT, P).transpose(2, 1, 0).reshape(P, KT * B),
        "wmod_in": f(L0_wmod).reshape(KT, P, 6, HID).transpose(2, 1, 0, 3),
        "wq_in": heads(L0_attn_Wq),
        "wg_in": heads(L0_attn_Wg),
        "wkv_in": np.concatenate([heads(L0_attn_Wk), heads(L0_attn_Wv)], axis=3),
        "wo_in": f(L0_attn_Wo).reshape(HID, KVH, GRP, D).transpose(1, 3, 2, 0),
        "win_in": np.pad(f(L0_attn_Win).reshape(H, KT, P).transpose(2, 1, 0),
                         ((0, 0), (0, 0), (0, P - H))),
        "rows_in": np.stack([f(L0_attn_dt_bias), f(L0_attn_A_log_bias)]),
        "gnorm_in": f(L0_attn_gnorm_w).reshape(P, 1),
        "wgu_in": np.concatenate([heads(wg), heads(wu)], axis=3),
        "wd_in": wd.T.reshape(IT, P, HID),
        "cst_in": constants(),
    }
    nc = bacc.Bacc("TRN2", target_bir_lowering=False, num_devices=1)
    arrays = {name: np.ascontiguousarray(a) for name, a in arrays.items()}
    args = {name: nc.dram_tensor(name, a.shape, F32, kind="ExternalInput").ap()
            for name, a in arrays.items()}
    out = nc.dram_tensor("out", (NT, P, HID), F32, kind="ExternalOutput").ap()
    build(nc, out=out, **args)
    r = run_bass_kernel_spmd(nc, [arrays], core_ids=[0])
    return r.results[0]["out"].reshape(B, L, HID)
```
